# Optimizing a Trainium2 kernel written in Bass

```python
import numpy as np
import jax
import jax.numpy as jnp

def _softmax(x, axis=-1):
    return jax.nn.softmax(x, axis=axis)

def _gelu(x):
    return jax.nn.gelu(x, approximate=True)

def _silu(x):
    return jax.nn.silu(x)

def _sigmoid(x):
    return jax.nn.sigmoid(x)

def _layernorm(x, axis=-1, eps=1e-05):
    m = jnp.mean(x, axis=axis, keepdims=True)
    v = jnp.var(x, axis=axis, keepdims=True)
    return (x - m) / jnp.sqrt(v + eps)

def _scatter_add(tgt, idx, src, axis=0):
    return tgt.at[idx].add(src)

def _segment_sum(src, seg, n):
    return jax.ops.segment_sum(src, seg, n)
kernel_name = 'mk_decoder_preln_d2_seqx_r4_78df49'

def setup_inputs(seed: int=0):
    np.random.seed(seed)
    _w = jnp.asarray

    def _rec_inputs():
        import jax
        import jax.numpy as jnp
        _rk = jax.random.key(seed)
        x = -0.0003929 + 0.9999 * jax.random.normal(jax.random.fold_in(_rk, 1), (8, 256, 512), jnp.float32)
        _lenS = 256 - jax.random.randint(jax.random.fold_in(_rk, 7), (8,), 0, max(1, 256 // 4) + 1, jnp.int32)
        _lenS2 = 256 - jax.random.randint(jax.random.fold_in(_rk, 8), (8,), 0, max(1, 256 // 4) + 1, jnp.int32)
        _ctx_2048P = jax.random.normal(jax.random.fold_in(_rk, 11), (8, 16, 512), jnp.float32)
        _ctx_2048c = jax.random.dirichlet(jax.random.fold_in(_rk, 511), 0.3 * jnp.ones((16,), jnp.float32), (8, 256))
        _ctx_2048t = jnp.einsum('bsk,bkd->bsd', _ctx_2048c, _ctx_2048P)
        _ctx_2048t = _ctx_2048t * jax.lax.rsqrt(jnp.mean(jnp.square(_ctx_2048t)) + 1e-12) * 0.953939
        ctx_2048 = -0.000514642 + 1.00011 * (_ctx_2048t + 0.3 * jax.random.normal(jax.random.fold_in(_rk, 611), (8, 256, 512), jnp.float32))
        _validS = jnp.arange(256)[None, :] < _lenS[:, None]
        _validS2 = jnp.arange(256)[None, :] < _lenS2[:, None]
        _causal = jnp.tril(jnp.ones((256, 256), dtype=bool))
        mask_BxS2_ik0 = jnp.where(jnp.broadcast_to(_validS2[:, :], (8, 256)), 0, 1).astype(jnp.int32)
        return (x, ctx_2048, mask_BxS2_ik0)
    x, ctx_2048, mask_BxS2_ik0 = _rec_inputs()

    def _L0_attn_setup():
        import jax, jax.numpy as jnp
        import numpy as np
        EMB = 512
        HEADS = 16
        HEAD_DIM = EMB // HEADS
        MIN_WINDOW = 64
        MAX_WINDOW = 64
        ROPE_BASE = 10000.0

        def _rotate_half(t):
            x1 = t[..., ::2]
            x2 = t[..., 1::2]
            return jnp.stack((-x2, x1), axis=-1).reshape(t.shape)

        def _rope_tables(seq_len, dtype):
            inv_freq = 1.0 / ROPE_BASE ** (jnp.arange(0, HEAD_DIM, 2, dtype=jnp.float32) / HEAD_DIM)
            pos = jnp.arange(seq_len, dtype=jnp.float32)
            freqs = jnp.outer(pos, inv_freq)
            emb = jnp.concatenate([freqs, freqs], axis=-1)
            return (jnp.cos(emb)[None, None].astype(dtype), jnp.sin(emb)[None, None].astype(dtype))

        def _forward(x, w_qkv, w_out, w_c1, w_c2):
            B, S, _ = x.shape
            scale = HEAD_DIM ** (-0.5)
            qkv = x @ w_qkv.T
            qkv = qkv.reshape(B, S, 3, HEADS, HEAD_DIM).transpose(2, 0, 3, 1, 4)
            q, k, v = (qkv[0], qkv[1], qkv[2])
            cos, sin = _rope_tables(S, x.dtype)
            q = q * cos + _rotate_half(q) * sin
            k = k * cos + _rotate_half(k) * sin
            scores = jnp.einsum('bhqd,bhkd->bhqk', q, k) * scale
            var = jnp.var(x.reshape(B, -1), axis=1, ddof=1)
            var_norm = jax.nn.sigmoid(var * 10.0 - 5.0)
            x_mean = x.mean(axis=1)
            hidden = jax.nn.silu(x_mean @ w_c1.T)
            learned = jax.nn.sigmoid(hidden @ w_c2.T)[:, 0]
            complexity = (var_norm + learned) / 2.0
            window_f = MIN_WINDOW + complexity * (MAX_WINDOW - MIN_WINDOW)
            window = window_f.mean().astype(jnp.int32)
            window = jnp.maximum(jnp.minimum(window, S), MIN_WINDOW)
            pos = jnp.arange(S)
            rel = pos[:, None] - pos[None, :]
            keep = (rel >= 0) & (rel < window)
            scores = jnp.where(keep[None, None], scores, -jnp.inf)
            attn = jax.nn.softmax(scores, axis=-1)
            out = jnp.einsum('bhqk,bhkd->bhqd', attn, v)
            out = out.transpose(0, 2, 1, 3).reshape(B, S, EMB)
            return out @ w_out.T
        key = jax.random.key(seed)
        ks = jax.random.split(key, 5)
        B, S = (2, 512)
        x = jax.random.normal(ks[0], (B, S, EMB), dtype=jnp.float32)
        w_qkv = jax.random.normal(ks[1], (3 * EMB, EMB), dtype=jnp.float32) * EMB ** (-0.5)
        w_out = jax.random.normal(ks[2], (EMB, EMB), dtype=jnp.float32) * EMB ** (-0.5)
        w_c1 = jax.random.normal(ks[3], (EMB // 4, EMB), dtype=jnp.float32) * 0.1 * EMB ** (-0.5)
        w_c2 = jax.random.normal(ks[4], (1, EMB // 4), dtype=jnp.float32) * 0.1 * (EMB // 4) ** (-0.5)
        return {'x': x, 'w_qkv': w_qkv, 'w_out': w_out, 'w_c1': w_c1, 'w_c2': w_c2}
    _L0_attn_all = _L0_attn_setup()
    _L0_attn_in = {k: v for k, v in _L0_attn_all.items() if k in ('w_qkv', 'w_out', 'w_c1', 'w_c2')}
    del _L0_attn_all

    def _L0_xattn_setup():
        import jax, jax.numpy as jnp
        import numpy as np
        import math
        H = 512
        NH = 16
        HD = H // NH
        EPS_LN = 1e-05
        RES_SCALE_MAX = 0.3

        def _nan_clean(x, lim=10000.0):
            return jnp.nan_to_num(x, nan=0.0, posinf=lim, neginf=-lim)
        key = jax.random.key(seed)
        ks = jax.random.split(key, 12)
        B, S, T = (4, 512, 64)
        std = 1.0 / math.sqrt(H)
        return {'hidden_states': jax.random.normal(ks[0], (B, S, H), jnp.float32), 'audio_tokens': jax.random.normal(ks[1], (B, T, H), jnp.float32), 'attention_mask': jax.random.randint(ks[2], (B, T), 0, 2, jnp.int32), 'Wq': jax.random.normal(ks[3], (H, H), jnp.float32) * std, 'bq': jnp.zeros((H,), jnp.float32), 'Wk': jax.random.normal(ks[4], (H, H), jnp.float32) * std, 'bk': jnp.zeros((H,), jnp.float32), 'Wv': jax.random.normal(ks[5], (H, H), jnp.float32) * std, 'bv': jnp.zeros((H,), jnp.float32), 'Wo': jax.random.normal(ks[6], (H, H), jnp.float32) * std, 'bo': jnp.zeros((H,), jnp.float32), 'ln_gamma': jnp.ones((H,), jnp.float32), 'ln_beta': jnp.zeros((H,), jnp.float32), 'residual_scale': jnp.float32(0.05)}
    _L0_xattn_all = _L0_xattn_setup()
    _L0_xattn_in = {k: v for k, v in _L0_xattn_all.items() if k in ('Wq', 'bq', 'Wk', 'bk', 'Wv', 'bv', 'Wo', 'bo', 'ln_gamma', 'ln_beta', 'residual_scale')}
    del _L0_xattn_all

    def _L0_ffn_setup():
        import jax, jax.numpy as jnp
        import numpy as np
        TOP_K = 6
        N_GROUP = 8
        TOPK_GROUP = 3
        CAPACITY = 192
        RSF = 1.0
        key = jax.random.key(seed)
        ks = jax.random.split(key, 8)
        B, S, H = (1, 1024, 512)
        E, M = (64, 352)
        MS = 704
        sc = 0.02
        return {'hidden_states': jax.random.normal(ks[0], (B, S, H), jnp.float32), 'gate_weight': jax.random.normal(ks[1], (E, H), jnp.float32) * sc, 'Wg': jax.random.normal(ks[2], (E, M, H), jnp.float32) * sc, 'Wu': jax.random.normal(ks[3], (E, M, H), jnp.float32) * sc, 'Wd': jax.random.normal(ks[4], (E, H, M), jnp.float32) * sc, 'Sg': jax.random.normal(ks[5], (MS, H), jnp.float32) * sc, 'Su': jax.random.normal(ks[6], (MS, H), jnp.float32) * sc, 'Sd': jax.random.normal(ks[7], (H, MS), jnp.float32) * sc}
    _L0_ffn_all = _L0_ffn_setup()
    _L0_ffn_in = {k: v for k, v in _L0_ffn_all.items() if k in ('gate_weight', 'Wg', 'Wu', 'Wd', 'Sg', 'Su', 'Sd')}
    del _L0_ffn_all

    def _L1_attn_setup():
        import jax, jax.numpy as jnp
        import numpy as np
        B_SZ, SEQ, D_MODEL = (2, 1024, 512)
        D_INNER, D_STATE, D_XB, D_CONV = (512, 128, 128, 4)
        NHEADS = D_INNER // D_STATE
        HEADDIM = D_STATE
        NKV = D_XB // HEADDIM
        N_REP = D_INNER // D_XB
        CHUNK = 64
        CONV_DIM = D_INNER + 2 * D_XB
        D_IN_PROJ = D_INNER + 2 * D_XB + D_INNER + NHEADS

        def _ssd(x, dt, A, Bm, Cm):
            b, l, h, p = x.shape
            c = l // CHUNK
            resh = lambda t: t.reshape(b, c, CHUNK, *t.shape[2:])
            x, dt, Bm, Cm = (resh(x), resh(dt), resh(Bm), resh(Cm))
            xdt = x * dt[..., None]
            dA = (dt * A).transpose(0, 3, 1, 2)
            Acs = jnp.cumsum(dA, axis=-1)
            seg = Acs[..., :, None] - Acs[..., None, :]
            mask = jnp.tril(jnp.ones((CHUNK, CHUNK), bool))
            Lmat = jnp.where(mask, jnp.exp(jnp.where(mask, seg, 0.0)), 0.0)
            Y_diag = jnp.einsum('bclhn,bcshn,bhcls,bcshp->bclhp', Cm, Bm, Lmat, xdt)
            decay_states = jnp.exp(Acs[..., -1:] - Acs)
            states = jnp.einsum('bclhn,bhcl,bclhp->bchpn', Bm, decay_states, xdt)
            chunk_decay = jnp.exp(Acs[..., -1])
            states_t = jnp.swapaxes(states, 0, 1)
            decay_t = jnp.transpose(chunk_decay, (2, 0, 1))

            def step(carry, inputs):
                s, d = inputs
                return (carry * d[..., None, None] + s, carry)
            _, prev = jax.lax.scan(step, jnp.zeros_like(states_t[0]), (states_t, decay_t))
            prev = jnp.swapaxes(prev, 0, 1)
            Y_off = jnp.einsum('bclhn,bchpn,bhcl->bclhp', Cm, prev, jnp.exp(Acs))
            return (Y_diag + Y_off).reshape(b, l, h, p)
        key = jax.random.key(seed)
        ks = jax.random.split(key, 8)
        dt = jnp.exp(jax.random.uniform(ks[4], (NHEADS,)) * (np.log(0.1) - np.log(0.001)) + np.log(0.001))
        dt_bias = dt + jnp.log(-jnp.expm1(-dt))
        A_log = jnp.log(jax.random.uniform(ks[5], (NHEADS,), minval=1.0, maxval=16.0))
        return {'hidden_states': jax.random.normal(ks[0], (B_SZ, SEQ, D_MODEL), jnp.float32), 'in_proj_w': jax.random.normal(ks[1], (D_IN_PROJ, D_MODEL), jnp.float32) * 0.02, 'conv_w': jax.random.normal(ks[2], (CONV_DIM, D_CONV), jnp.float32) * 0.2, 'conv_b': jnp.zeros((CONV_DIM,), jnp.float32), 'dt_bias': dt_bias.astype(jnp.float32), 'A_log': A_log.astype(jnp.float32), 'D': jnp.ones((NHEADS,), jnp.float32), 'norm_w': jnp.ones((D_INNER,), jnp.float32), 'out_proj_w': jax.random.normal(ks[3], (D_MODEL, D_INNER), jnp.float32) * 0.02}
    _L1_attn_all = _L1_attn_setup()
    _L1_attn_in = {k: v for k, v in _L1_attn_all.items() if k in ('in_proj_w', 'conv_w', 'conv_b', 'dt_bias', 'A_log', 'D', 'norm_w', 'out_proj_w')}
    del _L1_attn_all

    def _L1_xattn_setup():
        import jax, jax.numpy as jnp
        import numpy as np
        N_HEAD = 8
        key = jax.random.key(seed)
        k1, k2, k3 = jax.random.split(key, 3)
        B, D, L = (4, 256, 512)
        q = jax.random.normal(k1, (B, D, L), dtype=jnp.float32)
        k = jax.random.normal(k2, (B, D, L), dtype=jnp.float32)
        v = jax.random.normal(k3, (B, D, L), dtype=jnp.float32)
        gamma = jnp.ones((), dtype=jnp.float32)
        return {'q': q, 'k': k, 'v': v, 'gamma': gamma}
    _L1_xattn_all = _L1_xattn_setup()
    _L1_xattn_in = {k: v for k, v in _L1_xattn_all.items() if k in ('gamma',)}
    del _L1_xattn_all

    def _L1_ffn_setup():
        import jax, jax.numpy as jnp
        import numpy as np
        E = 8
        K = 2
        D = 512
        F = 2048
        R = 16
        SCALING = 32.0 / 16.0

        def gelu_new(x):
            return jax.nn.gelu(x, approximate=True)
        key = jax.random.key(seed)
        ks = jax.random.split(key, 9)
        std = 0.02
        hidden_states = jax.random.normal(ks[0], (1, 256, D), dtype=jnp.float32)
        Wr = jax.random.normal(ks[1], (D, E), dtype=jnp.float32) * std
        br = jnp.zeros((E,), dtype=jnp.float32)
        W1 = jax.random.normal(ks[2], (D, F), dtype=jnp.float32) * std
        b1 = jnp.zeros((F,), dtype=jnp.float32)
        W2 = jax.random.normal(ks[3], (F, D), dtype=jnp.float32) * std
        b2 = jnp.zeros((D,), dtype=jnp.float32)
        A1 = jax.random.normal(ks[4], (E, R, D), dtype=jnp.float32) * std
        B1 = jax.random.normal(ks[5], (E, F, R), dtype=jnp.float32) * std
        A2 = jax.random.normal(ks[6], (E, R, F), dtype=jnp.float32) * std
        B2 = jax.random.normal(ks[7], (E, D, R), dtype=jnp.float32) * std
        return {'hidden_states': hidden_states, 'Wr': Wr, 'br': br, 'W1': W1, 'b1': b1, 'W2': W2, 'b2': b2, 'A1': A1, 'B1': B1, 'A2': A2, 'B2': B2}
    _L1_ffn_all = _L1_ffn_setup()
    _L1_ffn_in = {k: v for k, v in _L1_ffn_all.items() if k in ('Wr', 'br', 'W1', 'b1', 'W2', 'b2', 'A1', 'B1', 'A2', 'B2')}
    del _L1_ffn_all
    return {'x': x, 'ctx_2048': ctx_2048, 'mask_BxS2_ik0': mask_BxS2_ik0, 'L0_attn_w_qkv': _L0_attn_in['w_qkv'], 'L0_attn_w_out': _L0_attn_in['w_out'], 'L0_attn_w_c1': _L0_attn_in['w_c1'], 'L0_attn_w_c2': _L0_attn_in['w_c2'], 'L0_xattn_Wq': _L0_xattn_in['Wq'], 'L0_xattn_bq': _L0_xattn_in['bq'], 'L0_xattn_Wk': _L0_xattn_in['Wk'], 'L0_xattn_bk': _L0_xattn_in['bk'], 'L0_xattn_Wv': _L0_xattn_in['Wv'], 'L0_xattn_bv': _L0_xattn_in['bv'], 'L0_xattn_Wo': _L0_xattn_in['Wo'], 'L0_xattn_bo': _L0_xattn_in['bo'], 'L0_xattn_ln_gamma': _L0_xattn_in['ln_gamma'], 'L0_xattn_ln_beta': _L0_xattn_in['ln_beta'], 'L0_xattn_residual_scale': _L0_xattn_in['residual_scale'], 'L0_ffn_gate_weight': _L0_ffn_in['gate_weight'], 'L0_ffn_Wg': _L0_ffn_in['Wg'], 'L0_ffn_Wu': _L0_ffn_in['Wu'], 'L0_ffn_Wd': _L0_ffn_in['Wd'], 'L0_ffn_Sg': _L0_ffn_in['Sg'], 'L0_ffn_Su': _L0_ffn_in['Su'], 'L0_ffn_Sd': _L0_ffn_in['Sd'], 'L1_attn_in_proj_w': _L1_attn_in['in_proj_w'], 'L1_attn_conv_w': _L1_attn_in['conv_w'], 'L1_attn_conv_b': _L1_attn_in['conv_b'], 'L1_attn_dt_bias': _L1_attn_in['dt_bias'], 'L1_attn_A_log': _L1_attn_in['A_log'], 'L1_attn_D': _L1_attn_in['D'], 'L1_attn_norm_w': _L1_attn_in['norm_w'], 'L1_attn_out_proj_w': _L1_attn_in['out_proj_w'], 'L1_xattn_gamma': _L1_xattn_in['gamma'], 'L1_ffn_Wr': _L1_ffn_in['Wr'], 'L1_ffn_br': _L1_ffn_in['br'], 'L1_ffn_W1': _L1_ffn_in['W1'], 'L1_ffn_b1': _L1_ffn_in['b1'], 'L1_ffn_W2': _L1_ffn_in['W2'], 'L1_ffn_b2': _L1_ffn_in['b2'], 'L1_ffn_A1': _L1_ffn_in['A1'], 'L1_ffn_B1': _L1_ffn_in['B1'], 'L1_ffn_A2': _L1_ffn_in['A2'], 'L1_ffn_B2': _L1_ffn_in['B2']}

def reference(x, ctx_2048, mask_BxS2_ik0, L0_attn_w_qkv, L0_attn_w_out, L0_attn_w_c1, L0_attn_w_c2, L0_xattn_Wq, L0_xattn_bq, L0_xattn_Wk, L0_xattn_bk, L0_xattn_Wv, L0_xattn_bv, L0_xattn_Wo, L0_xattn_bo, L0_xattn_ln_gamma, L0_xattn_ln_beta, L0_xattn_residual_scale, L0_ffn_gate_weight, L0_ffn_Wg, L0_ffn_Wu, L0_ffn_Wd, L0_ffn_Sg, L0_ffn_Su, L0_ffn_Sd, L1_attn_in_proj_w, L1_attn_conv_w, L1_attn_conv_b, L1_attn_dt_bias, L1_attn_A_log, L1_attn_D, L1_attn_norm_w, L1_attn_out_proj_w, L1_xattn_gamma, L1_ffn_Wr, L1_ffn_br, L1_ffn_W1, L1_ffn_b1, L1_ffn_W2, L1_ffn_b2, L1_ffn_A1, L1_ffn_B1, L1_ffn_A2, L1_ffn_B2):
    import jax
    import jax.numpy as jnp

    def _L0_attn_ref(x, w_qkv, w_out, w_c1, w_c2):
        import jax, jax.numpy as jnp
        import numpy as np
        EMB = 512
        HEADS = 16
        HEAD_DIM = EMB // HEADS
        MIN_WINDOW = 64
        MAX_WINDOW = 64
        ROPE_BASE = 10000.0

        def _rotate_half(t):
            x1 = t[..., ::2]
            x2 = t[..., 1::2]
            return jnp.stack((-x2, x1), axis=-1).reshape(t.shape)

        def _rope_tables(seq_len, dtype):
            inv_freq = 1.0 / ROPE_BASE ** (jnp.arange(0, HEAD_DIM, 2, dtype=jnp.float32) / HEAD_DIM)
            pos = jnp.arange(seq_len, dtype=jnp.float32)
            freqs = jnp.outer(pos, inv_freq)
            emb = jnp.concatenate([freqs, freqs], axis=-1)
            return (jnp.cos(emb)[None, None].astype(dtype), jnp.sin(emb)[None, None].astype(dtype))

        def _forward(x, w_qkv, w_out, w_c1, w_c2):
            B, S, _ = x.shape
            scale = HEAD_DIM ** (-0.5)
            qkv = x @ w_qkv.T
            qkv = qkv.reshape(B, S, 3, HEADS, HEAD_DIM).transpose(2, 0, 3, 1, 4)
            q, k, v = (qkv[0], qkv[1], qkv[2])
            cos, sin = _rope_tables(S, x.dtype)
            q = q * cos + _rotate_half(q) * sin
            k = k * cos + _rotate_half(k) * sin
            scores = jnp.einsum('bhqd,bhkd->bhqk', q, k) * scale
            var = jnp.var(x.reshape(B, -1), axis=1, ddof=1)
            var_norm = jax.nn.sigmoid(var * 10.0 - 5.0)
            x_mean = x.mean(axis=1)
            hidden = jax.nn.silu(x_mean @ w_c1.T)
            learned = jax.nn.sigmoid(hidden @ w_c2.T)[:, 0]
            complexity = (var_norm + learned) / 2.0
            window_f = MIN_WINDOW + complexity * (MAX_WINDOW - MIN_WINDOW)
            window = window_f.mean().astype(jnp.int32)
            window = jnp.maximum(jnp.minimum(window, S), MIN_WINDOW)
            pos = jnp.arange(S)
            rel = pos[:, None] - pos[None, :]
            keep = (rel >= 0) & (rel < window)
            scores = jnp.where(keep[None, None], scores, -jnp.inf)
            attn = jax.nn.softmax(scores, axis=-1)
            out = jnp.einsum('bhqk,bhkd->bhqd', attn, v)
            out = out.transpose(0, 2, 1, 3).reshape(B, S, EMB)
            return out @ w_out.T
        return _forward(x, w_qkv, w_out, w_c1, w_c2)

    def _L0_xattn_ref(hidden_states, audio_tokens, attention_mask, Wq, bq, Wk, bk, Wv, bv, Wo, bo, ln_gamma, ln_beta, residual_scale):
        import jax, jax.numpy as jnp
        import numpy as np
        import math
        H = 512
        NH = 16
        HD = H // NH
        EPS_LN = 1e-05
        RES_SCALE_MAX = 0.3

        def _nan_clean(x, lim=10000.0):
            return jnp.nan_to_num(x, nan=0.0, posinf=lim, neginf=-lim)
        B, S, _ = hidden_states.shape
        T = audio_tokens.shape[1]
        hs = _nan_clean(hidden_states).astype(jnp.float32)
        at = _nan_clean(audio_tokens).astype(jnp.float32)

        def proj(x, W, b, L):
            y = x @ W.T + b
            return y.reshape(B, L, NH, HD).transpose(0, 2, 1, 3)
        q = _nan_clean(proj(hs, Wq, bq, S))
        k = _nan_clean(proj(at, Wk, bk, T))
        v = _nan_clean(proj(at, Wv, bv, T))
        scale = max(math.sqrt(HD), 1e-08)
        scores = jnp.einsum('bhsd,bhtd->bhst', q, k) / scale
        scores = jnp.clip(scores, -50.0, 50.0)
        scores = jnp.nan_to_num(scores, nan=0.0, posinf=50.0, neginf=-50.0)
        attend = (attention_mask.astype(jnp.float32) > 0.5)[:, None, None, :]
        scores = jnp.where(attend, scores, -10000.0)
        scores = jnp.clip(scores, -50.0, 50.0)
        probs = jax.nn.softmax(scores, axis=-1)
        probs = jnp.nan_to_num(probs, nan=0.0, posinf=1.0, neginf=0.0)
        probs = probs / (probs.sum(axis=-1, keepdims=True) + 1e-08)
        ctx = jnp.einsum('bhst,bhtd->bhsd', probs, v)
        ctx = ctx.transpose(0, 2, 1, 3).reshape(B, S, H)
        delta = _nan_clean(ctx @ Wo.T + bo)
        rs = jnp.clip(residual_scale, 0.0, RES_SCALE_MAX)
        delta = rs * delta
        mu = delta.mean(axis=-1, keepdims=True)
        var = jnp.mean((delta - mu) ** 2, axis=-1, keepdims=True)
        delta = (delta - mu) / jnp.sqrt(var + EPS_LN) * ln_gamma + ln_beta
        return delta

    def _L0_ffn_ref(hidden_states, gate_weight, Wg, Wu, Wd, Sg, Su, Sd):
        import jax, jax.numpy as jnp
        import numpy as np
        TOP_K = 6
        N_GROUP = 8
        TOPK_GROUP = 3
        CAPACITY = 192
        RSF = 1.0
        B, S, H = hidden_states.shape
        E, M, _ = Wg.shape
        K, NG, TG, C = (TOP_K, N_GROUP, TOPK_GROUP, CAPACITY)
        x = hidden_states.reshape(-1, H)
        T = x.shape[0]
        logits = x.astype(jnp.float32) @ gate_weight.astype(jnp.float32).T
        scores = jax.nn.softmax(logits, axis=-1)
        group_scores = scores.reshape(T, NG, E // NG).max(axis=-1)
        _, gidx = jax.lax.top_k(group_scores, TG)
        gmask = jnp.zeros((T, NG), scores.dtype).at[jnp.arange(T)[:, None], gidx].set(1.0)
        smask = jnp.repeat(gmask, E // NG, axis=1)
        tmp_scores = jnp.where(smask > 0, scores, 0.0)
        topk_w, topk_i = jax.lax.top_k(tmp_scores, K)
        topk_w = topk_w * RSF
        flat = topk_i.reshape(-1)
        oh = jax.nn.one_hot(flat, E, dtype=jnp.int32)
        pos = jnp.sum(jnp.cumsum(oh, axis=0) * oh, axis=-1) - 1
        slot = flat * C + jnp.minimum(pos, C - 1)
        tok = jnp.arange(T * K) // K
        buf = jnp.zeros((E * C, H), x.dtype).at[slot].set(x[tok]).reshape(E, C, H)
        g = jnp.einsum('ech,emh->ecm', buf, Wg)
        u = jnp.einsum('ech,emh->ecm', buf, Wu)
        out = jnp.einsum('ecm,ehm->ech', jax.nn.silu(g) * u, Wd).reshape(E * C, H)
        yk = out[slot].reshape(T, K, H)
        y = jnp.sum(yk * topk_w[..., None].astype(yk.dtype), axis=1)
        shared = jax.nn.silu(x @ Sg.T) * (x @ Su.T) @ Sd.T
        return (y + shared).reshape(B, S, H)

    def _L1_attn_ref(hidden_states, in_proj_w, conv_w, conv_b, dt_bias, A_log, D, norm_w, out_proj_w):
        import jax, jax.numpy as jnp
        import numpy as np
        B_SZ, SEQ, D_MODEL = (2, 1024, 512)
        D_INNER, D_STATE, D_XB, D_CONV = (512, 128, 128, 4)
        NHEADS = D_INNER // D_STATE
        HEADDIM = D_STATE
        NKV = D_XB // HEADDIM
        N_REP = D_INNER // D_XB
        CHUNK = 64
        CONV_DIM = D_INNER + 2 * D_XB
        D_IN_PROJ = D_INNER + 2 * D_XB + D_INNER + NHEADS

        def _ssd(x, dt, A, Bm, Cm):
            b, l, h, p = x.shape
            c = l // CHUNK
            resh = lambda t: t.reshape(b, c, CHUNK, *t.shape[2:])
            x, dt, Bm, Cm = (resh(x), resh(dt), resh(Bm), resh(Cm))
            xdt = x * dt[..., None]
            dA = (dt * A).transpose(0, 3, 1, 2)
            Acs = jnp.cumsum(dA, axis=-1)
            seg = Acs[..., :, None] - Acs[..., None, :]
            mask = jnp.tril(jnp.ones((CHUNK, CHUNK), bool))
            Lmat = jnp.where(mask, jnp.exp(jnp.where(mask, seg, 0.0)), 0.0)
            Y_diag = jnp.einsum('bclhn,bcshn,bhcls,bcshp->bclhp', Cm, Bm, Lmat, xdt)
            decay_states = jnp.exp(Acs[..., -1:] - Acs)
            states = jnp.einsum('bclhn,bhcl,bclhp->bchpn', Bm, decay_states, xdt)
            chunk_decay = jnp.exp(Acs[..., -1])
            states_t = jnp.swapaxes(states, 0, 1)
            decay_t = jnp.transpose(chunk_decay, (2, 0, 1))

            def step(carry, inputs):
                s, d = inputs
                return (carry * d[..., None, None] + s, carry)
            _, prev = jax.lax.scan(step, jnp.zeros_like(states_t[0]), (states_t, decay_t))
            prev = jnp.swapaxes(prev, 0, 1)
            Y_off = jnp.einsum('bclhn,bchpn,bhcl->bclhp', Cm, prev, jnp.exp(Acs))
            return (Y_diag + Y_off).reshape(b, l, h, p)
        b, l, _ = hidden_states.shape
        zxbcdt = hidden_states @ in_proj_w.T
        z = zxbcdt[..., :D_INNER]
        xBC = zxbcdt[..., D_INNER:D_INNER + CONV_DIM]
        dt = zxbcdt[..., D_INNER + CONV_DIM:]
        xp = jnp.pad(xBC, ((0, 0), (D_CONV - 1, 0), (0, 0)))
        conv = conv_b + sum((xp[:, k:k + l, :] * conv_w[:, k] for k in range(D_CONV)))
        xBC = jax.nn.silu(conv)
        x = xBC[..., :D_XB].reshape(b, l, NKV, HEADDIM)
        Bm = xBC[..., D_XB:2 * D_XB].reshape(b, l, NKV, HEADDIM)
        Cm = xBC[..., 2 * D_XB:].reshape(b, l, NHEADS, D_STATE)
        x = jnp.repeat(x, N_REP, axis=2)
        Bm = jnp.repeat(Bm, N_REP, axis=2)
        dt = jax.nn.softplus(dt + dt_bias)
        A = -jnp.exp(A_log)
        y = _ssd(x, dt, A, Bm, Cm) + D[None, None, :, None] * x
        g = y.reshape(b, l, D_INNER) * jax.nn.silu(z)
        gr = g.reshape(b, l, NHEADS, HEADDIM)
        rstd = jax.lax.rsqrt(jnp.mean(gr * gr, axis=-1, keepdims=True) + 1e-05)
        yn = (gr * rstd).reshape(b, l, D_INNER) * norm_w
        return yn @ out_proj_w.T

    def _L1_xattn_ref(q, k, v, gamma):
        import jax, jax.numpy as jnp
        import numpy as np
        N_HEAD = 8
        B, Dq, Lq = q.shape
        Dv, Lk = (v.shape[-2], v.shape[-1])
        h = N_HEAD
        dq = Dq // h
        dv = Dv // h
        qh = q.reshape(B, h, dq, Lq)
        kh = k.reshape(B, h, dq, Lk)
        vh = v.reshape(B, h, dv, Lk)
        scale = 1.0 / jnp.sqrt(jnp.asarray(dq, dtype=q.dtype))
        qk = jnp.einsum('bhdq,bhdl->bhql', qh, kh) * scale
        sm = jax.nn.softmax(qk, axis=-1)
        ret = jnp.einsum('bhql,bhdl->bhdq', sm, vh)
        ret = ret.reshape(B, Dv, Lq)
        return gamma * ret

    def _L1_ffn_ref(hidden_states, Wr, br, W1, b1, W2, b2, A1, B1, A2, B2):
        import jax, jax.numpy as jnp
        import numpy as np
        E = 8
        K = 2
        D = 512
        F = 2048
        R = 16
        SCALING = 32.0 / 16.0

        def gelu_new(x):
            return jax.nn.gelu(x, approximate=True)
        B, S, Dm = hidden_states.shape
        x = hidden_states.reshape(-1, Dm)
        probs = jax.nn.softmax(x @ Wr + br, axis=-1)
        w, idx = jax.lax.top_k(probs, K)
        combine = jnp.einsum('tk,tke->te', w, jax.nn.one_hot(idx, E, dtype=x.dtype))
        base_h1 = x @ W1 + b1
        t1 = jnp.einsum('td,erd->ter', x, A1)
        l1 = jnp.einsum('ter,efr->tef', t1, B1) * SCALING
        a = gelu_new(base_h1[:, None, :] + l1)
        ca = a * combine[:, :, None]
        mix = ca.sum(axis=1)
        t2 = jnp.einsum('tef,erf->ter', ca, A2)
        l2 = jnp.einsum('ter,edr->td', t2, B2) * SCALING
        out = mix @ W2 + combine.sum(-1, keepdims=True) * b2 + l2
        return out.reshape(B, S, Dm)
    x = x + _L0_attn_ref(_layernorm(x, axis=-1), L0_attn_w_qkv, L0_attn_w_out, L0_attn_w_c1, L0_attn_w_c2)
    x = x + _L0_xattn_ref(_layernorm(x, axis=-1), ctx_2048, mask_BxS2_ik0, L0_xattn_Wq, L0_xattn_bq, L0_xattn_Wk, L0_xattn_bk, L0_xattn_Wv, L0_xattn_bv, L0_xattn_Wo, L0_xattn_bo, L0_xattn_ln_gamma, L0_xattn_ln_beta, L0_xattn_residual_scale)
    x = x + _L0_ffn_ref(_layernorm(x, axis=-1), L0_ffn_gate_weight, L0_ffn_Wg, L0_ffn_Wu, L0_ffn_Wd, L0_ffn_Sg, L0_ffn_Su, L0_ffn_Sd)
    x = x + _L1_attn_ref(_layernorm(x, axis=-1), L1_attn_in_proj_w, L1_attn_conv_w, L1_attn_conv_b, L1_attn_dt_bias, L1_attn_A_log, L1_attn_D, L1_attn_norm_w, L1_attn_out_proj_w)
    x = x + _L1_xattn_ref(_layernorm(x, axis=-1), ctx_2048, ctx_2048, L1_xattn_gamma)
    x = x + _L1_ffn_ref(_layernorm(x, axis=-1), L1_ffn_Wr, L1_ffn_br, L1_ffn_W1, L1_ffn_b1, L1_ffn_W2, L1_ffn_b2, L1_ffn_A1, L1_ffn_B1, L1_ffn_A2, L1_ffn_B2)
    return x

_drawn_inputs = setup_inputs


def setup_inputs(seed=0):
    import zlib

    import numpy as np

    out = dict(_drawn_inputs(seed))
    spreads = {'L0_xattn_bq': (0.0, 0.1),
     'L0_xattn_bk': (0.0, 2.0),
     'L0_xattn_bv': (0.0, 0.1),
     'L0_xattn_bo': (0.0, 0.1),
     'L0_xattn_ln_gamma': (1.0, 0.2),
     'L0_xattn_ln_beta': (0.0, 0.1),
     'L1_attn_conv_b': (0.0, 0.1),
     'L1_attn_D': (1.0, 0.6),
     'L1_attn_norm_w': (1.0, 0.6),
     'L1_ffn_br': (0.0, 0.8),
     'L1_ffn_b1': (0.0, 0.8),
     'L1_ffn_b2': (0.0, 2.0)}
    factors = {'L0_ffn_gate_weight': 8.0,
     'L0_ffn_Wg': 8.0,
     'L0_ffn_Wu': 8.0,
     'L0_ffn_Wd': 8.0,
     'L1_attn_dt_bias': 64.0,
     'L1_attn_A_log': 8.0,
     'L1_ffn_Wr': 7.134,
     'L1_ffn_A1': 8.0,
     'L1_ffn_B1': 8.0,
     'L1_ffn_A2': 8.0,
     'L1_ffn_B2': 8.0,
     'L0_ffn_Sg': 3.658,
     'L0_ffn_Su': 5.271,
     'L0_ffn_Sd': 3.443}
    for name, (base, spread) in spreads.items():
        noise = np.random.default_rng([zlib.crc32(name.encode()), seed]).standard_normal(out[name].shape)
        drawn = base * np.exp(spread * noise) if base else spread * noise
        out[name] = jnp.asarray(drawn.astype(out[name].dtype))
    for name, factor in factors.items():
        out[name] = (out[name] * factor).astype(out[name].dtype)
    return out
```

```python
from contextlib import ExitStack

import numpy as np

import concourse.bass as bass
from concourse import mybir

ALU = mybir.AluOpType
ACT = mybir.ActivationFunctionType
AX = mybir.AxisListType
F32 = mybir.dt.float32
U32 = mybir.dt.uint32
I32 = mybir.dt.int32
BF16 = mybir.dt.bfloat16

P = 128
NSEQ, S, D = 8, 256, 512
T = NSEQ * S
NT = S // P
KC = D // P
EPS = 1e-5

HEADS = 16
HD = D // HEADS
HPC = P // HD
WINDOW = 64
QK_SCALE = float(np.float32(HD ** -0.5))
SCORE_CLIP = 50.0
ROOT_HD = float(np.float32(HD ** 0.5))
NEG = -1e30
BAND = S - P + WINDOW

E, M, TOPK = 64, 352, 6
NG, TG = 8, 3
EPG = E // NG
CAP = 192
MS = 704
MS_CHUNKS = [(m, min(P, MS - m)) for m in range(0, MS, P)]
M_CHUNKS = [(m, min(P, M - m)) for m in range(0, M, P)]
C_TILES = [(0, P), (P, CAP - P)]
DROPPED = 1 << 15

TURN_SEMS = """
stats_ready rstd_ready normed_ready rowsT_psum colsT_ready dve_link pool_link act_link pe_link
qk_proj qk_raw_ready rope_cos_ready rot_psum rope_ready v_psum v_ready scores_psum masked_ready
negmax_ready probs_ready probsT_psum probsT_ready pv_psum attn_ready attnT_psum attnT_ready
out_psum resid_ready xk_psum xk_ready xv_psum xv_ready xq_psum xq_ready xs_psum clipped_ready
xprobs_ready xpv_psum xattn_ready delta_psum router_psum logits_used negmax_router exp_router
gate_psum tanh_ready act_sh_ready down_psum shared_ready route_ready
xbc_psum xbc_raw_ready conv_ready convtanh_ready xbc_ready z_psum ztanh_ready zs_ready dt_psum
dtabs_ready dtexp_ready dtone_ready dtln_ready dA_ready tri_ready bc_psum decay_psum decay_ready
decaymask_ready w_ready xrows_psum xrows_ready xdt_ready y_psum gated_ready sumsq_ready gated_norm
s_psum smax_ready snegmax_ready sexp_ready snormed_ready sT_psum sT_act sT_dve ret_psum
sel_ready pos_psum slot_ready moe_psum moe_negmax moe_exp mask_rows maskT_psum maskT_ready t1_psum m0_ready base_psum gelu0_ready
base1_psum gelu1_ready ca_ready mix_ready t2_psum t2m_ready y_out_psum x_out_ready
""".split()


class Sync:

    def __init__(self, nc, ctx):
        self.nc, self.ctx, self.by_name, self.counts, self.turns = nc, ctx, {}, {}, 0
        for name in TURN_SEMS:
            self[name]
        nums = [self.by_name[n].num for n in TURN_SEMS]
        assert nums == list(range(nums[0], nums[0] + len(nums)))
        self.turn_range = range(nums[0], nums[0] + len(nums))

    def __getitem__(self, name):
        if name not in self.by_name:
            self.by_name[name] = self.ctx.enter_context(self.nc.semaphore(name))
        return self.by_name[name]

    def link(self, eng, name, ins):
        self.counts[name] = self.counts.get(name, 0) + 1
        ins.then_inc(self[name], 1)
        eng.wait_ge(self[name], self.counts[name])

    def mark(self, name, ins):
        self.counts[name] = self.counts.get(name, 0) + 1
        ins.then_inc(self[name], 1)

    def sync_link(self, eng, name):
        if self.counts.get(name, 0):
            eng.wait_ge(self[name], self.counts[name])

    def end_turn(self, eng, i, base, chain=None):
        if chain is not None:
            self.counts[chain] = 0
        eng.drain().then_inc(self["turn_done"], 1)
        eng.wait_ge(self["turn_go"], i + (base + 1))

    def clear_turn(self, sp, i, base):
        self.alone(sp)
        sp.wait_ge(self["turn_done"], (i + (base + 1)) * 4)
        self.alone(sp)
        sp.sem_clear(self.turn_range)
        sp.sem_inc(self["turn_go"], 1)
        sp.wait_ge(self["turn_go"], i + (base + 1))
        self.alone(sp)

    def alone(self, eng):
        eng.sem_inc(self["passed"], 1)


def heads_view(ap, n):
    return ap.rearrange("p (h d) -> p h d", h=n)


def layernorm_rows(dve, sy, k, src, dst, st, mv, rstd):
    for j in range(NT):
        ins = dve.bn_stats(st[:, j, :], src[:, j, :])
    sy.link(dve, "dve_link", ins)
    for j in range(NT):
        ins = dve.bn_aggr(mv[:, j, :], st[:, j, :])
    ins.then_inc(sy["stats_ready"], 1)
    dve.wait_ge(sy["rstd_ready"], k + 1)
    for j in range(NT):
        dve.tensor_scalar(dst[:, j, :], src[:, j, :], mv[:, j, 0:1], rstd[:, j:j + 1],
                          ALU.subtract, ALU.mult).then_inc(sy["normed_ready"], 1)


def rstd_pool(pool, sy, k, mv, ve, rstd, minus_half):
    pool.wait_ge(sy["stats_ready"], k + 1)
    sy.link(pool, "pool_link", pool.tensor_scalar(ve[:, :], mv[:, :, 1], EPS, None, ALU.add))
    pool.tensor_tensor(rstd[:, :], ve[:, :], minus_half[:, 0:NT], ALU.pow).then_inc(sy["rstd_ready"], 1)


def transposes_pe(pe, ident, src, bank, j):
    for kc in range(KC):
        ins = pe.transpose(bank[:, kc * P:(kc + 1) * P], src[:, j, kc * P:(kc + 1) * P], ident)
    return ins


def project_pe(pe, out, lhs_of, rhs_of, chunks=KC):
    for kc in range(chunks):
        ins = pe.matmul(out, lhs_of(kc), rhs_of(kc), start=(kc == 0), stop=(kc == chunks - 1))
    return ins


def phase1(nc, sy, const, dr, base, nseq=NSEQ):
    with ExitStack() as ctx:
        def sb(name, shape, dt=F32):
            return ctx.enter_context(nc.sbuf_tensor(name, shape, dt))

        w_qkv = sb("w_qkv", [P, KC, 3 * D])
        w_out = sb("w_out", [P, KC, D])
        w_x = {n: sb(f"w_x{n}", [P, KC, D]) for n in "qkvo"}
        w_gate = sb("w_gate", [P, KC, E])
        w_sg = sb("w_sg", [P, KC, MS])
        w_su = sb("w_su", [P, KC, MS])
        w_sd = sb("w_sd", [P, len(MS_CHUNKS), D])
        cosT, sinT = sb("cosT", [P, S]), sb("sinT", [P, S])
        rot = sb("rot", [P, P])
        wmask = sb("wmask", [P, P + BAND])
        bq, bk = sb("bq", [P, KC]), sb("bk", [P, KC])
        rows_bc = sb("rows_bc", [P, 4, D])
        rs = sb("rs", [P, 1])
        mask_i = sb("mask_i", [P, NT], I32)
        hi = sb("hi", [P, NT])
        iota8, iota64 = const["iota"][:, 0:NG], const["iota"][:, 0:E]

        x = sb("x", [P, NT, D])
        h = sb("h", [P, NT, D])
        hT = sb("hT", [P, KC, S])
        ctxT = sb("ctxT", [P, KC, S])
        qk_raw = sb("qk_raw", [P, 2 * KC, S])
        qk = sb("qk", [P, 2 * KC, S])
        cosq, sinq = sb("cosq", [P, 2, S]), sb("sinq", [P, 2, S])
        vaug = sb("vaug", [P, NT, HEADS, HD + 1])
        xvaug = sb("xvaug", [P, NT, HEADS, HD + 1])
        masked = sb("masked", [P, 2, P + BAND])
        probs = sb("probs", [P, 2, P + S])
        probsT = sb("probsT", [P, 2, P + S])
        smax, negmax = sb("smax", [P, HEADS, NT]), sb("negmax", [P, HEADS, NT])
        clipped, xprobs = sb("clipped", [P, 2, NT, S]), sb("xprobs", [P, 2, NT, S])
        o = sb("o", [P, NT, D])
        oT = hT
        rec, sec = sb("rec", [P, NT, 8]), sb("sec", [P, NT, 8])
        st, mv = sb("st", [P, NT, 6]), sb("mv", [P, NT, 2])
        ve, rstd = sb("ve", [P, NT]), sb("rstd", [P, NT])
        ex = sb("ex", [P, NT, E])
        sc, tsc = sb("sc", [P, NT, E]), sb("tsc", [P, NT, E])
        rm, rsum, rrec = sb("rm", [P, NT]), sb("rsum", [P, NT]), sb("rrec", [P, NT])
        gs, gtop, gmask = sb("gs", [P, NT, NG]), sb("gtop", [P, NT, 8]), sb("gmask", [P, NT, NG])
        gidx, gidxf = sb("gidx", [P, NT, 8], U32), sb("gidxf", [P, NT, 8])
        etop = sb("etop", [P, NT, 8])
        eidx, eidxf = sb("eidx", [P, NT, 8], U32), sb("eidxf", [P, NT, 8])
        sel, pos, junk = sb("sel", [P, NT, E]), sb("pos", [P, NT, E]), sb("junk", [P, E])
        taken = sb("taken", [P, NT, E])
        carry = sb("carry", [P, E])
        last = const["last"]
        slot_v, over = sb("slot_v", [P, NT, 8]), sb("over", [P, NT, 8])
        slot_w, slot_r = sb("slot_w", [P, NT, 8], I32), sb("slot_r", [P, NT, 8], I32)
        tok_f, tok_i = sb("tok_f", [P, NT]), sb("tok_i", [P, NT], I32)
        ebase = sb("ebase", [P, E])
        zeros = sb("zeros", [P, E * CAP // P], I32)
        th = sb("th", [P, 2, S])
        shT = sb("shT", [P, len(MS_CHUNKS), S])

        ident, bank = const["ident"], const["bank"]
        one_mask = const["minus_half"]

        def pv(j, hh):
            b = bank(4 + 2 * (hh // 8) + j)
            return b[:, (hh % 8) * (HD + 1):(hh % 8 + 1) * (HD + 1)]

        def pv_bank(half, j):
            return bank(4 + 2 * half + j)[:, 0:8 * (HD + 1)].rearrange("p (h d) -> p h d", h=8)

        block = ctx.enter_context(nc.Block())

        @block.sync
        def _(sp):
            for dst, src in ((w_qkv, "w_qkv"), (w_out, "w_out")):
                sp.dma_start(dst[:], dr[src]).then_inc(sy["w1_in"], 16)
            for dst, src in ((cosT, "cosT"), (sinT, "sinT"), (rot, "rot"), (wmask, "wmask"), (bq, "bq"),
                             (bk, "bk"), (rows_bc, "rows_bc"), (rs, "rs")):
                sp.dma_start(dst[:], dr[src]).then_inc(sy["w1_in"], 16)
            for n in "qkvo":
                sp.dma_start(w_x[n][:], dr["w_x" + n]).then_inc(sy["w1_in"], 16)
            sp.dma_start(w_gate[:], dr["w_gate"]).then_inc(sy["w1_in"], 16)
            sp.dma_start(w_sg[:], dr["w_sg"]).then_inc(sy["w1_in"], 16)
            sp.dma_start(w_su[:], dr["w_su"]).then_inc(sy["w1_in"], 16)
            n_full = MS // P
            sp.dma_start(w_sd[:, 0:n_full, :], dr["w_sd"][0:n_full * P].rearrange("(c p) n -> p c n", p=P)
                         ).then_inc(sy["w1_in"], 16)
            sp.dma_start(w_sd[0:MS - n_full * P, n_full, :], dr["w_sd"][n_full * P:MS]).then_inc(sy["w1_in"], 16)
            with sp.Fori(0, nseq) as i:
                sp.dma_start(x[:], dr["x"][bass.ds(i, 1)].rearrange("o p t d -> (o p) t d")
                             ).then_inc(sy["x_in"], 16)
                sp.dma_start(ctxT[:], dr["ctxT"][bass.ds(i, 1)].rearrange("o p t d -> (o p) t d")
                             ).then_inc(sy["ctx_in"], 16)
                sp.dma_start(mask_i[:], dr["mask"][bass.ds(i, 1)].rearrange("o p t -> (o p) t")
                             ).then_inc(sy["mask_in"], 16)
                sp.wait_ge(sy["normed_ready"], 3 * NT)
                sp.dma_start(dr["normed_rows"][bass.ds(i, 1)].rearrange("o (t p) d -> (o p) t d", p=P),
                             h[:]).then_inc(sy["rows_out"], 16)
                sp.wait_ge(sy["route_ready"], 2)
                sp.dma_start(dr["route_w"][bass.ds(i, 1)].rearrange("o p t k -> (o p) t k"), etop[:]
                             ).then_inc(sy["rows_out"], 16)
                sp.dma_start(dr["route_e"][bass.ds(i, 1)].rearrange("o p t k -> (o p) t k"), eidxf[:]
                             ).then_inc(sy["rows_out"], 16)
                sp.wait_ge(sy["slot_ready"], 2)
                sp.dma_start(dr["slots"][bass.ds(i, 1)].rearrange("o p t k -> (o p) t k"), slot_r[:]
                             ).then_inc(sy["rows_out"], 16)
                sp.wait_ge(sy["shared_ready"], 2)
                sp.dma_start(dr["mid"][bass.ds(i, 1)].rearrange("o p t d -> (o p) t d"), o[:]
                             ).then_inc(sy["rows_out"], 16)
                sp.wait_ge(sy["rows_out"], (i + 1) * 80)
                sy.clear_turn(sp, i, base)

        @block.gpsimd
        def _(pool):
            pool.memset(vaug[:, :, :, HD:HD + 1], 1.0)
            pool.memset(xvaug[:, :, :, HD:HD + 1], 1.0)
            pool.memset(probs[:, :, P:P + WINDOW], 0.0).then_inc(sy["init1"], 1)
            pool.iota(ebase[:], pattern=[[CAP, E]], base=0, channel_multiplier=0,
                      allow_small_or_imprecise_dtypes=True)
            pool.iota(tok_f[:], pattern=[[P, NT]], base=0, channel_multiplier=1,
                      allow_small_or_imprecise_dtypes=True)
            pool.memset(carry[:], 0.0)
            pool.memset(slot_v[:], 0.0)
            pool.memset(last, 0.0).then_inc(sy["init1"], 1)
            pool.memset(zeros[:], 0).then_inc(sy["zeros_set"], 1)
            pool.wait_ge(sy["zeros_set"], 1)
            pool.dma_start(dr["slot_token"].rearrange("(p c) o -> p (c o)", p=P), zeros[:]
                           ).then_inc(sy["zeros_out"], 16)
            pool.wait_ge(sy["zeros_out"], 16)
            pool.wait_ge(sy["w1_in"], 16 * 19)
            with pool.Fori(0, nseq) as i:
                rstd_pool(pool, sy, 0, mv, ve, rstd, const["minus_half"])
                for c in range(2 * KC):
                    pool.wait_ge(sy["qk_raw_ready"], c + 1)
                    if c >= 2:
                        pool.wait_ge(sy["rope_ready"], c - 1)
                    pool.tensor_tensor(cosq[:, c % 2, :], qk_raw[:, c, :], cosT[:], ALU.mult
                                       ).then_inc(sy["rope_cos_ready"], 1)
                for hh in range(HEADS):
                    pool.wait_ge(sy["masked_ready"], 2 * hh + 2)
                    pool.tensor_scalar(negmax[:, hh, :], smax[:, hh, :], -QK_SCALE, None, ALU.mult
                                       ).then_inc(sy["negmax_ready"], 1)
                pool.wait_ge(sy["mask_in"], (i + 1) * 16)
                sy.alone(pool)
                sy.link(pool, "pool_link", pool.tensor_copy(hi[:], mask_i[:]))
                sy.link(pool, "pool_link", pool.tensor_scalar(hi[:], hi[:], 0.5, None, ALU.is_gt))
                pool.tensor_scalar(hi[:], hi[:], 2 * SCORE_CLIP * ROOT_HD, -SCORE_CLIP * ROOT_HD,
                                   ALU.mult, ALU.add).then_inc(sy["misc1_ready"], 1)
                for k in (1, 2, 3):
                    rstd_pool(pool, sy, k, mv, ve, rstd, const["minus_half"])
                for j in range(NT):
                    pool.wait_ge(sy["slot_ready"], j + 1)
                    for k in range(TOPK):
                        pool.indirect_dma_start(
                            out=dr["slot_token"], out_offset=bass.IndirectOffsetOnAxis(ap=slot_w[:, j, k:k + 1], axis=0),
                            in_=tok_i[:, j:j + 1], in_offset=None, bounds_check=E * CAP - 1, oob_is_err=False
                        ).then_inc(sy["scattered"], 16)
                pool.wait_ge(sy["scattered"], (i + 1) * (16 * NT * TOPK))
                sy.alone(pool)
                sy.end_turn(pool, i, base, "pool_link")

        @block.scalar
        def _(act):
            act.wait_ge(sy["w1_in"], 16 * 19)
            act.wait_ge(sy["init1"], 2)
            with act.Fori(0, nseq) as i:
                def cols_copy(k):
                    for j in range(NT):
                        act.wait_ge(sy["rowsT_psum"], NT * k + j + 1)
                        act.activation(hT[:, :, j * P:(j + 1) * P],
                                       bank(j)[:, :].rearrange("p (c t) -> p c t", c=KC), ACT.Copy
                                       ).then_inc(sy["colsT_ready"], 1)

                cols_copy(0)
                for c in range(2 * KC):
                    act.wait_ge(sy["qk_proj"], c + 1)
                    act.activation(qk_raw[:, c, :], bank(2 + c % 2)[:, 0:S], ACT.Copy
                                   ).then_inc(sy["qk_raw_ready"], 1)
                for j in range(NT):
                    act.wait_ge(sy["v_psum"], j + 1)
                    act.activation(vaug[:, j, :, 0:HD], heads_view(bank(6 + j)[:, :], HEADS), ACT.Copy
                                   ).then_inc(sy["v_ready"], 1)
                for hh in range(HEADS):
                    act.wait_ge(sy["negmax_ready"], hh + 1)
                    if hh >= 2:
                        act.wait_ge(sy["probsT_psum"], hh - 1)
                    act.activation(probs[:, hh % 2, 0:P], masked[:, hh % 2, 0:P], ACT.Exp,
                                   bias=negmax[:, hh, 0:1], scale=QK_SCALE)
                    act.activation(probs[:, hh % 2, P + WINDOW:P + S], masked[:, hh % 2, P:P + BAND], ACT.Exp,
                                   bias=negmax[:, hh, 1:2], scale=QK_SCALE).then_inc(sy["probs_ready"], 1)
                for c in range(KC):
                    act.wait_ge(sy["xk_psum"], c + 1)
                    act.activation(qk[:, KC + c, :], bank(c % 2)[:, 0:S], ACT.Identity, bias=bk[:, c:c + 1]
                                   ).then_inc(sy["xk_ready"], 1)
                cols_copy(1)
                cols_copy(2)
                for c in range(KC):
                    act.wait_ge(sy["xq_psum"], c + 1)
                    act.activation(qk[:, c, :], bank(2 + c % 2)[:, 0:S], ACT.Identity, bias=bq[:, c:c + 1]
                                   ).then_inc(sy["xq_ready"], 1)
                for hh in range(HEADS):
                    act.wait_ge(sy["clipped_ready"], 2 * hh + 2)
                    if hh >= 2:
                        act.wait_ge(sy["xpv_psum"], hh - 1)
                    act.activation(xprobs[:, hh % 2], clipped[:, hh % 2], ACT.Exp, scale=1.0 / ROOT_HD
                                   ).then_inc(sy["xprobs_ready"], 1)
                cols_copy(3)
                cols_copy(4)
                for j in range(NT):
                    act.wait_ge(sy["negmax_router"], j + 1)
                    act.activation(ex[:, j, :], bank(6 + j)[:, 0:E], ACT.Exp, bias=rm[:, j:j + 1],
                                   accum_out=rsum[:, j:j + 1]).then_inc(sy["exp_router"], 1)
                for n, (m, w) in enumerate(MS_CHUNKS):
                    act.wait_ge(sy["gate_psum"], n + 1)
                    if n >= 2:
                        act.wait_ge(sy["act_sh_ready"], n - 1)
                    act.activation(th[0:w, n % 2, :], bank(2 + n % 2)[0:w, 0:S], ACT.Tanh, scale=0.5
                                   ).then_inc(sy["tanh_ready"], 1)
                sy.end_turn(act, i, base, "act_link")

        @block.tensor
        def _(pe):
            pe.wait_ge(sy["w1_in"], 16 * 19)
            pe.wait_ge(sy["init1"], 2)
            with pe.Fori(0, nseq) as i:
                def rows_to_cols(k, src, ready, at):
                    for j in range(NT):
                        pe.wait_ge(ready, at + j + 1)
                        transposes_pe(pe, ident, src, bank(j), j).then_inc(sy["rowsT_psum"], 1)

                rows_to_cols(0, h, sy["normed_ready"], 0)
                for c in range(2 * KC + 1):
                    if c < 2 * KC:
                        pe.wait_ge(sy["colsT_ready"], NT)
                        if c >= 2:
                            pe.wait_ge(sy["qk_raw_ready"], c - 1)
                        project_pe(pe, bank(2 + c % 2)[:, 0:S], lambda kc: w_qkv[:, kc, c * P:(c + 1) * P],
                                   lambda kc: hT[:, kc, :]).then_inc(sy["qk_proj"], 1)
                    if c >= 1:
                        pe.wait_ge(sy["qk_raw_ready"], c)
                        if c >= 3:
                            pe.wait_ge(sy["rope_ready"], c - 2)
                        pe.matmul(bank(4 + (c - 1) % 2)[:, 0:S], rot[:], qk_raw[:, c - 1, :], start=True,
                                  stop=True).then_inc(sy["rot_psum"], 1)
                for j in range(NT):
                    project_pe(pe, bank(6 + j)[:, :], lambda kc: hT[:, kc, j * P:(j + 1) * P],
                               lambda kc: w_qkv[:, kc, 2 * D:3 * D]).then_inc(sy["v_psum"], 1)
                pe.wait_ge(sy["rope_ready"], 2 * KC)
                pe.wait_ge(sy["v_ready"], NT)
                for s in range(HEADS + 2):
                    if s < HEADS:
                        c, r = s // HPC, (s % HPC) * HD
                        if s >= 2:
                            pe.wait_ge(sy["masked_ready"], 2 * (s - 1))
                        q, k, b = qk[r:r + HD, c, :], qk[r:r + HD, KC + c, :], bank(s % 2)
                        pe.matmul(b[:, 0:P], q[:, 0:P], k[:, 0:P], start=True, stop=True)
                        pe.matmul(b[:, P:P + BAND], q[:, P:S], k[:, WINDOW:S], start=True, stop=True
                                  ).then_inc(sy["scores_psum"], 1)
                    if 1 <= s <= HEADS:
                        hh = s - 1
                        pe.wait_ge(sy["probs_ready"], hh + 1)
                        if hh >= 2:
                            pe.wait_ge(sy["probsT_ready"], hh - 1)
                        for b3 in range(3):
                            ins = pe.transpose(bank(2 + hh % 2)[:, b3 * P:(b3 + 1) * P],
                                               probs[:, hh % 2, b3 * P:(b3 + 1) * P], ident)
                        ins.then_inc(sy["probsT_psum"], 1)
                    if s >= 2:
                        hh = s - 2
                        pe.wait_ge(sy["probsT_ready"], hh + 1)
                        pt = probsT[:, hh % 2]
                        pe.matmul(pv(0, hh), pt[:, 0:P], vaug[:, 0, hh, :], start=True, stop=True)
                        pe.matmul(pv(1, hh), pt[:, P:2 * P], vaug[:, 0, hh, :], start=True, stop=False)
                        pe.matmul(pv(1, hh), pt[:, 2 * P:3 * P], vaug[:, 1, hh, :], start=False, stop=True
                                  ).then_inc(sy["pv_psum"], 1)
                pe.wait_ge(sy["ctx_in"], (i + 1) * 16)
                for c in range(KC):
                    if c >= 2:
                        pe.wait_ge(sy["xk_ready"], c - 1)
                    else:
                        pe.wait_ge(sy["masked_ready"], 2 * HEADS)
                    project_pe(pe, bank(c % 2)[:, 0:S], lambda kc: w_x["k"][:, kc, c * P:(c + 1) * P],
                               lambda kc: ctxT[:, kc, :]).then_inc(sy["xk_psum"], 1)
                for j in range(NT):
                    pe.wait_ge(sy["probsT_ready"], HEADS)
                    project_pe(pe, bank(2 + j)[:, :], lambda kc: ctxT[:, kc, j * P:(j + 1) * P],
                               lambda kc: w_x["v"][:, kc, :]).then_inc(sy["xv_psum"], 1)
                pe.wait_ge(sy["xk_ready"], KC)
                rows_to_cols(1, o, sy["attn_ready"], 0)
                pe.wait_ge(sy["colsT_ready"], 2 * NT)
                for j in range(NT):
                    project_pe(pe, bank(4 + j)[:, :], lambda kc: oT[:, kc, j * P:(j + 1) * P],
                               lambda kc: w_out[:, kc, :]).then_inc(sy["out_psum"], 1)
                rows_to_cols(2, h, sy["normed_ready"], NT)
                pe.wait_ge(sy["colsT_ready"], 3 * NT)
                for c in range(KC):
                    if c >= 2:
                        pe.wait_ge(sy["xq_ready"], c - 1)
                    else:
                        pe.wait_ge(sy["xv_ready"], NT)
                    project_pe(pe, bank(2 + c % 2)[:, 0:S], lambda kc: w_x["q"][:, kc, c * P:(c + 1) * P],
                               lambda kc: hT[:, kc, :]).then_inc(sy["xq_psum"], 1)
                pe.wait_ge(sy["xq_ready"], KC)
                for s in range(HEADS + 2):
                    if s < HEADS:
                        c, r, b = s // HPC, (s % HPC) * HD, bank(s % 4)
                        if s >= 4:
                            pe.wait_ge(sy["clipped_ready"], 2 * (s - 3))
                        for kt in range(NT):
                            ins = pe.matmul(b[:, kt * S:(kt + 1) * S], qk[r:r + HD, KC + c, kt * P:(kt + 1) * P],
                                            qk[r:r + HD, c, :], start=True, stop=True)
                        ins.then_inc(sy["xs_psum"], 1)
                    if s >= 2:
                        hh = s - 2
                        pe.wait_ge(sy["xprobs_ready"], hh + 1)
                        for j in range(NT):
                            for kt in range(NT):
                                ins = pe.matmul(pv(j, hh), xprobs[:, hh % 2, kt, j * P:(j + 1) * P],
                                                xvaug[:, kt, hh, :], start=(kt == 0), stop=(kt == NT - 1))
                        ins.then_inc(sy["xpv_psum"], 1)
                rows_to_cols(3, o, sy["xattn_ready"], 0)
                pe.wait_ge(sy["colsT_ready"], 4 * NT)
                for j in range(NT):
                    project_pe(pe, bank(2 + j)[:, :], lambda kc: oT[:, kc, j * P:(j + 1) * P],
                               lambda kc: w_x["o"][:, kc, :]).then_inc(sy["delta_psum"], 1)
                rows_to_cols(4, h, sy["normed_ready"], 2 * NT)
                pe.wait_ge(sy["colsT_ready"], 5 * NT)
                for j in range(NT):
                    project_pe(pe, bank(6 + j)[:, 0:E], lambda kc: hT[:, kc, j * P:(j + 1) * P],
                               lambda kc: w_gate[:, kc, :]).then_inc(sy["router_psum"], 1)
                for n, (m, w) in enumerate(MS_CHUNKS):
                    if n >= 2:
                        pe.wait_ge(sy["act_sh_ready"], n - 1)
                    b = bank(2 + n % 2)
                    project_pe(pe, b[0:w, 0:S], lambda kc: w_sg[:, kc, m:m + w], lambda kc: hT[:, kc, :])
                    project_pe(pe, b[0:w, S:2 * S], lambda kc: w_su[:, kc, m:m + w], lambda kc: hT[:, kc, :]
                               ).then_inc(sy["gate_psum"], 1)
                pe.wait_ge(sy["act_sh_ready"], len(MS_CHUNKS))
                for j in range(NT):
                    for n, (m, w) in enumerate(MS_CHUNKS):
                        ins = pe.matmul(bank(4 + j)[:, :], shT[0:w, n, j * P:(j + 1) * P], w_sd[0:w, n, :],
                                        start=(n == 0), stop=(n == len(MS_CHUNKS) - 1))
                    ins.then_inc(sy["down_psum"], 1)
                    pe.wait_ge(sy["sel_ready"], j + 1)
                    pe.matmul(bank(6 + j)[:, E:2 * E], const["tri_lt"], sel[:, j, :], start=True, stop=True)
                    pe.matmul(bank(6 + j)[:, 2 * E:3 * E], const["ones"], sel[:, j, :], start=True, stop=True
                              ).then_inc(sy["pos_psum"], 1)
                sy.end_turn(pe, i, base)

        @block.vector
        def _(dve):
            dve.wait_ge(sy["w1_in"], 16 * 19)
            dve.wait_ge(sy["init1"], 2)
            sy.link(dve, "dve_link0", dve.tensor_scalar(rs[:], rs[:], 0.0, 0.3, ALU.max, ALU.min))
            with dve.Fori(0, nseq) as i:
                dve.wait_ge(sy["x_in"], (i + 1) * 16)
                layernorm_rows(dve, sy, 0, x, h, st, mv, rstd)
                for c in range(2 * KC):
                    dve.wait_ge(sy["rot_psum"], c + 1)
                    sy.link(dve, "dve_link", dve.tensor_tensor(sinq[:, c % 2, :], bank(4 + c % 2)[:, 0:S],
                                                               sinT[:], ALU.mult))
                    dve.wait_ge(sy["rope_cos_ready"], c + 1)
                    dve.tensor_tensor(qk[:, c, :], cosq[:, c % 2, :], sinq[:, c % 2, :], ALU.add
                                      ).then_inc(sy["rope_ready"], 1)
                for s in range(HEADS + 1):
                    if s < HEADS:
                        dve.wait_ge(sy["scores_psum"], s + 1)
                        if s >= 2:
                            dve.wait_ge(sy["probs_ready"], s - 1)
                        for j, (a, w) in enumerate(((0, P), (P, BAND))):
                            dve.tensor_tensor_reduce(
                                out=masked[:, s % 2, a:a + w], in0=bank(s % 2)[:, a:a + w], in1=wmask[:, a:a + w],
                                scale=1.0, scalar=3 * NEG, op0=ALU.add, op1=ALU.max,
                                accum_out=smax[:, s, j:j + 1]).then_inc(sy["masked_ready"], 1)
                    if s >= 1:
                        hh = s - 1
                        dve.wait_ge(sy["probsT_psum"], hh + 1)
                        if hh >= 2:
                            dve.wait_ge(sy["pv_psum"], hh - 1)
                        dve.tensor_copy(probsT[:, hh % 2], bank(2 + hh % 2)[:, 0:P + S]
                                        ).then_inc(sy["probsT_ready"], 1)
                for half in range(2):
                    dve.wait_ge(sy["pv_psum"], 8 * half + 8)
                    for j in range(NT):
                        b = pv_bank(half, j)
                        sy.link(dve, "dve_link", dve.reciprocal(rec[:, j, :], b[:, :, HD]))
                        ins = dve.tensor_tensor(heads_view(o[:, j, half * 256:(half + 1) * 256], 8), b[:, :, 0:HD],
                                                rec[:, j, :].unsqueeze(2).broadcast_to([P, 8, HD]), ALU.mult)
                        if half == 1:
                            ins.then_inc(sy["attn_ready"], 1)
                        else:
                            sy.link(dve, "dve_link", ins)
                for j in range(NT):
                    dve.wait_ge(sy["xv_psum"], j + 1)
                    dve.tensor_tensor(xvaug[:, j, :, 0:HD], heads_view(bank(2 + j)[:, :], HEADS),
                                      heads_view(rows_bc[:, 0, :], HEADS), ALU.add).then_inc(sy["xv_ready"], 1)
                for j in range(NT):
                    dve.wait_ge(sy["out_psum"], j + 1)
                    ins = dve.tensor_tensor(x[:, j, :], x[:, j, :], bank(4 + j)[:, :], ALU.add)
                sy.link(dve, "dve_link", ins)
                layernorm_rows(dve, sy, 1, x, h, st, mv, rstd)
                dve.wait_ge(sy["misc1_ready"], 1)
                for hh in range(HEADS):
                    dve.wait_ge(sy["xs_psum"], hh + 1)
                    if hh >= 2:
                        dve.wait_ge(sy["xprobs_ready"], hh - 1)
                    for kt in range(NT):
                        dve.tensor_scalar(clipped[:, hh % 2, kt, :], bank(hh % 4)[:, kt * S:(kt + 1) * S],
                                          hi[:, kt:kt + 1], -SCORE_CLIP * ROOT_HD, ALU.min, ALU.max
                                          ).then_inc(sy["clipped_ready"], 1)
                for half in range(2):
                    dve.wait_ge(sy["xpv_psum"], 8 * half + 8)
                    for j in range(NT):
                        b = pv_bank(half, j)
                        sy.link(dve, "dve_link", dve.reciprocal(rec[:, j, :], b[:, :, HD]))
                        sy.link(dve, "dve_link", dve.tensor_tensor(sec[:, j, :], b[:, :, HD], rec[:, j, :], ALU.mult))
                        sy.link(dve, "dve_link", dve.tensor_scalar(sec[:, j, :], sec[:, j, :], 1e-8, None, ALU.add))
                        sy.link(dve, "dve_link", dve.reciprocal(sec[:, j, :], sec[:, j, :]))
                        sy.link(dve, "dve_link", dve.tensor_tensor(rec[:, j, :], rec[:, j, :], sec[:, j, :], ALU.mult))
                        ins = dve.tensor_tensor(heads_view(o[:, j, half * 256:(half + 1) * 256], 8), b[:, :, 0:HD],
                                                rec[:, j, :].unsqueeze(2).broadcast_to([P, 8, HD]), ALU.mult)
                        if half == 1:
                            ins.then_inc(sy["xattn_ready"], 1)
                        else:
                            sy.link(dve, "dve_link", ins)
                for j in range(NT):
                    dve.wait_ge(sy["delta_psum"], j + 1)
                    sy.link(dve, "dve_link", dve.tensor_tensor(h[:, j, :], bank(2 + j)[:, :], rows_bc[:, 1, :], ALU.add))
                    sy.link(dve, "dve_link", dve.tensor_scalar(h[:, j, :], h[:, j, :], rs[:, 0:1], None, ALU.mult))
                for j in range(NT):
                    ins = dve.bn_stats(st[:, j, :], h[:, j, :])
                sy.link(dve, "dve_link", ins)
                for j in range(NT):
                    ins = dve.bn_aggr(mv[:, j, :], st[:, j, :])
                ins.then_inc(sy["stats_ready"], 1)
                dve.wait_ge(sy["rstd_ready"], 3)
                for j in range(NT):
                    sy.link(dve, "dve_link", dve.tensor_scalar(h[:, j, :], h[:, j, :], mv[:, j, 0:1], rstd[:, j:j + 1],
                                                               ALU.subtract, ALU.mult))
                    sy.link(dve, "dve_link", dve.tensor_tensor(h[:, j, :], h[:, j, :], rows_bc[:, 2, :], ALU.mult))
                    sy.link(dve, "dve_link", dve.tensor_tensor(h[:, j, :], h[:, j, :], rows_bc[:, 3, :], ALU.add))
                    sy.link(dve, "dve_link", dve.tensor_tensor(x[:, j, :], x[:, j, :], h[:, j, :], ALU.add))
                layernorm_rows(dve, sy, 3, x, h, st, mv, rstd)
                for j in range(NT):
                    dve.wait_ge(sy["router_psum"], j + 1)
                    sy.link(dve, "dve_link", dve.tensor_reduce(rm[:, j:j + 1], bank(6 + j)[:, 0:E], AX.X, ALU.max))
                    dve.tensor_scalar(rm[:, j:j + 1], rm[:, j:j + 1], -1.0, None, ALU.mult
                                      ).then_inc(sy["negmax_router"], 1)
                def shared(n):
                    m, w = MS_CHUNKS[n]
                    dve.wait_ge(sy["tanh_ready"], n + 1)
                    b = bank(2 + n % 2)
                    sy.link(dve, "dve_link", dve.scalar_tensor_tensor(
                        out=shT[0:w, n, :], in0=th[0:w, n % 2, :], scalar=1.0, in1=b[0:w, 0:S], op0=ALU.add,
                        op1=ALU.mult))
                    dve.tensor_tensor(shT[0:w, n, :], shT[0:w, n, :], b[0:w, S:2 * S], ALU.mult
                                      ).then_inc(sy["act_sh_ready"], 1)

                for n in range(2):
                    shared(n)
                for j in range(NT):
                    def ln(ins):
                        sy.link(dve, "dve_link", ins)
                    dve.wait_ge(sy["exp_router"], j + 1)
                    ln(dve.reciprocal(rrec[:, j:j + 1], rsum[:, j:j + 1]))
                    ln(dve.tensor_scalar(sc[:, j, :], ex[:, j, :], rrec[:, j:j + 1], None, ALU.mult))
                    ln(dve.tensor_reduce(gs[:, j, :], sc[:, j, :].rearrange("p (g e) -> p g e", g=NG), AX.X, ALU.max))
                    ln(dve.max(gtop[:, j, :], gs[:, j, :]))
                    ln(dve.max_index(gidx[:, j, :], gtop[:, j, :], gs[:, j, :]))
                    ln(dve.tensor_copy(gidxf[:, j, :], gidx[:, j, :]))
                    ln(dve.tensor_scalar(gmask[:, j, :], iota8, gidxf[:, j, 0:1], None, ALU.is_equal))
                    for g in range(1, TG):
                        ln(dve.scalar_tensor_tensor(out=gmask[:, j, :], in0=iota8, scalar=gidxf[:, j, g:g + 1],
                                                    in1=gmask[:, j, :], op0=ALU.is_equal, op1=ALU.add))
                    ln(dve.tensor_tensor(tsc[:, j, :].rearrange("p (g e) -> p g e", g=NG),
                                         sc[:, j, :].rearrange("p (g e) -> p g e", g=NG),
                                         gmask[:, j, :].unsqueeze(2).broadcast_to([P, NG, EPG]), ALU.mult))
                    ln(dve.max(etop[:, j, :], tsc[:, j, :]))
                    ln(dve.max_index(eidx[:, j, :], etop[:, j, :], tsc[:, j, :]))
                    ins = dve.tensor_copy(eidxf[:, j, :], eidx[:, j, :])
                    ins.then_inc(sy["route_ready"], 1)
                    dve.wait_ge(sy["route_ready"], j + 1)
                    ln(dve.tensor_scalar(sel[:, j, :], iota64, eidxf[:, j, 0:1], None, ALU.is_equal))
                    for k in range(1, TOPK):
                        ins = dve.scalar_tensor_tensor(out=sel[:, j, :], in0=iota64, scalar=eidxf[:, j, k:k + 1],
                                                       in1=sel[:, j, :], op0=ALU.is_equal, op1=ALU.add)
                        if k < TOPK - 1:
                            ln(ins)
                    ins.then_inc(sy["sel_ready"], 1)
                    shared(2 + 2 * j)
                    shared(3 + 2 * j)
                for j in range(NT):
                    dve.wait_ge(sy["down_psum"], j + 1)
                    dve.scalar_tensor_tensor(out=o[:, j, :], in0=bank(4 + j)[:, :], scalar=0.5, in1=x[:, j, :],
                                             op0=ALU.mult, op1=ALU.add).then_inc(sy["shared_ready"], 1)
                for j in range(NT):
                    dve.wait_ge(sy["pos_psum"], j + 1)
                    ln(dve.scalar_tensor_tensor(out=last, in0=sel[:, j, :], scalar=tok_f[:, j:j + 1], in1=last,
                                                op0=ALU.mult, op1=ALU.max))
                    ln(dve.tensor_tensor(pos[:, j, :], bank(6 + j)[:, E:2 * E], carry[:], ALU.add))
                    ln(dve.tensor_tensor(carry[:], carry[:], bank(6 + j)[:, 2 * E:3 * E], ALU.add))
                    ln(dve.tensor_scalar(taken[:, j, :], pos[:, j, :], float(CAP - 1), float(DROPPED), ALU.is_ge,
                                         ALU.mult))
                    ln(dve.scalar_tensor_tensor(out=pos[:, j, :], in0=pos[:, j, :], scalar=float(CAP - 1),
                                                in1=ebase[:], op0=ALU.min, op1=ALU.add))
                    ln(dve.tensor_tensor(pos[:, j, :], pos[:, j, :], taken[:, j, :], ALU.add))
                    for k in range(TOPK):
                        ln(dve.scalar_tensor_tensor(out=junk[:], in0=iota64, scalar=eidxf[:, j, k:k + 1],
                                                    in1=pos[:, j, :], op0=ALU.is_equal, op1=ALU.mult,
                                                    accum_out=slot_v[:, j, k:k + 1]))
                    ln(dve.tensor_scalar(over[:, j, :], slot_v[:, j, :], float(DROPPED), -float(DROPPED),
                                         ALU.is_ge, ALU.mult))
                    ln(dve.tensor_tensor(over[:, j, :], over[:, j, :], slot_v[:, j, :], ALU.add))
                    ln(dve.tensor_copy(slot_w[:, j, :], slot_v[:, j, :]))
                    ln(dve.tensor_copy(tok_i[:, j:j + 1], tok_f[:, j:j + 1]))
                    dve.tensor_copy(slot_r[:, j, :], over[:, j, :]).then_inc(sy["slot_ready"], 1)
                ln(dve.tensor_scalar(tok_f[:], tok_f[:], float(S), None, ALU.add))
                sy.end_turn(dve, i, base, "dve_link")




def phase2(nc, sy, const, dr):
    with ExitStack() as ctx:
        def sb(name, shape, dt=F32):
            return ctx.enter_context(nc.sbuf_tensor(name, shape, dt))

        wgu = [sb(f"wgu{b}", [P, 2, KC, M]) for b in range(2)]
        wd = [sb(f"wd{b}", [P, len(M_CHUNKS), D]) for b in range(2)]
        idx = [sb(f"idx{b}", [P, 2], I32) for b in range(2)]
        xg = [sb(f"xg{b}", [P, 2, D]) for b in range(2)]
        xT = [sb(f"xT{b}", [P, KC, CAP]) for b in range(2)]
        th = sb("eth", [P, len(M_CHUNKS), CAP])
        aT = [sb(f"aT{b}", [P, len(M_CHUNKS), CAP]) for b in range(2)]
        yo = [sb(f"yo{b}", [P, 2, D]) for b in range(2)]
        last_c, last_i = sb("last_c", [E, 1]), sb("last_i", [E, 1], I32)
        ident, bank = const["ident"], const["bank"]
        NM = len(M_CHUNKS)
        slot_token, expert_out = dr["slot_token"], dr["expert_out"]
        rows = dr["normed_rows"].rearrange("n s d -> (n s) d")

        block = ctx.enter_context(nc.Block())

        def pairs(eng, step):
            step(0, 0, 0, True)
            step(1, 0, 1, True)
            with eng.Fori(1, E // 2 - 1) as n:
                step(n * 2, n, 0, False)
                step(n * 2 + 1, n, 1, False)
            step(E - 2, E // 2 - 1, 0, False)
            step(E - 1, E // 2 - 1, 1, False)

        @block.sync
        def _(sp):
            sp.wait_ge(sy["last_ready"], 1)
            sp.dma_start(slot_token.rearrange("(e c) o -> e (c o)", c=CAP)[:, CAP - 1:CAP], last_i[:],
                         allow_slow_non_contiguous=True
                         ).then_inc(sy["last_out"], 16)
            sp.wait_ge(sy["last_out"], 16)

            def step(e, n, b, first):
                if not first:
                    sp.wait_ge(sy[f"xg_in{b}"], n * 32)
                sp.dma_start(idx[b][:, 0:1], slot_token[bass.ds(e * CAP, P)]).then_inc(sy[f"idx_in{b}"], 16)
                sp.dma_start(idx[b][0:CAP - P, 1:2], slot_token[bass.ds(e * CAP + P, CAP - P)]
                             ).then_inc(sy[f"idx_in{b}"], 16)
                if not first:
                    sp.wait_ge(sy["edown_psum"], e - 1)
                sp.dma_start(wgu[b][:], dr["w_gu"][bass.ds(e, 1)].rearrange("o p t c m -> (o p) t c m")
                             ).then_inc(sy[f"ew_in{b}"], 16)
                sp.dma_start(wd[b][:, 0:2, :], dr["w_d"][bass.ds(e, 1), 0:2 * P].rearrange(
                    "o (c p) n -> (o p) c n", p=P)).then_inc(sy[f"ew_in{b}"], 16)
                sp.dma_start(wd[b][0:M - 2 * P, 2, :], dr["w_d"][bass.ds(e, 1), 2 * P:M].rearrange(
                    "o p n -> (o p) n")).then_inc(sy[f"ew_in{b}"], 16)

            pairs(sp, step)

        @block.gpsimd
        def _(pool):
            def step(e, n, b, first):
                pool.wait_ge(sy[f"idx_in{b}"], n * 32 + 32)
                if not first:
                    pool.wait_ge(sy["exT_psum"], e - 1)
                sy.alone(pool)
                for t, (c0, w) in enumerate(C_TILES):
                    pool.indirect_dma_start(
                        out=xg[b][0:w, t, :], out_offset=None, in_=rows,
                        in_offset=bass.IndirectOffsetOnAxis(ap=idx[b][0:w, t:t + 1], axis=0)
                    ).then_inc(sy[f"xg_in{b}"], 16)

            pairs(pool, step)

        @block.scalar
        def _(act):
            def xT_copy(e, b):
                act.wait_ge(sy["exT_psum"], e + 1)
                for t in range(2):
                    ins = act.activation(xT[b][:, 2 * t:2 * t + 2, :],
                                         bank(t)[:, 0:2 * CAP].rearrange("p (c t) -> p c t", c=2), ACT.Copy)
                ins.then_inc(sy["exT_ready"], 1)

            def step(e, n, b, first):
                for m, (m0, w) in enumerate(M_CHUNKS):
                    act.wait_ge(sy["egu_psum"], e * NM + (m + 1))
                    if not (first and b == 0):
                        act.wait_ge(sy["eact_ready"], e * NM + (m + 1 - NM))
                    act.activation(th[0:w, m, :], bank(2 + m)[0:w, 0:CAP], ACT.Tanh, scale=0.5
                                   ).then_inc(sy["etanh_ready"], 1)
                if e is not E - 1:
                    xT_copy(e + 1, 1 - b)
                act.wait_ge(sy["edown_psum"], e + 1)
                if not first:
                    act.wait_ge(sy[f"eout{b}"], n * 32)
                for t, (c0, w) in enumerate(C_TILES):
                    ins = act.activation(yo[b][0:w, t, :], bank(5 + t)[0:w, :], ACT.Copy, scale=0.5)
                ins.then_inc(sy["eout_ready"], 1)
                act.wait_ge(sy["eout_ready"], e + 1)
                for t, (c0, w) in enumerate(C_TILES):
                    act.dma_start(expert_out[bass.ds(e * CAP + c0, w)], yo[b][0:w, t, :]).then_inc(sy[f"eout{b}"], 16)

            xT_copy(0, 0)
            pairs(act, step)
            act.wait_ge(sy["eout0"], 16 * E)
            act.wait_ge(sy["eout1"], 16 * E)

        @block.tensor
        def _(pe):
            pe.transpose(bank(7)[0:E, 0:P], const["last"], ident).then_inc(sy["last_psum"], 1)

            def turn_rows(e, b, n, first):
                pe.wait_ge(sy[f"xg_in{b}"], n * 32 + 32)
                if not first:
                    pe.wait_ge(sy["exT_ready"], e)
                for kc in range(KC):
                    for t, (c0, w) in enumerate(C_TILES):
                        at = (kc % 2) * CAP + c0
                        ins = pe.transpose(bank(kc // 2)[:, at:at + w], xg[b][0:w, t, kc * P:(kc + 1) * P],
                                           ident[0:w, 0:w])
                ins.then_inc(sy["exT_psum"], 1)

            def step(e, n, b, first):
                pe.wait_ge(sy[f"ew_in{b}"], n * 48 + 48)
                pe.wait_ge(sy["exT_ready"], e + 1)
                for m, (m0, w) in enumerate(M_CHUNKS):
                    if not (first and b == 0):
                        pe.wait_ge(sy["eact_ready"], e * NM + (m + 1 - NM))
                    for gu in range(2):
                        ins = project_pe(pe, bank(2 + m)[0:w, gu * CAP:(gu + 1) * CAP],
                                         lambda kc: wgu[b][:, gu, kc, m0:m0 + w], lambda kc: xT[b][:, kc, :])
                    ins.then_inc(sy["egu_psum"], 1)
                if e is not E - 1:
                    turn_rows(e + 1, 1 - b, n + b, False)
                for t, (c0, w) in enumerate(C_TILES):
                    if t == 0 and not (first and b == 0):
                        pe.wait_ge(sy["eout_ready"], e)
                    for m, (m0, mw) in enumerate(M_CHUNKS):
                        if t == 0:
                            pe.wait_ge(sy["eact_ready"], e * NM + (m + 1))
                        ins = pe.matmul(bank(5 + t)[0:w, :], aT[b][0:mw, m, c0:c0 + w], wd[b][0:mw, m, :],
                                        start=(m == 0), stop=(m == NM - 1))
                ins.then_inc(sy["edown_psum"], 1)

            turn_rows(0, 0, 0, True)
            pairs(pe, step)

        @block.vector
        def _(dve):
            dve.wait_ge(sy["last_psum"], 1)
            sy.link(dve, "last_link", dve.tensor_reduce(last_c[:], bank(7)[0:E, 0:P], AX.X, ALU.max))
            dve.tensor_copy(last_i[:], last_c[:]).then_inc(sy["last_ready"], 1)

            def step(e, n, b, first):
                if not first:
                    dve.wait_ge(sy["edown_psum"], e - 1)
                for m, (m0, w) in enumerate(M_CHUNKS):
                    dve.wait_ge(sy["etanh_ready"], e * NM + (m + 1))
                    g = bank(2 + m)
                    dve.scalar_tensor_tensor(out=aT[b][0:w, m, :], in0=th[0:w, m, :], scalar=1.0,
                                             in1=g[0:w, 0:CAP], op0=ALU.add, op1=ALU.mult
                                             ).then_inc(sy["egate_ready"], 1)
                    dve.wait_ge(sy["egate_ready"], e * NM + (m + 1))
                    dve.tensor_tensor(aT[b][0:w, m, :], aT[b][0:w, m, :], g[0:w, CAP:2 * CAP], ALU.mult
                                      ).then_inc(sy["eact_ready"], 1)

            pairs(dve, step)


CONV = 4
MH = 4
XBC = D + 2 * P
NXBC = XBC // P
LH = 8
LD = S // LH
HPT = P // LD
LD_SCALE = float(np.float32(1.0) / np.sqrt(np.float32(LD)))
LE, LR, LK = 8, 16, 2
F = 2048
FC = F // P
SCALING = 2.0


def phase3(nc, sy, const, dr, base, nseq=NSEQ):
    with ExitStack() as ctx:
        def sb(name, shape, dt=F32):
            return ctx.enter_context(nc.sbuf_tensor(name, shape, dt))

        w_in = sb("w_in", [P, KC, D + XBC + MH])
        w_mo = sb("w_mo", [P, KC, D])
        w1 = sb("w1", [P, KC, F])
        w2 = sb("w2", [P, FC, D])
        a1 = sb("a1", [P, KC, P])
        b1l = sb("b1l", [P, F])
        a2 = sb("a2", [P, FC, P])
        b2l = sb("b2l", [P, D])
        wr = sb("wr", [P, KC, LE])
        norm_bc, bias2_bc = sb("norm_bc", [P, D]), sb("bias2_bc", [P, D])
        small = sb("small", [P, 64])
        conv_w = small[:, 0:24].rearrange("p (c k) -> p c k", k=CONV)
        conv_b = small[:, 24:30]
        dt_bias, a_log, d_skip = small[:, 32:36], small[:, 36:40], small[:, 40:44]
        gamma, br = small[:, 44:45], small[:, 48:56]
        bias1 = sb("bias1", [P, FC])
        neg_a = sb("neg_a", [P, MH])
        tri_gt = sb("tri_gt", [P, P])
        tri_le = sb("tri_le", [P, 3 * P])
        erow = sb("erow", [P, P])

        x, h, hT = sb("x3", [P, NT, D]), sb("h3", [P, NT, D]), sb("hT3", [P, KC, S])
        cx, cxT = sb("cx", [P, NT, D]), sb("cxT", [P, KC, S])
        zs = sb("zs", [P, NT, D])
        y = sb("y", [P, NT, D])
        slots, wk = sb("slots3", [P, NT, 8], I32), sb("wk", [P, NT, 8])
        scratch = sb("scratch", [P, 8192])
        st, mv = sb("st3", [P, NT, 6]), sb("mv3", [P, NT, 2])
        ve, rstd = sb("ve3", [P, NT]), sb("rstd3", [P, NT])

        yk = scratch[:, 0:NT * TOPK * D].rearrange("p (j k d) -> p j k d", j=NT, k=TOPK)

        def view(at, *shape):
            n = int(np.prod(shape))
            names = "abcd"[:len(shape)]
            ap = scratch[:, at:at + n]
            if len(shape) == 1:
                return ap
            return ap.rearrange(f"p ({' '.join(names)}) -> p {' '.join(names)}",
                                **{k: v for k, v in zip(names[1:], shape[1:])})

        raw, convh = view(0, NXBC, S), view(1536, NXBC, S)
        xbc = raw
        cth = view(3072, 2, S)
        xr, xdt = view(3584, NT, P), view(3840, NT, MH, P)
        trid = view(4864, MH, 3, P)
        decay, wgt = view(6400, 2, 3 * P), view(7168, 2, 3 * P)
        dts = sb("dts", [P, 10, NT * MH])
        ssq, grstd = sb("ssq", [P, NT * MH]), sb("grstd", [P, NT * MH])
        prob, probT = view(0, 2, 4, D), view(4096, 2, 4, D)
        smx, snm, ssum = sb("smx", [P, LH, 4]), sb("snm", [P, LH, 4]), sb("ssum", [P, LH, 4])
        mixT = view(0, FC, S)
        act2, ca = view(4096, 2, LK, S), view(5120, 3, LK, S)
        mrow = view(6656, NT, 4, P)
        maskT = sb("maskT", [P, 4, S])
        m0, m01, t2m, t2b = (sb(n, [P, S]) for n in ("m0", "m01", "t2m", "t2b"))
        lg = sb("lg", [P, NT, LE])
        lex, lpr, ltop, lidxf = (sb(n, [P, NT, 8]) for n in ("lex", "lpr", "ltop", "lidxf"))
        lidx = sb("lidx", [P, NT, 8], U32)
        lmax, lsum, lw = sb("lmax", [P, NT, 8]), sb("lsum", [P, NT]), sb("lw", [P, NT])

        ident, bank = const["ident"], const["bank"]
        block = ctx.enter_context(nc.Block())
        W_IN = 16 * 12

        @block.sync
        def _(sp):
            for dst, src in ((w_in, "w_in"), (w_mo, "w_mo"), (small, "small"), (bias1, "bias1"),
                             (norm_bc, "norm_bc"), (bias2_bc, "bias2_bc"), (wr, "wr"), (a1, "a1"), (b1l, "b1l"),
                             (a2, "a2"), (b2l, "b2l")):
                sp.dma_start(dst[:], dr[src]).then_inc(sy["w3_in"], 16)
            sp.dma_start(w1[:], dr["w1"]).then_inc(sy["w3b_in"], 16)
            sp.dma_start(w2[:], dr["w2"]).then_inc(sy["w3b_in"], 16)
            with sp.Fori(0, nseq) as i:
                for dst, src, sem in ((slots, "slots", "slots_in"), (x, "mid", "x3_in"), (wk, "route_w", "x3_in"),
                                      (cx, "ctx", "ctx3_in"), (cxT, "ctxT", "ctx3_in")):
                    sp.dma_start(dst[:], dr[src][bass.ds(i, 1)].rearrange("o p t d -> (o p) t d")
                                 ).then_inc(sy[sem], 16)
                sp.wait_ge(sy["x_out_ready"], 2)
                sp.dma_start(dr["out"][bass.ds(i, 1)].rearrange("o (t p) d -> (o p) t d", p=P), x[:]
                             ).then_inc(sy["out_done"], 16)
                sp.wait_ge(sy["out_done"], (i + 1) * 16)
                sy.clear_turn(sp, i, base)

        @block.gpsimd
        def _(pool):
            sy.link(pool, "init3_link", pool.memset(tri_le[:], 1.0))
            pool.affine_select(out=tri_le[:, 0:P], in_=tri_le[:, 0:P], compare_op=ALU.is_ge, fill=0.0, base=0,
                               pattern=[[1, P]], channel_multiplier=-1)
            pool.affine_select(out=tri_le[:, 2 * P:3 * P], in_=tri_le[:, 2 * P:3 * P], compare_op=ALU.is_ge,
                               fill=0.0, base=0, pattern=[[1, P]], channel_multiplier=-1)
            sy.link(pool, "init3_link", pool.memset(tri_gt[:], 1.0))
            pool.affine_select(out=tri_gt[:], in_=tri_gt[:], compare_op=ALU.is_gt, fill=0.0, base=0,
                               pattern=[[-1, P]], channel_multiplier=1)
            pool.iota(erow[:], pattern=[[1, LE], [0, LR]], base=0, channel_multiplier=0,
                      allow_small_or_imprecise_dtypes=True).then_inc(sy["init3"], 1)
            pool.wait_ge(sy["w3_in"], 16 * 11)
            with pool.Fori(0, nseq) as i:
                pool.wait_ge(sy["slots_in"], (i + 1) * 16)
                sy.alone(pool)
                for j in range(NT):
                    for k in range(TOPK):
                        pool.indirect_dma_start(
                            out=yk[:, j, k, :], out_offset=None, in_=dr["expert_out"],
                            in_offset=bass.IndirectOffsetOnAxis(ap=slots[:, j, k:k + 1], axis=0)
                        ).then_inc(sy["yk_in"], 16)
                rstd_pool(pool, sy, 0, mv, ve, rstd, const["minus_half"])
                pool.wait_ge(sy["dA_ready"], 1)
                dt, da = dts[:, 8, :], dts[:, 9, :]
                for hd in range(MH):
                    for m, (src, t) in enumerate(((tri_gt[:], 0), (tri_gt[:], 1), (tri_le[:, P:2 * P], 1))):
                        ins = pool.tensor_scalar(trid[:, hd, m, :], src, da[:, t * MH + hd:t * MH + hd + 1], None,
                                                 ALU.mult)
                    ins.then_inc(sy["tri_ready"], 1)
                pool.wait_ge(sy["xrows_ready"], 1)
                for t in range(NT):
                    for hd in range(MH):
                        ins = pool.tensor_scalar(xdt[:, t, hd, :], xr[:, t, :], dt[:, t * MH + hd:t * MH + hd + 1],
                                                 None, ALU.mult)
                ins.then_inc(sy["xdt_ready"], 1)
                for hd in range(MH):
                    pool.wait_ge(sy["decay_ready"], hd + 1)
                    pool.tensor_tensor(decay[:, hd % 2, :], decay[:, hd % 2, :], tri_le[:], ALU.mult
                                       ).then_inc(sy["decaymask_ready"], 1)
                pool.wait_ge(sy["sumsq_ready"], 1)
                sy.link(pool, "pool_link", pool.tensor_scalar(ssq[:], ssq[:], 1.0 / P, EPS, ALU.mult, ALU.add))
                pool.tensor_tensor(grstd[:], ssq[:], const["minus_half"][:, 0:NT * MH], ALU.pow
                                   ).then_inc(sy["gated_norm"], 1)
                rstd_pool(pool, sy, 1, mv, ve, rstd, const["minus_half"])
                for n in range(4 * LH):
                    hd, lc = n // 4, n % 4
                    pool.wait_ge(sy["smax_ready"], n + 1)
                    pool.tensor_scalar(snm[:, hd, lc:lc + 1], smx[:, hd, lc:lc + 1], -LD_SCALE, None, ALU.mult
                                       ).then_inc(sy["snegmax_ready"], 1)
                rstd_pool(pool, sy, 2, mv, ve, rstd, const["minus_half"])
                for f in range(FC):
                    pool.wait_ge(sy["ca_ready"], f + 1)
                    pool.tensor_tensor(mixT[:, f, :], ca[:, f % 3, 0, :], ca[:, f % 3, 1, :], ALU.add
                                       ).then_inc(sy["mix_ready"], 1)
                sy.end_turn(pool, i, base, "pool_link")

        @block.scalar
        def _(act):
            act.wait_ge(sy["w3_in"], 16 * 11)
            act.activation(neg_a[:], a_log, ACT.Exp).then_inc(sy["a_exp"], 1)
            with act.Fori(0, nseq) as i:
                def cols_copy(k):
                    for j in range(NT):
                        act.wait_ge(sy["rowsT_psum"], NT * k + j + 1)
                        act.activation(hT[:, :, j * P:(j + 1) * P],
                                       bank(j)[:, :].rearrange("p (c t) -> p c t", c=KC), ACT.Copy
                                       ).then_inc(sy["colsT_ready"], 1)

                cols_copy(0)
                act.wait_ge(sy["dtabs_ready"], 1)
                act.activation(dts[:, 2, :], dts[:, 1, :], ACT.Exp, scale=-1.0).then_inc(sy["dtexp_ready"], 1)
                act.wait_ge(sy["dtone_ready"], 1)
                act.activation(dts[:, 4, :], dts[:, 3, :], ACT.Ln).then_inc(sy["dtln_ready"], 1)
                for c in range(NXBC + 1):
                    if c < NXBC:
                        act.wait_ge(sy["xbc_psum"], c + 1)
                        act.activation(raw[:, c, :], bank(2 + c % 2)[:, 0:S], ACT.Copy
                                       ).then_inc(sy["xbc_raw_ready"], 1)
                    if c >= 1:
                        act.wait_ge(sy["conv_ready"], c)
                        if c >= 3:
                            act.wait_ge(sy["xbc_ready"], c - 2)
                        act.activation(cth[:, (c - 1) % 2, :], convh[:, c - 1, :], ACT.Tanh
                                       ).then_inc(sy["convtanh_ready"], 1)
                for j in range(NT):
                    act.wait_ge(sy["z_psum"], j + 1)
                    act.activation(zs[:, j, :], bank(4 + j)[:, :], ACT.Tanh, scale=0.5
                                   ).then_inc(sy["ztanh_ready"], 1)
                act.wait_ge(sy["xrows_psum"], 1)
                act.activation(xr[:], bank(6)[:, 0:NT * P].rearrange("p (t d) -> p t d", t=NT), ACT.Copy
                               ).then_inc(sy["xrows_ready"], 1)
                for hd in range(MH):
                    act.wait_ge(sy["decay_psum"], hd + 1)
                    if hd >= 2:
                        act.wait_ge(sy["w_ready"], hd - 1)
                    act.activation(decay[:, hd % 2, :], bank(hd % 2)[:, 0:3 * P], ACT.Exp
                                   ).then_inc(sy["decay_ready"], 1)
                for j in range(NT):
                    act.wait_ge(sy["gated_ready"], j + 1)
                    for hd in range(MH):
                        ins = act.activation(h[:, j, hd * P:(hd + 1) * P], y[:, j, hd * P:(hd + 1) * P], ACT.Square,
                                             accum_out=ssq[:, j * MH + hd:j * MH + hd + 1])
                ins.then_inc(sy["sumsq_ready"], 1)
                cols_copy(1)
                def copy_blocks(n):
                    act.wait_ge(sy["sT_psum"], n + 1)
                    hd, lc = n // 4, n % 4
                    act.activation(probT[:, hd % 2, :, lc * P:(lc + 1) * P],
                                   bank(4 + lc % 2)[:, :].rearrange("p (c t) -> p c t", c=4), ACT.Copy
                                   ).then_inc(sy["sT_act"], 1)

                for n in range(4 * LH + 4):
                    if n < 4 * LH:
                        hd, lc = n // 4, n % 4
                        act.wait_ge(sy["snegmax_ready"], n + 1)
                        if hd >= 2:
                            act.wait_ge(sy["sT_psum"], n - 7)
                        act.activation(prob[:, hd % 2, lc, :], bank(lc)[:, :], ACT.Exp, bias=snm[:, hd, lc:lc + 1],
                                       scale=LD_SCALE, accum_out=ssum[:, hd, lc:lc + 1]).then_inc(sy["sexp_ready"], 1)
                    if n >= 4 and n % 2 == 0:
                        if (n - 4) % 4 == 0 and n >= 12:
                            act.wait_ge(sy["ret_psum"], (n - 4) // 4 - 1)
                        copy_blocks(n - 4)
                cols_copy(2)
                for j in range(NT):
                    act.wait_ge(sy["moe_negmax"], j + 1)
                    act.activation(lex[:, j, :], lg[:, j, :], ACT.Exp, bias=lw[:, j:j + 1],
                                   accum_out=lsum[:, j:j + 1]).then_inc(sy["moe_exp"], 1)
                for j in range(NT):
                    act.wait_ge(sy["maskT_psum"], j + 1)
                    act.activation(maskT[:, :, j * P:(j + 1) * P],
                                   bank(j)[:, :].rearrange("p (c t) -> p c t", c=4), ACT.Copy
                                   ).then_inc(sy["maskT_ready"], 1)
                for f in range(FC + 1):
                    if f < FC:
                        act.wait_ge(sy["base_psum"], f + 1)
                        if f >= 2:
                            act.wait_ge(sy["ca_ready"], f - 1)
                        act.activation(act2[:, f % 2, 0, :], bank(f % 4)[:, 0:S], ACT.Gelu_apprx_tanh,
                                       bias=bias1[:, f:f + 1]).then_inc(sy["gelu0_ready"], 1)
                    if f >= 1:
                        g = f - 1
                        act.wait_ge(sy["base1_psum"], g + 1)
                        act.activation(act2[:, g % 2, 1, :], bank(g % 4)[:, 0:S], ACT.Gelu_apprx_tanh,
                                       bias=bias1[:, g:g + 1]).then_inc(sy["gelu1_ready"], 1)
                sy.end_turn(act, i, base, "act_link")

        @block.tensor
        def _(pe):
            pe.wait_ge(sy["w3_in"], 16 * 11)
            pe.wait_ge(sy["w3b_in"], 32)
            pe.wait_ge(sy["init3"], 1)
            with pe.Fori(0, nseq) as i:
                def rows_to_cols(src, ready, at):
                    for j in range(NT):
                        pe.wait_ge(ready, at + j + 1)
                        transposes_pe(pe, ident, src, bank(j), j).then_inc(sy["rowsT_psum"], 1)

                rows_to_cols(h, sy["normed_ready"], 0)
                pe.wait_ge(sy["colsT_ready"], NT)
                for j in range(NT):
                    ins = project_pe(pe, bank(6)[:, j * MH:(j + 1) * MH], lambda kc: hT[:, kc, j * P:(j + 1) * P],
                                     lambda kc: w_in[:, kc, D + XBC:D + XBC + MH])
                ins.then_inc(sy["dt_psum"], 1)
                for c in range(NXBC):
                    if c >= 2:
                        pe.wait_ge(sy["xbc_raw_ready"], c - 1)
                    project_pe(pe, bank(2 + c % 2)[:, 0:S], lambda kc: w_in[:, kc, D + c * P:D + (c + 1) * P],
                               lambda kc: hT[:, kc, :]).then_inc(sy["xbc_psum"], 1)
                for j in range(NT):
                    project_pe(pe, bank(4 + j)[:, :], lambda kc: hT[:, kc, j * P:(j + 1) * P],
                               lambda kc: w_in[:, kc, 0:D]).then_inc(sy["z_psum"], 1)
                pe.wait_ge(sy["xbc_ready"], 1)
                pe.wait_ge(sy["tri_ready"], 1)
                for t in range(NT):
                    ins = pe.transpose(bank(6)[:, t * P:(t + 1) * P], xbc[:, 0, t * P:(t + 1) * P], ident)
                ins.then_inc(sy["xrows_psum"], 1)
                pe.wait_ge(sy["xbc_ready"], NXBC)
                for s in range(MH + 1):
                    if s < MH:
                        pe.wait_ge(sy["tri_ready"], s + 1)
                        if s >= 2:
                            pe.wait_ge(sy["w_ready"], s - 1)
                        b, g = bank(s % 2), bank(2 + s % 2)
                        pe.matmul(b[:, 0:2 * P], trid[:, s, 0, :], tri_le[:, 0:2 * P], start=True, stop=False,
                                  skip_group_check=True)
                        pe.matmul(b[:, P:2 * P], trid[:, s, 2, :], tri_le[:, 0:P], start=False, stop=True,
                                  skip_group_check=True)
                        pe.matmul(b[:, 2 * P:3 * P], trid[:, s, 1, :], tri_le[:, 0:P], start=True, stop=True,
                                  skip_group_check=True).then_inc(sy["decay_psum"], 1)
                        pe.matmul(g[:, 0:2 * P], xbc[:, 1, 0:P], xbc[:, 2 + s, :], start=True, stop=True)
                        pe.matmul(g[:, 2 * P:3 * P], xbc[:, 1, P:S], xbc[:, 2 + s, P:S], start=True, stop=True
                                  ).then_inc(sy["bc_psum"], 1)
                    if s >= 1:
                        hd = s - 1
                        if hd == 0:
                            pe.wait_ge(sy["zs_ready"], NT)
                            pe.wait_ge(sy["xdt_ready"], 1)
                        pe.wait_ge(sy["w_ready"], hd + 1)
                        w = wgt[:, hd % 2, :]
                        cols = slice(hd * P, (hd + 1) * P)
                        pe.matmul(bank(4)[:, cols], w[:, 0:P], xdt[:, 0, hd, :], start=True, stop=True)
                        pe.matmul(bank(5)[:, cols], w[:, P:2 * P], xdt[:, 0, hd, :], start=True, stop=False)
                        pe.matmul(bank(5)[:, cols], w[:, 2 * P:3 * P], xdt[:, 1, hd, :], start=False, stop=True
                                  ).then_inc(sy["y_psum"], 1)
                rows_to_cols(y, sy["attn_ready"], 0)
                pe.wait_ge(sy["colsT_ready"], 2 * NT)
                for j in range(NT):
                    project_pe(pe, bank(2 + j)[:, :], lambda kc: hT[:, kc, j * P:(j + 1) * P],
                               lambda kc: w_mo[:, kc, :]).then_inc(sy["out_psum"], 1)
                pe.wait_ge(sy["normed_ready"], 2 * NT)
                pe.wait_ge(sy["ctx3_in"], (i + 1) * 32)
                for n in range(4 * LH + 6):
                    if n < 4 * LH:
                        hd, lc = n // 4, n % 4
                        j, r = hd // HPT, (hd % HPT) * LD
                        if n >= 4:
                            pe.wait_ge(sy["sexp_ready"], n - 3)
                        pe.matmul(bank(lc)[:, :], h[r:r + LD, j, lc * P:(lc + 1) * P], cx[r:r + LD, j, :],
                                  start=True, stop=True).then_inc(sy["s_psum"], 1)
                    if 4 <= n < 4 * LH + 4:
                        m = n - 4
                        hd, lc = m // 4, m % 4
                        pe.wait_ge(sy["snormed_ready"], m + 1)
                        if m >= 2:
                            pe.wait_ge(sy["sT_act" if m % 2 == 0 else "sT_dve"], m // 2)
                        for mc in range(4):
                            ins = pe.transpose(bank(4 + lc % 2)[:, mc * P:(mc + 1) * P],
                                               prob[:, hd % 2, lc, mc * P:(mc + 1) * P], ident)
                        ins.then_inc(sy["sT_psum"], 1)
                    if n >= 9 and (n - 9) % 4 == 0:
                        hd = (n - 9) // 4
                        j, r = hd // HPT, (hd % HPT) * LD
                        pe.wait_ge(sy["sT_act"], 2 * hd + 2)
                        pe.wait_ge(sy["sT_dve"], 2 * hd + 2)
                        for mc in range(4):
                            ins = pe.matmul(bank(6 + j)[r:r + LD, :], cxT[:, mc, hd * LD:(hd + 1) * LD],
                                            probT[:, hd % 2, mc, :], start=(mc == 0), stop=(mc == 3),
                                            tile_position=(0, r))
                        ins.then_inc(sy["ret_psum"], 1)
                rows_to_cols(h, sy["normed_ready"], 2 * NT)
                pe.wait_ge(sy["colsT_ready"], 3 * NT)
                for j in range(NT):
                    ins = project_pe(pe, bank(4)[:, j * LE:(j + 1) * LE], lambda kc: hT[:, kc, j * P:(j + 1) * P],
                                     lambda kc: wr[:, kc, :])
                ins.then_inc(sy["moe_psum"], 1)
                project_pe(pe, bank(5)[:, 0:S], lambda kc: a1[:, kc, :], lambda kc: hT[:, kc, :]
                           ).then_inc(sy["t1_psum"], 1)
                for j in range(NT):
                    pe.wait_ge(sy["mask_rows"], j + 1)
                    for m in range(4):
                        ins = pe.transpose(bank(j)[:, m * P:(m + 1) * P], mrow[:, j, m, :], ident)
                    ins.then_inc(sy["maskT_psum"], 1)
                pe.wait_ge(sy["m0_ready"], 1)
                for f in range(FC + 3):
                    if f < FC:
                        if f >= 4:
                            pe.wait_ge(sy["gelu1_ready"], f - 3)
                        for kc in range(KC):
                            pe.matmul(bank(f % 4)[:, 0:S], w1[:, kc, f * P:(f + 1) * P], hT[:, kc, :],
                                      start=(kc == 0), stop=False, skip_group_check=True)
                        pe.matmul(bank(f % 4)[:, 0:S], b1l[:, f * P:(f + 1) * P], m0[:], start=False, stop=True,
                                  skip_group_check=True).then_inc(sy["base_psum"], 1)
                    if 1 <= f <= FC:
                        g = f - 1
                        pe.wait_ge(sy["gelu0_ready"], g + 1)
                        pe.matmul(bank(g % 4)[:, 0:S], b1l[:, g * P:(g + 1) * P], m01[:], start=False, stop=True,
                                  skip_group_check=True).then_inc(sy["base1_psum"], 1)
                    if f >= 3:
                        g = f - 3
                        pe.wait_ge(sy["ca_ready"], g + 1)
                        pe.matmul(bank(4)[:, :], a2[:, g, :], ca[:, g % 3].rearrange("p k t -> p (k t)"),
                                  start=(g == 0), stop=(g == FC - 1)).then_inc(sy["t2_psum"], 1)
                        pe.wait_ge(sy["mix_ready"], g + 1)
                        for j in range(NT):
                            pe.matmul(bank(6 + j)[:, :], mixT[:, g, j * P:(j + 1) * P], w2[:, g, :],
                                      start=(g == 0), stop=False)
                pe.wait_ge(sy["t2m_ready"], 1)
                for j in range(NT):
                    pe.matmul(bank(6 + j)[:, :], t2m[:, j * P:(j + 1) * P], b2l[:], start=False, stop=True
                              ).then_inc(sy["y_out_psum"], 1)
                sy.end_turn(pe, i, base)

        @block.vector
        def _(dve):
            def ln(ins):
                sy.link(dve, "dve_link", ins)

            dve.wait_ge(sy["w3_in"], 16 * 11)
            dve.wait_ge(sy["init3"], 1)
            dve.wait_ge(sy["a_exp"], 1)
            sy.link(dve, "dve_link3", dve.tensor_scalar(neg_a[:], neg_a[:], -1.0, None, ALU.mult))
            sy.link(dve, "dve_link3", dve.tensor_scalar(small[:, 0:30], small[:, 0:30], 0.5, None, ALU.mult))
            with dve.Fori(0, nseq) as i:
                dve.wait_ge(sy["x3_in"], (i + 1) * 32)
                dve.wait_ge(sy["yk_in"], (i + 1) * (16 * NT * TOPK))
                for k in range(TOPK):
                    for j in range(NT):
                        ins = dve.scalar_tensor_tensor(out=x[:, j, :], in0=yk[:, j, k, :], scalar=wk[:, j, k:k + 1],
                                                       in1=x[:, j, :], op0=ALU.mult, op1=ALU.add)
                    ln(ins)
                layernorm_rows(dve, sy, 0, x, h, st, mv, rstd)
                dve.wait_ge(sy["dt_psum"], 1)
                v, av, e, w, lnw, d, m, sp_, dt, da = (dts[:, k, :] for k in range(10))
                ln(dve.tensor_tensor(v.rearrange("p (t h) -> p t h", t=NT),
                                     bank(6)[:, 0:NT * MH].rearrange("p (t h) -> p t h", t=NT),
                                     dt_bias.unsqueeze(1).broadcast_to([P, NT, MH]), ALU.add))
                dve.scalar_tensor_tensor(out=av, in0=v, scalar=-1.0, in1=v, op0=ALU.mult, op1=ALU.max).then_inc(sy["dtabs_ready"], 1)
                dve.wait_ge(sy["dtexp_ready"], 1)
                dve.tensor_scalar(w, e, 1.0, None, ALU.add).then_inc(sy["dtone_ready"], 1)
                dve.wait_ge(sy["dtln_ready"], 1)
                ln(dve.tensor_scalar(d, w, -1.0, None, ALU.add))
                ln(dve.tensor_scalar(m, d, 0.0, None, ALU.is_equal))
                ln(dve.tensor_tensor(d, d, m, ALU.add))
                ln(dve.reciprocal(d, d))
                ln(dve.tensor_tensor(m, m, lnw, ALU.add))
                ln(dve.tensor_tensor(m, m, d, ALU.mult))
                ln(dve.tensor_tensor(m, m, e, ALU.mult))
                ln(dve.scalar_tensor_tensor(out=dt, in0=v, scalar=0.0, in1=m, op0=ALU.max, op1=ALU.add))
                dve.tensor_tensor(da.rearrange("p (t h) -> p t h", t=NT), dt.rearrange("p (t h) -> p t h", t=NT),
                                  neg_a[:].unsqueeze(1).broadcast_to([P, NT, MH]), ALU.mult
                                  ).then_inc(sy["dA_ready"], 1)
                for c in range(NXBC + 1):
                    if c < NXBC:
                        dve.wait_ge(sy["xbc_raw_ready"], c + 1)
                        ln(dve.tensor_scalar(convh[:, c, :], raw[:, c, :], conv_w[:, c, 3:4], conv_b[:, c:c + 1],
                                             ALU.mult, ALU.add))
                        for k in range(CONV - 1):
                            lag = CONV - 1 - k
                            ins = dve.scalar_tensor_tensor(
                                out=convh[:, c, lag:S], in0=raw[:, c, 0:S - lag], scalar=conv_w[:, c, k:k + 1],
                                in1=convh[:, c, lag:S], op0=ALU.mult, op1=ALU.add)
                            if k < CONV - 2:
                                ln(ins)
                        ins.then_inc(sy["conv_ready"], 1)
                    if c >= 1:
                        dve.wait_ge(sy["convtanh_ready"], c)
                        dve.scalar_tensor_tensor(out=xbc[:, c - 1, :], in0=cth[:, (c - 1) % 2, :], scalar=1.0,
                                                 in1=convh[:, c - 1, :], op0=ALU.add, op1=ALU.mult
                                                 ).then_inc(sy["xbc_ready"], 1)
                for j in range(NT):
                    dve.wait_ge(sy["ztanh_ready"], j + 1)
                    dve.scalar_tensor_tensor(out=zs[:, j, :], in0=zs[:, j, :], scalar=1.0, in1=bank(4 + j)[:, :],
                                             op0=ALU.add, op1=ALU.mult).then_inc(sy["zs_ready"], 1)
                for hd in range(MH):
                    dve.wait_ge(sy["decaymask_ready"], hd + 1)
                    dve.wait_ge(sy["bc_psum"], hd + 1)
                    if hd >= 2:
                        dve.wait_ge(sy["y_psum"], hd - 1)
                    dve.tensor_tensor(wgt[:, hd % 2, :], decay[:, hd % 2, :], bank(2 + hd % 2)[:, 0:3 * P], ALU.mult
                                      ).then_inc(sy["w_ready"], 1)
                dve.wait_ge(sy["y_psum"], MH)
                for j in range(NT):
                    for hd in range(MH):
                        c = slice(hd * P, (hd + 1) * P)
                        ins = dve.scalar_tensor_tensor(out=y[:, j, c], in0=xr[:, j, :], scalar=d_skip[:, hd:hd + 1],
                                                       in1=bank(4 + j)[:, c], op0=ALU.mult, op1=ALU.add)
                    ln(ins)
                    dve.scalar_tensor_tensor(out=y[:, j, :], in0=y[:, j, :], scalar=0.5, in1=zs[:, j, :],
                                             op0=ALU.mult, op1=ALU.mult).then_inc(sy["gated_ready"], 1)
                dve.wait_ge(sy["gated_norm"], 1)
                for j in range(NT):
                    ln(dve.tensor_tensor(heads_view(y[:, j, :], MH), heads_view(y[:, j, :], MH),
                                         grstd[:, j * MH:(j + 1) * MH].unsqueeze(2).broadcast_to([P, MH, P]),
                                         ALU.mult))
                    dve.tensor_tensor(y[:, j, :], y[:, j, :], norm_bc[:], ALU.mult).then_inc(sy["attn_ready"], 1)
                for j in range(NT):
                    dve.wait_ge(sy["out_psum"], j + 1)
                    ins = dve.tensor_tensor(x[:, j, :], x[:, j, :], bank(2 + j)[:, :], ALU.add)
                ln(ins)
                layernorm_rows(dve, sy, 1, x, h, st, mv, rstd)
                rinv = y
                for n in range(4 * LH + 6):
                    if n < 4 * LH:
                        hd, lc = n // 4, n % 4
                        dve.wait_ge(sy["s_psum"], n + 1)
                        dve.tensor_reduce(smx[:, hd, lc:lc + 1], bank(lc)[:, :], AX.X, ALU.max
                                          ).then_inc(sy["smax_ready"], 1)
                    if 2 <= n < 4 * LH + 2:
                        m = n - 2
                        hd, lc = m // 4, m % 4
                        dve.wait_ge(sy["sexp_ready"], m + 1)
                        ln(dve.reciprocal(ssum[:, hd, lc:lc + 1], ssum[:, hd, lc:lc + 1]))
                        dve.tensor_scalar(prob[:, hd % 2, lc, :], prob[:, hd % 2, lc, :], ssum[:, hd, lc:lc + 1],
                                          None, ALU.mult).then_inc(sy["snormed_ready"], 1)
                    if n >= 5 and n % 2 == 1 and n - 4 < 4 * LH:
                        m = n - 4
                        hd, lc = m // 4, m % 4
                        dve.wait_ge(sy["sT_psum"], m + 1)
                        if lc == 1 and hd >= 2:
                            dve.wait_ge(sy["ret_psum"], hd - 1)
                        dve.tensor_copy(probT[:, hd % 2, :, lc * P:(lc + 1) * P],
                                        bank(4 + lc % 2)[:, :].rearrange("p (c t) -> p c t", c=4)
                                        ).then_inc(sy["sT_dve"], 1)
                for j in range(NT):
                    dve.wait_ge(sy["ret_psum"], HPT * (j + 1))
                    ins = dve.scalar_tensor_tensor(out=x[:, j, :], in0=bank(6 + j)[:, :], scalar=gamma,
                                                   in1=x[:, j, :], op0=ALU.mult, op1=ALU.add)
                ln(ins)
                layernorm_rows(dve, sy, 2, x, h, st, mv, rstd)
                dve.wait_ge(sy["moe_psum"], 1)
                for j in range(NT):
                    ln(dve.tensor_tensor(lg[:, j, :], bank(4)[:, j * LE:(j + 1) * LE], br, ALU.add))
                    ln(dve.max(lmax[:, j, :], lg[:, j, :]))
                    dve.tensor_scalar(lw[:, j:j + 1], lmax[:, j, 0:1], -1.0, None, ALU.mult
                                      ).then_inc(sy["moe_negmax"], 1)
                for j in range(NT):
                    dve.wait_ge(sy["moe_exp"], j + 1)
                    ln(dve.reciprocal(lsum[:, j:j + 1], lsum[:, j:j + 1]))
                    ln(dve.tensor_scalar(lpr[:, j, :], lex[:, j, :], lsum[:, j:j + 1], None, ALU.mult))
                    ln(dve.max(ltop[:, j, :], lpr[:, j, :]))
                    ln(dve.max_index(lidx[:, j, :], ltop[:, j, :], lpr[:, j, :]))
                    ln(dve.tensor_copy(lidxf[:, j, :], lidx[:, j, :]))
                    for k in range(LK):
                        dve.tensor_scalar(mrow[:, j, k, :], erow[:], lidxf[:, j, k:k + 1], SCALING, ALU.is_equal,
                                          ALU.mult)
                        ins = dve.tensor_scalar(mrow[:, j, LK + k, :], tri_le[:, P:2 * P], ltop[:, j, k:k + 1], None,
                                                ALU.mult)
                    ins.then_inc(sy["mask_rows"], 1)
                    ln(dve.tensor_tensor(lw[:, j:j + 1], ltop[:, j, 0:1], ltop[:, j, 1:2], ALU.add))
                    ln(dve.scalar_tensor_tensor(out=x[:, j, :], in0=bias2_bc[:], scalar=lw[:, j:j + 1],
                                                in1=x[:, j, :], op0=ALU.mult, op1=ALU.add))
                dve.wait_ge(sy["t1_psum"], 1)
                dve.wait_ge(sy["maskT_ready"], NT)
                ln(dve.tensor_tensor(m0[:], bank(5)[:, 0:S], maskT[:, 0, :], ALU.mult))
                ln(dve.tensor_tensor(m01[:], bank(5)[:, 0:S], maskT[:, 1, :], ALU.mult))
                dve.tensor_tensor(m01[:], m01[:], m0[:], ALU.subtract).then_inc(sy["m0_ready"], 1)
                for f in range(FC):
                    dve.wait_ge(sy["gelu1_ready"], f + 1)
                    if f >= 3:
                        dve.wait_ge(sy["t2_psum"], f - 2)
                        dve.wait_ge(sy["mix_ready"], f - 2)
                    dve.tensor_tensor(ca[:, f % 3], act2[:, f % 2], maskT[:, 2:4, :], ALU.mult
                                      ).then_inc(sy["ca_ready"], 1)
                dve.wait_ge(sy["t2_psum"], FC)
                ln(dve.tensor_tensor(t2m[:], bank(4)[:, 0:S], maskT[:, 0, :], ALU.mult))
                ln(dve.tensor_tensor(t2b[:], bank(4)[:, S:2 * S], maskT[:, 1, :], ALU.mult))
                dve.tensor_tensor(t2m[:], t2m[:], t2b[:], ALU.add).then_inc(sy["t2m_ready"], 1)
                for j in range(NT):
                    dve.wait_ge(sy["y_out_psum"], j + 1)
                    dve.tensor_tensor(x[:, j, :], x[:, j, :], bank(6 + j)[:, :], ALU.add
                                      ).then_inc(sy["x_out_ready"], 1)
                sy.end_turn(dve, i, base, "dve_link")


def constants(nc, sy, ctx):
    ident = ctx.enter_context(nc.sbuf_tensor("ident", [P, P], F32))
    iota_t = ctx.enter_context(nc.sbuf_tensor("iota_row", [P, E], F32))
    minus_half = ctx.enter_context(nc.sbuf_tensor("minus_half", [P, 16], F32))
    psum = ctx.enter_context(nc.psum_tensor("psum", [P, 8, 512], F32))
    last = ctx.enter_context(nc.sbuf_tensor("last_token", [P, E], F32))
    tri_lt = ctx.enter_context(nc.sbuf_tensor("tri_lt", [P, P], F32))
    ones = ctx.enter_context(nc.sbuf_tensor("ones", [P, P], F32))
    with nc.Block() as block:
        @block.gpsimd
        def _(pool):
            pool.memset(minus_half[:], -0.5)
            pool.memset(ones[:], 1.0)
            sy.link(pool, "const_link", pool.memset(tri_lt[:], 1.0))
            pool.affine_select(out=tri_lt[:], in_=tri_lt[:], compare_op=ALU.is_gt, fill=0.0, base=0,
                               pattern=[[1, P]], channel_multiplier=-1)
            sy.link(pool, "const_link", pool.memset(ident[:], 0.0))
            pool.affine_select(out=ident[:], in_=ident[:], compare_op=ALU.not_equal, fill=1.0, base=0,
                               pattern=[[-1, P]], channel_multiplier=1).then_inc(sy["const_ready"], 1)
            pool.iota(iota_t[:], pattern=[[1, E]], base=0, channel_multiplier=0,
                      allow_small_or_imprecise_dtypes=True).then_inc(sy["const_ready"], 1)
            pool.wait_ge(sy["const_ready"], 2)
    return {"ident": ident[:], "iota": iota_t[:], "minus_half": minus_half[:], "bank": lambda b: psum[:, b, :],
            "last": last[:], "tri_lt": tri_lt[:], "ones": ones[:]}


def program(nc, dr, phases=(1, 2, 3), nseq=NSEQ, nexp=E):
    with ExitStack() as ctx:
        sy = Sync(nc, ctx)
        for n in ("turn_done", "turn_go"):
            sy[n]
        const = constants(nc, sy, ctx)
        dr["normed_rows"] = dr.get("normed_rows", None) or nc.dram_tensor("normed_rows", [NSEQ, S, D], F32).ap()
        for name, shape in (("mid", [NSEQ, P, NT, D]), ("route_w", [NSEQ, P, NT, 8]), ("route_e", [NSEQ, P, NT, 8]), ("expert_out", [E * CAP, D])):
            if name not in dr:
                dr[name] = nc.dram_tensor(name, shape, F32).ap()
        for name, shape in (("slots", [NSEQ, P, NT, 8]), ("slot_token", [E * CAP, 1])):
            if name not in dr:
                dr[name] = nc.dram_tensor(name, shape, I32).ap()
        if 1 in phases:
            phase1(nc, sy, const, dr, 0, nseq)
        if 2 in phases:
            phase2(nc, sy, const, dr)
        if 3 in phases:
            phase3(nc, sy, const, dr, nseq if 1 in phases else 0, nseq)


def cols_layout(w):
    o, i = w.shape
    return w.T.reshape(i // P, P, o).transpose(1, 0, 2)


def host_layout(a):
    a = {k: np.asarray(v) for k, v in a.items()}
    inv = (1.0 / np.power(np.float32(10000.0), np.arange(0, HD, 2, dtype=np.float32) / np.float32(HD))).astype(np.float32)
    freqs = np.outer(np.arange(S, dtype=np.float32), inv).astype(np.float32)
    emb = np.concatenate([freqs, freqs], -1)
    rot = np.zeros((P, P), np.float32)
    for i in range(0, P, 2):
        rot[i + 1, i], rot[i, i + 1] = -1.0, 1.0
    q, k = np.arange(P)[:, None], np.arange(P)[None, :]
    k1 = np.arange(WINDOW, S)[None, :]
    keep = np.concatenate([(q >= k) & (q - k < WINDOW), (q + P >= k1) & (q + P - k1 < WINDOW)], 1)
    bc = lambda v: np.broadcast_to(v.reshape(1, -1), (P, v.size))
    tokens = lambda t: t.reshape(NSEQ, NT, P, -1).transpose(0, 2, 1, 3)
    d = {
        "x": tokens(a["x"]),
        "ctxT": a["ctx_2048"].transpose(0, 2, 1).reshape(NSEQ, KC, P, S).transpose(0, 2, 1, 3),
        "mask": a["mask_BxS2_ik0"].reshape(NSEQ, NT, P).transpose(0, 2, 1),
        "w_qkv": cols_layout(a["L0_attn_w_qkv"]), "w_out": cols_layout(a["L0_attn_w_out"]),
        "w_gate": cols_layout(a["L0_ffn_gate_weight"]),
        "w_sg": cols_layout(a["L0_ffn_Sg"]), "w_su": cols_layout(a["L0_ffn_Su"]), "w_sd": a["L0_ffn_Sd"].T,
        "cosT": np.tile(np.cos(emb).T, (HPC, 1)), "sinT": np.tile(np.sin(emb).T, (HPC, 1)), "rot": rot,
        "wmask": np.where(keep, 0.0, NEG).astype(np.float32),
        "bq": a["L0_xattn_bq"].reshape(KC, P).T, "bk": a["L0_xattn_bk"].reshape(KC, P).T,
        "rows_bc": np.stack([bc(a["L0_xattn_" + n]) for n in ("bv", "bo", "ln_gamma", "ln_beta")], 1),
        "rs": np.broadcast_to(a["L0_xattn_residual_scale"].reshape(1, 1), (P, 1)),
    }
    small = np.zeros((P, 64), np.float32)
    small[:, 0:24] = a["L1_attn_conv_w"].reshape(NXBC, P, CONV).transpose(1, 0, 2).reshape(P, -1)
    small[:, 24:30] = a["L1_attn_conv_b"].reshape(NXBC, P).T
    small[:, 32:36], small[:, 36:40], small[:, 40:44] = a["L1_attn_dt_bias"], a["L1_attn_A_log"], a["L1_attn_D"]
    small[:, 44], small[:, 48:56] = a["L1_xattn_gamma"], a["L1_ffn_br"]
    d |= {
        "w_gu": np.stack([a["L0_ffn_W" + n].transpose(0, 2, 1).reshape(E, KC, P, M).transpose(0, 2, 1, 3)
                          for n in "gu"], 2),
        "w_d": a["L0_ffn_Wd"].transpose(0, 2, 1),
        "ctx": tokens(a["ctx_2048"]), "small": small, "bias1": a["L1_ffn_b1"].reshape(FC, P).T,
        "w_in": cols_layout(a["L1_attn_in_proj_w"]), "w_mo": cols_layout(a["L1_attn_out_proj_w"]),
        "norm_bc": bc(a["L1_attn_norm_w"]), "bias2_bc": bc(a["L1_ffn_b2"]),
        "wr": cols_layout(a["L1_ffn_Wr"].T), "w1": cols_layout(a["L1_ffn_W1"].T),
        "w2": cols_layout(a["L1_ffn_W2"].T), "a1": cols_layout(a["L1_ffn_A1"].reshape(LE * LR, D)),
        "b1l": a["L1_ffn_B1"].transpose(0, 2, 1).reshape(LE * LR, F),
        "a2": cols_layout(a["L1_ffn_A2"].reshape(LE * LR, F)),
        "b2l": a["L1_ffn_B2"].transpose(0, 2, 1).reshape(LE * LR, D),
    }
    for n in "qkvo":
        d["w_x" + n] = cols_layout(a["L0_xattn_W" + n])
    return {k: np.ascontiguousarray(v) for k, v in d.items()}


def kernel(**inputs):
    import concourse.bacc as bacc
    from concourse.bass_utils import run_bass_kernel_spmd as run

    arrays = host_layout(inputs)
    nc = bacc.Bacc("TRN2", target_bir_lowering=False, num_devices=1)
    dr = {n: nc.dram_tensor(f"in_{n}_dram", a.shape, mybir.dt.from_np(a.dtype), kind="ExternalInput").ap()
          for n, a in arrays.items()}
    dr["out"] = nc.dram_tensor("out_dram", [NSEQ, S, D], F32, kind="ExternalOutput").ap()
    program(nc, dr)
    r = run(nc, [{f"in_{n}_dram": a for n, a in arrays.items()}], core_ids=[0])
    return r.results[0]["out_dram"]
```

```python
from contextlib import ExitStack

import numpy as np

import concourse.bass as bass
from concourse import mybir

ALU = mybir.AluOpType
ACT = mybir.ActivationFunctionType
AX = mybir.AxisListType
F32 = mybir.dt.float32
U32 = mybir.dt.uint32
I32 = mybir.dt.int32
BF16 = mybir.dt.bfloat16

P = 128
NSEQ, S, D = 8, 256, 512
T = NSEQ * S
NT = S // P
KC = D // P
EPS = 1e-5

HEADS = 16
HD = D // HEADS
HPC = P // HD
WINDOW = 64
QK_SCALE = float(np.float32(HD ** -0.5))
SCORE_CLIP = 50.0
ROOT_HD = float(np.float32(HD ** 0.5))
NEG = -1e30
BAND = S - P + WINDOW

E, M, TOPK = 64, 352, 6
NG, TG = 8, 3
EPG = E // NG
CAP = 192
MS = 704
MS_CHUNKS = [(m, min(P, MS - m)) for m in range(0, MS, P)]
M_CHUNKS = [(m, min(P, M - m)) for m in range(0, M, P)]
C_TILES = [(0, P), (P, CAP - P)]
DROPPED = 1 << 15

TURN_SEMS = """
stats_ready rstd_ready normed_ready rowsT_psum colsT_ready dve_link pool_link
qk_proj qk_raw_ready rope_cos_ready rot_psum rope_ready v_psum v_ready scores_psum masked_ready
negmax_ready probs_ready probsT_psum probsT_ready pv_psum attn_ready
out_psum resid_ready xk_psum xk_ready xv_psum xv_ready xq_psum xq_ready xs_psum clipped_ready
xprobs_ready xpv_psum xattn_ready delta_psum router_psum negmax_router exp_router
gate_psum tanh_ready act_sh_ready down_psum shared_ready route_ready
xbc_psum xbc_raw_ready conv_ready convtanh_ready xbc_ready z_psum ztanh_ready zs_ready dt_psum
dtabs_ready dtexp_ready dtone_ready dtln_ready dA_ready tri_ready bc_psum decay_psum decay_ready
decaymask_ready w_ready xrows_psum xrows_ready xdt_ready y_psum gated_ready sumsq_ready gated_norm
s_psum smax_ready snegmax_ready sexp_ready snormed_ready sT_psum sT_act sT_dve ret_psum
sel_ready pos_psum slot_ready moe_psum moe_negmax moe_exp mask_rows maskT_psum maskT_ready t1_psum m0_ready base_psum gelu0_ready
base1_psum gelu1_ready ca_ready mix_ready t2_psum t2m_ready y_out_psum x_out_ready
yk_used clip_bounds
""".split()


class Sync:

    def __init__(self, nc, ctx):
        self.nc, self.ctx, self.by_name, self.counts, self.turns = nc, ctx, {}, {}, 0
        for name in TURN_SEMS:
            self[name]
        nums = [self.by_name[n].num for n in TURN_SEMS]
        assert nums == list(range(nums[0], nums[0] + len(nums)))
        self.turn_range = range(nums[0], nums[0] + len(nums))

    def __getitem__(self, name):
        if name not in self.by_name:
            self.by_name[name] = self.ctx.enter_context(self.nc.semaphore(name))
        return self.by_name[name]

    def link(self, eng, name, ins):
        self.counts[name] = self.counts.get(name, 0) + 1
        ins.then_inc(self[name], 1)
        eng.wait_ge(self[name], self.counts[name])

    def end_turn(self, eng, i, base, chain=None):
        if chain is not None:
            self.counts[chain] = 0
        eng.drain().then_inc(self["turn_done"], 1)
        eng.wait_ge(self["turn_go"], i + (base + 1))

    def clear_turn(self, sp, i, base):
        self.alone(sp)
        sp.wait_ge(self["turn_done"], (i + (base + 1)) * 4)
        self.alone(sp)
        sp.sem_clear(self.turn_range)
        sp.sem_inc(self["turn_go"], 1)
        sp.wait_ge(self["turn_go"], i + (base + 1))
        self.alone(sp)

    def alone(self, eng):
        eng.sem_inc(self["passed"], 1)


def heads_view(ap, n):
    return ap.rearrange("p (h d) -> p h d", h=n)


def layernorm_stats(dve, sy, src, st, mv):
    for j in range(NT):
        ins = dve.bn_stats(st[:, j, :], src[:, j, :])
    sy.link(dve, "dve_link", ins)
    for j in range(NT):
        ins = dve.bn_aggr(mv[:, j, :], st[:, j, :])
    ins.then_inc(sy["stats_ready"], 1)


def layernorm_apply(dve, sy, k, src, dst, mv, rstd):
    dve.wait_ge(sy["rstd_ready"], k + 1)
    for j in range(NT):
        dve.tensor_scalar(dst[:, j, :], src[:, j, :], mv[:, j, 0:1], rstd[:, j:j + 1],
                          ALU.subtract, ALU.mult).then_inc(sy["normed_ready"], 1)


def layernorm_rows(dve, sy, k, src, dst, st, mv, rstd):
    layernorm_stats(dve, sy, src, st, mv)
    layernorm_apply(dve, sy, k, src, dst, mv, rstd)


def rstd_pool(pool, sy, k, mv, ve, rstd, minus_half):
    pool.wait_ge(sy["stats_ready"], k + 1)
    sy.link(pool, "pool_link", pool.tensor_scalar(ve[:, :], mv[:, :, 1], EPS, None, ALU.add))
    pool.tensor_tensor(rstd[:, :], ve[:, :], minus_half[:, 0:NT], ALU.pow).then_inc(sy["rstd_ready"], 1)


def transposes_pe(pe, ident, src, bank, j):
    for kc in range(KC):
        ins = pe.transpose(bank[:, kc * P:(kc + 1) * P], src[:, j, kc * P:(kc + 1) * P], ident)
    return ins


def project_pe(pe, out, lhs_of, rhs_of, chunks=KC):
    for kc in range(chunks):
        ins = pe.matmul(out, lhs_of(kc), rhs_of(kc), start=(kc == 0), stop=(kc == chunks - 1))
    return ins


def phase1(nc, sy, const, dr, base, nseq=NSEQ):
    with ExitStack() as ctx:
        def sb(name, shape, dt=F32):
            return ctx.enter_context(nc.sbuf_tensor(name, shape, dt))

        w_qkv = sb("w_qkv", [P, KC, 3 * D])
        w_out = sb("w_out", [P, KC, D])
        w_x = {n: sb(f"w_x{n}", [P, KC, D]) for n in "qkvo"}
        w_gate = sb("w_gate", [P, KC, E])
        w_sg = sb("w_sg", [P, KC, MS])
        w_su = sb("w_su", [P, KC, MS])
        w_sd = sb("w_sd", [P, len(MS_CHUNKS), D])
        cosT, sinT = sb("cosT", [P, S]), sb("sinT", [P, S])
        rot = sb("rot", [P, P])
        wmask = sb("wmask", [P, P + BAND])
        bq, bk = sb("bq", [P, KC]), sb("bk", [P, KC])
        rows_bc = sb("rows_bc", [P, 4, D])
        rs = sb("rs", [P, 1])
        mask_i = sb("mask_i", [P, NT], I32)
        hi = sb("hi", [P, NT])
        iota8, iota64 = const["iota"][:, 0:NG], const["iota"][:, 0:E]

        x = sb("x", [P, NT, D])
        xn = sb("xn", [P, NT, D])
        h = sb("h", [P, NT, D])
        hT = sb("hT", [P, KC, S])
        ctxT = sb("ctxT", [P, KC, S])
        qk_raw = sb("qk_raw", [P, 2 * KC, S])
        qk = sb("qk", [P, 2 * KC, S])
        hn = qk_raw[:, 0:KC, :].rearrange("p (t c) s -> p t (c s)", t=NT)
        cosq, sinq = sb("cosq", [P, 2, S]), sb("sinq", [P, 2, S])
        vaug = sb("vaug", [P, NT, HEADS, HD + 1])
        xvaug = sb("xvaug", [P, NT, HEADS, HD + 1])
        masked = sb("masked", [P, 2, P + BAND])
        probs = sb("probs", [P, 2, P + S])
        probsT = sb("probsT", [P, 2, P + S])
        smax, negmax = sb("smax", [P, HEADS, NT]), sb("negmax", [P, HEADS, NT])
        clipped, xprobs = sb("clipped", [P, 2, NT, S]), sb("xprobs", [P, 2, NT, S])
        o = sb("o", [P, NT, D])
        oT = hT
        rec, sec = sb("rec", [P, NT, 8]), sb("sec", [P, NT, 8])
        st, mv = sb("st", [P, NT, 6]), sb("mv", [P, NT, 2])
        ve, rstd = sb("ve", [P, NT]), sb("rstd", [P, NT])
        ex = sb("ex", [P, NT, E])
        sc, tsc = sb("sc", [P, NT, E]), sb("tsc", [P, NT, E])
        rm, rsum, rrec = sb("rm", [P, NT]), sb("rsum", [P, NT]), sb("rrec", [P, NT])
        gs, gtop, gmask = sb("gs", [P, NT, NG]), sb("gtop", [P, NT, 8]), sb("gmask", [P, NT, NG])
        gidx, gidxf = sb("gidx", [P, NT, 8], U32), sb("gidxf", [P, NT, 8])
        etop = sb("etop", [P, NT, 8])
        eidx, eidxf = sb("eidx", [P, NT, 8], U32), sb("eidxf", [P, NT, 8])
        sel, pos, junk = sb("sel", [P, NT, E]), sb("pos", [P, NT, E]), sb("junk", [P, E])
        taken = sb("taken", [P, NT, E])
        carry = sb("carry", [P, E])
        last = const["last"]
        slot_v, over = sb("slot_v", [P, NT, 8]), sb("over", [P, NT, 8])
        slot_w, slot_r = sb("slot_w", [P, NT, 8], I32), sb("slot_r", [P, NT, 8], I32)
        tok_f, tok_i = sb("tok_f", [P, NT]), sb("tok_i", [P, NT], I32)
        ebase = sb("ebase", [P, E])
        zeros = sb("zeros", [P, E * CAP // P], I32)
        th = sb("th", [P, 2, S])
        shT = sb("shT", [P, len(MS_CHUNKS), S])

        ident, bank = const["ident"], const["bank"]

        def pv(j, hh):
            b = bank(4 + 2 * (hh // 8) + j)
            return b[:, (hh % 8) * (HD + 1):(hh % 8 + 1) * (HD + 1)]

        def pv_bank(half, j):
            return bank(4 + 2 * half + j)[:, 0:8 * (HD + 1)].rearrange("p (h d) -> p h d", h=8)

        def gate_bank(n):
            return bank((2, 3, 0, 1)[n % 4])

        W1A, W1B = 16 * (KC + 5), 16 * 13
        block = ctx.enter_context(nc.Block())

        @block.sync
        def _(sp):
            def load_x(i):
                sp.dma_start(xn[:], dr["x"][bass.ds(i, 1)].rearrange("o p t d -> (o p) t d")
                             ).then_inc(sy["x_in"], 16)

            def load_ctx(i):
                sp.dma_start(ctxT[:], dr["ctxT"][bass.ds(i, 1)].rearrange("o p t d -> (o p) t d")
                             ).then_inc(sy["ctx_in"], 16)
                sp.dma_start(mask_i[:], dr["mask"][bass.ds(i, 1)].rearrange("o p t -> (o p) t")
                             ).then_inc(sy["mask_in"], 16)

            load_x(0)
            for kc in range(KC):
                sp.dma_start(w_qkv[:, kc, :], dr["w_qkv"][:, kc, :]).then_inc(sy["w1_in"], 16)
            for dst, src in ((cosT, "cosT"), (sinT, "sinT"), (rot, "rot"), (wmask, "wmask"), (rs, "rs")):
                sp.dma_start(dst[:], dr[src]).then_inc(sy["w1_in"], 16)
            load_ctx(0)
            for dst, src in ((bq, "bq"), (bk, "bk"), (rows_bc, "rows_bc"), (w_x["k"], "w_xk"), (w_x["v"], "w_xv"),
                             (w_out, "w_out"), (w_x["q"], "w_xq"), (w_x["o"], "w_xo"), (w_gate, "w_gate"),
                             (w_sg, "w_sg"), (w_su, "w_su")):
                sp.dma_start(dst[:], dr[src]).then_inc(sy["w1b_in"], 16)
            n_full = MS // P
            sp.dma_start(w_sd[:, 0:n_full, :], dr["w_sd"][0:n_full * P].rearrange("(c p) n -> p c n", p=P)
                         ).then_inc(sy["w1b_in"], 16)
            sp.dma_start(w_sd[0:MS - n_full * P, n_full, :], dr["w_sd"][n_full * P:MS]).then_inc(sy["w1b_in"], 16)
            sp.sem_inc(sy["mid_out"], 1)
            sp.sem_inc(sy["rows_out"], 1)
            sy.clear_turn(sp, 0, base)

            def turn(i, more):
                if more:
                    sp.wait_ge(sy["resid_ready"], 1)
                    load_x(i + 1)
                    sp.wait_ge(sy["xv_psum"], NT)
                    sp.wait_ge(sy["clip_bounds"], 1)
                    load_ctx(i + 1)
                sp.wait_ge(sy["normed_ready"], 2 * NT)
                sp.dma_start(dr["normed_rows"][bass.ds(i, 1)].rearrange("o (t p) d -> (o p) t d", p=P),
                             h[:]).then_inc(sy["rows_out"], 16)
                sp.wait_ge(sy["route_ready"], 2)
                sp.dma_start(dr["route_w"][bass.ds(i, 1)].rearrange("o p t k -> (o p) t k"), etop[:]
                             ).then_inc(sy["rows_out"], 16)
                sp.wait_ge(sy["slot_ready"], 2)
                sp.dma_start(dr["slots"][bass.ds(i, 1)].rearrange("o p t k -> (o p) t k"), slot_r[:]
                             ).then_inc(sy["rows_out"], 16)
                sp.wait_ge(sy["shared_ready"], 2)
                sp.dma_start(dr["mid"][bass.ds(i, 1)].rearrange("o p t d -> (o p) t d"), o[:]
                             ).then_inc(sy["mid_out"], 16)
                sy.clear_turn(sp, i, base + 1)

            with sp.Fori(0, nseq - 1) as i:
                turn(i, True)
            turn(nseq - 1, False)
            sp.wait_ge(sy["rows_out"], nseq * 48 + 1)
            sp.wait_ge(sy["mid_out"], nseq * 16 + 1)

        @block.gpsimd
        def _(pool):
            pool.memset(vaug[:, :, :, HD:HD + 1], 1.0)
            pool.memset(xvaug[:, :, :, HD:HD + 1], 1.0)
            pool.memset(probs[:, :, P:P + WINDOW], 0.0).then_inc(sy["init1"], 1)
            pool.iota(ebase[:], pattern=[[CAP, E]], base=0, channel_multiplier=0,
                      allow_small_or_imprecise_dtypes=True)
            pool.iota(tok_f[:], pattern=[[P, NT]], base=0, channel_multiplier=1,
                      allow_small_or_imprecise_dtypes=True)
            pool.memset(carry[:], 0.0)
            pool.memset(slot_v[:], 0.0)
            pool.memset(last, 0.0).then_inc(sy["init1"], 1)
            pool.memset(zeros[:], 0).then_inc(sy["zeros_set"], 1)
            pool.wait_ge(sy["zeros_set"], 1)
            pool.dma_start(dr["slot_token"].rearrange("(p c) o -> p (c o)", p=P), zeros[:]
                           ).then_inc(sy["zeros_out"], 16)
            pool.wait_ge(sy["zeros_out"], 16)
            rstd_pool(pool, sy, 0, mv, ve, rstd, const["minus_half"])
            pool.wait_ge(sy["w1_in"], W1A)
            sy.end_turn(pool, 0, base, "pool_link")

            def turn(i, more):
                for c in range(2 * KC):
                    pool.wait_ge(sy["qk_raw_ready"], c + 1)
                    if c >= 2:
                        pool.wait_ge(sy["rope_ready"], c - 1)
                    pool.tensor_tensor(cosq[:, c % 2, :], qk_raw[:, c, :], cosT[:], ALU.mult
                                       ).then_inc(sy["rope_cos_ready"], 1)
                for hh in range(HEADS):
                    pool.wait_ge(sy["masked_ready"], 2 * hh + 2)
                    pool.tensor_scalar(negmax[:, hh, :], smax[:, hh, :], -QK_SCALE, None, ALU.mult
                                       ).then_inc(sy["negmax_ready"], 1)
                pool.wait_ge(sy["mask_in"], (i + 1) * 16)
                sy.alone(pool)
                sy.link(pool, "pool_link", pool.tensor_copy(hi[:], mask_i[:]))
                sy.link(pool, "pool_link", pool.tensor_scalar(hi[:], hi[:], 0.5, None, ALU.is_gt))
                pool.tensor_scalar(hi[:], hi[:], 2 * SCORE_CLIP * ROOT_HD, -SCORE_CLIP * ROOT_HD,
                                   ALU.mult, ALU.add).then_inc(sy["clip_bounds"], 1)
                for k in (0, 1, 2, 3) if more else (0, 1, 2):
                    rstd_pool(pool, sy, k, mv, ve, rstd, const["minus_half"])
                for j in range(NT):
                    pool.wait_ge(sy["slot_ready"], j + 1)
                    for k in range(TOPK):
                        pool.indirect_dma_start(
                            out=dr["slot_token"], out_offset=bass.IndirectOffsetOnAxis(ap=slot_w[:, j, k:k + 1], axis=0),
                            in_=tok_i[:, j:j + 1], in_offset=None, bounds_check=E * CAP - 1, oob_is_err=False
                        ).then_inc(sy["scattered"], 16)
                pool.wait_ge(sy["scattered"], (i + 1) * (16 * NT * TOPK))
                sy.alone(pool)
                sy.end_turn(pool, i, base + 1, "pool_link")

            with pool.Fori(0, nseq - 1) as i:
                turn(i, True)
            turn(nseq - 1, False)

        @block.scalar
        def _(act):
            def cols_copy(k):
                for j in range(NT):
                    act.wait_ge(sy["rowsT_psum"], NT * k + j + 1)
                    act.activation(hT[:, :, j * P:(j + 1) * P],
                                   bank(j)[:, :].rearrange("p (c t) -> p c t", c=KC), ACT.Copy
                                   ).then_inc(sy["colsT_ready"], 1)

            cols_copy(0)
            act.wait_ge(sy["init1"], 2)
            sy.end_turn(act, 0, base)

            def turn(i, more):
                for c in range(2 * KC):
                    act.wait_ge(sy["qk_proj"], c + 1)
                    act.activation(qk_raw[:, c, :], bank(2 + c % 2)[:, 0:S], ACT.Copy
                                   ).then_inc(sy["qk_raw_ready"], 1)
                for j in range(NT):
                    act.wait_ge(sy["v_psum"], j + 1)
                    act.activation(vaug[:, j, :, 0:HD], heads_view(bank(6 + j)[:, :], HEADS), ACT.Copy
                                   ).then_inc(sy["v_ready"], 1)
                for hh in range(HEADS):
                    act.wait_ge(sy["negmax_ready"], hh + 1)
                    if hh >= 2:
                        act.wait_ge(sy["probsT_psum"], hh - 1)
                    act.activation(probs[:, hh % 2, 0:P], masked[:, hh % 2, 0:P], ACT.Exp,
                                   bias=negmax[:, hh, 0:1], scale=QK_SCALE)
                    act.activation(probs[:, hh % 2, P + WINDOW:P + S], masked[:, hh % 2, P:P + BAND], ACT.Exp,
                                   bias=negmax[:, hh, 1:2], scale=QK_SCALE).then_inc(sy["probs_ready"], 1)
                act.wait_ge(sy["w1b_in"], W1B)
                for c in range(KC):
                    act.wait_ge(sy["xk_psum"], c + 1)
                    act.activation(qk[:, KC + c, :], bank(c % 2)[:, 0:S], ACT.Identity, bias=bk[:, c:c + 1]
                                   ).then_inc(sy["xk_ready"], 1)
                cols_copy(0)
                cols_copy(1)
                for c in range(KC):
                    act.wait_ge(sy["xq_psum"], c + 1)
                    act.activation(qk[:, c, :], bank(2 + c % 2)[:, 0:S], ACT.Identity, bias=bq[:, c:c + 1]
                                   ).then_inc(sy["xq_ready"], 1)
                for hh in range(HEADS):
                    act.wait_ge(sy["clipped_ready"], 2 * hh + 2)
                    if hh >= 2:
                        act.wait_ge(sy["xpv_psum"], hh - 1)
                    act.activation(xprobs[:, hh % 2], clipped[:, hh % 2], ACT.Exp, scale=1.0 / ROOT_HD
                                   ).then_inc(sy["xprobs_ready"], 1)
                cols_copy(2)
                cols_copy(3)
                for j in range(NT):
                    act.wait_ge(sy["negmax_router"], j + 1)
                    act.activation(ex[:, j, :], bank(6 + j)[:, 0:E], ACT.Exp, bias=rm[:, j:j + 1],
                                   accum_out=rsum[:, j:j + 1]).then_inc(sy["exp_router"], 1)
                for n, (m, w) in enumerate(MS_CHUNKS):
                    act.wait_ge(sy["gate_psum"], n + 1)
                    if n >= 2:
                        act.wait_ge(sy["act_sh_ready"], n - 1)
                    act.activation(th[0:w, n % 2, :], gate_bank(n)[0:w, 0:S], ACT.Tanh, scale=0.5
                                   ).then_inc(sy["tanh_ready"], 1)
                if more:
                    cols_copy(4)
                sy.end_turn(act, i, base + 1)

            with act.Fori(0, nseq - 1) as i:
                turn(i, True)
            turn(nseq - 1, False)

        @block.tensor
        def _(pe):
            def rows_to_cols(src, ready, at):
                for j in range(NT):
                    pe.wait_ge(ready, at + j + 1)
                    transposes_pe(pe, ident, src, bank(j), j).then_inc(sy["rowsT_psum"], 1)

            rows_to_cols(hn, sy["normed_ready"], 0)
            pe.wait_ge(sy["w1_in"], W1A)
            pe.wait_ge(sy["init1"], 2)
            sy.end_turn(pe, 0, base)

            def turn(i, more):
                for c in range(2 * KC + 1):
                    if c < 2 * KC:
                        if c >= 2:
                            pe.wait_ge(sy["qk_raw_ready"], c - 1)
                        project_pe(pe, bank(2 + c % 2)[:, 0:S], lambda kc: w_qkv[:, kc, c * P:(c + 1) * P],
                                   lambda kc: hT[:, kc, :]).then_inc(sy["qk_proj"], 1)
                    if c >= 1:
                        pe.wait_ge(sy["qk_raw_ready"], c)
                        if c >= 3:
                            pe.wait_ge(sy["rope_ready"], c - 2)
                        pe.matmul(bank(4 + (c - 1) % 2)[:, 0:S], rot[:], qk_raw[:, c - 1, :], start=True,
                                  stop=True).then_inc(sy["rot_psum"], 1)
                for j in range(NT):
                    project_pe(pe, bank(6 + j)[:, :], lambda kc: hT[:, kc, j * P:(j + 1) * P],
                               lambda kc: w_qkv[:, kc, 2 * D:3 * D]).then_inc(sy["v_psum"], 1)
                pe.wait_ge(sy["rope_ready"], 2 * KC)
                pe.wait_ge(sy["v_ready"], NT)
                for s in range(HEADS + 2):
                    if s < HEADS:
                        c, r = s // HPC, (s % HPC) * HD
                        if s >= 2:
                            pe.wait_ge(sy["masked_ready"], 2 * (s - 1))
                        q, k, b = qk[r:r + HD, c, :], qk[r:r + HD, KC + c, :], bank(s % 2)
                        pe.matmul(b[:, 0:P], q[:, 0:P], k[:, 0:P], start=True, stop=True)
                        pe.matmul(b[:, P:P + BAND], q[:, P:S], k[:, WINDOW:S], start=True, stop=True
                                  ).then_inc(sy["scores_psum"], 1)
                    if 1 <= s <= HEADS:
                        hh = s - 1
                        pe.wait_ge(sy["probs_ready"], hh + 1)
                        if hh >= 2:
                            pe.wait_ge(sy["probsT_ready"], hh - 1)
                        for b3 in range(3):
                            ins = pe.transpose(bank(2 + hh % 2)[:, b3 * P:(b3 + 1) * P],
                                               probs[:, hh % 2, b3 * P:(b3 + 1) * P], ident)
                        ins.then_inc(sy["probsT_psum"], 1)
                    if s >= 2:
                        hh = s - 2
                        pe.wait_ge(sy["probsT_ready"], hh + 1)
                        pt = probsT[:, hh % 2]
                        pe.matmul(pv(0, hh), pt[:, 0:P], vaug[:, 0, hh, :], start=True, stop=True)
                        pe.matmul(pv(1, hh), pt[:, P:2 * P], vaug[:, 0, hh, :], start=True, stop=False)
                        pe.matmul(pv(1, hh), pt[:, 2 * P:3 * P], vaug[:, 1, hh, :], start=False, stop=True
                                  ).then_inc(sy["pv_psum"], 1)
                pe.wait_ge(sy["ctx_in"], (i + 1) * 16)
                pe.wait_ge(sy["w1b_in"], W1B)
                for c in range(KC):
                    if c >= 2:
                        pe.wait_ge(sy["xk_ready"], c - 1)
                    else:
                        pe.wait_ge(sy["masked_ready"], 2 * HEADS)
                    project_pe(pe, bank(c % 2)[:, 0:S], lambda kc: w_x["k"][:, kc, c * P:(c + 1) * P],
                               lambda kc: ctxT[:, kc, :]).then_inc(sy["xk_psum"], 1)
                for j in range(NT):
                    pe.wait_ge(sy["probsT_ready"], HEADS)
                    project_pe(pe, bank(2 + j)[:, :], lambda kc: ctxT[:, kc, j * P:(j + 1) * P],
                               lambda kc: w_x["v"][:, kc, :]).then_inc(sy["xv_psum"], 1)
                pe.wait_ge(sy["xk_ready"], KC)
                rows_to_cols(o, sy["attn_ready"], 0)
                pe.wait_ge(sy["colsT_ready"], NT)
                for j in range(NT):
                    project_pe(pe, bank(4 + j)[:, :], lambda kc: oT[:, kc, j * P:(j + 1) * P],
                               lambda kc: w_out[:, kc, :]).then_inc(sy["out_psum"], 1)
                rows_to_cols(h, sy["normed_ready"], 0)
                pe.wait_ge(sy["colsT_ready"], 2 * NT)
                for c in range(KC):
                    if c >= 2:
                        pe.wait_ge(sy["xq_ready"], c - 1)
                    else:
                        pe.wait_ge(sy["xv_ready"], NT)
                    project_pe(pe, bank(2 + c % 2)[:, 0:S], lambda kc: w_x["q"][:, kc, c * P:(c + 1) * P],
                               lambda kc: hT[:, kc, :]).then_inc(sy["xq_psum"], 1)
                pe.wait_ge(sy["xq_ready"], KC)
                for s in range(HEADS + 2):
                    if s < HEADS:
                        c, r, b = s // HPC, (s % HPC) * HD, bank(s % 4)
                        if s >= 4:
                            pe.wait_ge(sy["clipped_ready"], 2 * (s - 3))
                        for kt in range(NT):
                            ins = pe.matmul(b[:, kt * S:(kt + 1) * S], qk[r:r + HD, KC + c, kt * P:(kt + 1) * P],
                                            qk[r:r + HD, c, :], start=True, stop=True)
                        ins.then_inc(sy["xs_psum"], 1)
                    if s >= 2:
                        hh = s - 2
                        pe.wait_ge(sy["xprobs_ready"], hh + 1)
                        for j in range(NT):
                            for kt in range(NT):
                                ins = pe.matmul(pv(j, hh), xprobs[:, hh % 2, kt, j * P:(j + 1) * P],
                                                xvaug[:, kt, hh, :], start=(kt == 0), stop=(kt == NT - 1))
                        ins.then_inc(sy["xpv_psum"], 1)
                rows_to_cols(o, sy["xattn_ready"], 0)
                pe.wait_ge(sy["colsT_ready"], 3 * NT)
                for j in range(NT):
                    project_pe(pe, bank(2 + j)[:, :], lambda kc: oT[:, kc, j * P:(j + 1) * P],
                               lambda kc: w_x["o"][:, kc, :]).then_inc(sy["delta_psum"], 1)
                rows_to_cols(h, sy["normed_ready"], NT)
                pe.wait_ge(sy["colsT_ready"], 4 * NT)
                for j in range(NT):
                    project_pe(pe, bank(6 + j)[:, 0:E], lambda kc: hT[:, kc, j * P:(j + 1) * P],
                               lambda kc: w_gate[:, kc, :]).then_inc(sy["router_psum"], 1)
                def counts(j):
                    pe.wait_ge(sy["sel_ready"], j + 1)
                    pe.matmul(bank(6 + j)[:, E:2 * E], const["tri_lt"], sel[:, j, :], start=True, stop=True)
                    pe.matmul(bank(6 + j)[:, 2 * E:3 * E], const["ones"], sel[:, j, :], start=True, stop=True
                              ).then_inc(sy["pos_psum"], 1)

                for n, (m, w) in enumerate(MS_CHUNKS):
                    if n >= 4:
                        pe.wait_ge(sy["act_sh_ready"], n - 3)
                    b = gate_bank(n)
                    project_pe(pe, b[0:w, 0:S], lambda kc: w_sg[:, kc, m:m + w], lambda kc: hT[:, kc, :])
                    project_pe(pe, b[0:w, S:2 * S], lambda kc: w_su[:, kc, m:m + w], lambda kc: hT[:, kc, :]
                               ).then_inc(sy["gate_psum"], 1)
                    if n == 3:
                        counts(0)
                counts(1)
                if more:
                    pe.wait_ge(sy["act_sh_ready"], 4)
                    rows_to_cols(hn, sy["normed_ready"], 2 * NT)
                for j in range(NT):
                    for n, (m, w) in enumerate(MS_CHUNKS):
                        if j == 0:
                            pe.wait_ge(sy["act_sh_ready"], n + 1)
                        ins = pe.matmul(bank(4 + j)[:, :], shT[0:w, n, j * P:(j + 1) * P], w_sd[0:w, n, :],
                                        start=(n == 0), stop=(n == len(MS_CHUNKS) - 1))
                    ins.then_inc(sy["down_psum"], 1)
                sy.end_turn(pe, i, base + 1)

            with pe.Fori(0, nseq - 1) as i:
                turn(i, True)
            turn(nseq - 1, False)

        @block.vector
        def _(dve):
            def ln(ins):
                sy.link(dve, "dve_link", ins)

            dve.wait_ge(sy["x_in"], 16)
            layernorm_rows(dve, sy, 0, xn, hn, st, mv, rstd)
            dve.wait_ge(sy["w1_in"], W1A)
            dve.wait_ge(sy["init1"], 2)
            ln(dve.tensor_scalar(rs[:], rs[:], 0.0, 0.3, ALU.max, ALU.min))
            sy.end_turn(dve, 0, base, "dve_link")

            def turn(i, more):
                for c in range(2 * KC):
                    dve.wait_ge(sy["rot_psum"], c + 1)
                    sy.link(dve, "dve_link", dve.tensor_tensor(sinq[:, c % 2, :], bank(4 + c % 2)[:, 0:S],
                                                               sinT[:], ALU.mult))
                    dve.wait_ge(sy["rope_cos_ready"], c + 1)
                    dve.tensor_tensor(qk[:, c, :], cosq[:, c % 2, :], sinq[:, c % 2, :], ALU.add
                                      ).then_inc(sy["rope_ready"], 1)
                for s in range(HEADS + 1):
                    if s < HEADS:
                        dve.wait_ge(sy["scores_psum"], s + 1)
                        if s >= 2:
                            dve.wait_ge(sy["probs_ready"], s - 1)
                        for j, (a, w) in enumerate(((0, P), (P, BAND))):
                            dve.tensor_tensor_reduce(
                                out=masked[:, s % 2, a:a + w], in0=bank(s % 2)[:, a:a + w], in1=wmask[:, a:a + w],
                                scale=1.0, scalar=3 * NEG, op0=ALU.add, op1=ALU.max,
                                accum_out=smax[:, s, j:j + 1]).then_inc(sy["masked_ready"], 1)
                    if s >= 1:
                        hh = s - 1
                        dve.wait_ge(sy["probsT_psum"], hh + 1)
                        if hh >= 2:
                            dve.wait_ge(sy["pv_psum"], hh - 1)
                        dve.tensor_copy(probsT[:, hh % 2], bank(2 + hh % 2)[:, 0:P + S]
                                        ).then_inc(sy["probsT_ready"], 1)
                dve.wait_ge(sy["mid_out"], i * 16 + 1)
                dve.wait_ge(sy["rows_out"], i * 48 + 1)
                sy.alone(dve)
                for half in range(2):
                    dve.wait_ge(sy["pv_psum"], 8 * half + 8)
                    for j in range(NT):
                        b = pv_bank(half, j)
                        sy.link(dve, "dve_link", dve.reciprocal(rec[:, j, :], b[:, :, HD]))
                        ins = dve.tensor_tensor(heads_view(o[:, j, half * 256:(half + 1) * 256], 8), b[:, :, 0:HD],
                                                rec[:, j, :].unsqueeze(2).broadcast_to([P, 8, HD]), ALU.mult)
                        if half == 1:
                            ins.then_inc(sy["attn_ready"], 1)
                        else:
                            sy.link(dve, "dve_link", ins)
                dve.wait_ge(sy["w1b_in"], W1B)
                for j in range(NT):
                    dve.wait_ge(sy["xv_psum"], j + 1)
                    dve.tensor_tensor(xvaug[:, j, :, 0:HD], heads_view(bank(2 + j)[:, :], HEADS),
                                      heads_view(rows_bc[:, 0, :], HEADS), ALU.add).then_inc(sy["xv_ready"], 1)
                for j in range(NT):
                    dve.wait_ge(sy["out_psum"], j + 1)
                    ins = dve.tensor_tensor(x[:, j, :], xn[:, j, :], bank(4 + j)[:, :], ALU.add)
                ins.then_inc(sy["resid_ready"], 1)
                dve.wait_ge(sy["resid_ready"], 1)
                layernorm_rows(dve, sy, 0, x, h, st, mv, rstd)
                dve.wait_ge(sy["clip_bounds"], 1)
                for hh in range(HEADS):
                    dve.wait_ge(sy["xs_psum"], hh + 1)
                    if hh >= 2:
                        dve.wait_ge(sy["xprobs_ready"], hh - 1)
                    for kt in range(NT):
                        dve.tensor_scalar(clipped[:, hh % 2, kt, :], bank(hh % 4)[:, kt * S:(kt + 1) * S],
                                          hi[:, kt:kt + 1], -SCORE_CLIP * ROOT_HD, ALU.min, ALU.max
                                          ).then_inc(sy["clipped_ready"], 1)
                for half in range(2):
                    dve.wait_ge(sy["xpv_psum"], 8 * half + 8)
                    for j in range(NT):
                        b = pv_bank(half, j)
                        sy.link(dve, "dve_link", dve.reciprocal(rec[:, j, :], b[:, :, HD]))
                        sy.link(dve, "dve_link", dve.tensor_tensor(sec[:, j, :], b[:, :, HD], rec[:, j, :], ALU.mult))
                        sy.link(dve, "dve_link", dve.tensor_scalar(sec[:, j, :], sec[:, j, :], 1e-8, None, ALU.add))
                        sy.link(dve, "dve_link", dve.reciprocal(sec[:, j, :], sec[:, j, :]))
                        sy.link(dve, "dve_link", dve.tensor_tensor(rec[:, j, :], rec[:, j, :], sec[:, j, :], ALU.mult))
                        ins = dve.tensor_tensor(heads_view(o[:, j, half * 256:(half + 1) * 256], 8), b[:, :, 0:HD],
                                                rec[:, j, :].unsqueeze(2).broadcast_to([P, 8, HD]), ALU.mult)
                        if half == 1:
                            ins.then_inc(sy["xattn_ready"], 1)
                        else:
                            sy.link(dve, "dve_link", ins)
                for j in range(NT):
                    dve.wait_ge(sy["delta_psum"], j + 1)
                    sy.link(dve, "dve_link", dve.tensor_tensor(h[:, j, :], bank(2 + j)[:, :], rows_bc[:, 1, :], ALU.add))
                    sy.link(dve, "dve_link", dve.tensor_scalar(h[:, j, :], h[:, j, :], rs[:, 0:1], None, ALU.mult))
                for j in range(NT):
                    ins = dve.bn_stats(st[:, j, :], h[:, j, :])
                sy.link(dve, "dve_link", ins)
                for j in range(NT):
                    ins = dve.bn_aggr(mv[:, j, :], st[:, j, :])
                ins.then_inc(sy["stats_ready"], 1)
                dve.wait_ge(sy["rstd_ready"], 2)
                for j in range(NT):
                    sy.link(dve, "dve_link", dve.tensor_scalar(h[:, j, :], h[:, j, :], mv[:, j, 0:1], rstd[:, j:j + 1],
                                                               ALU.subtract, ALU.mult))
                    sy.link(dve, "dve_link", dve.tensor_tensor(h[:, j, :], h[:, j, :], rows_bc[:, 2, :], ALU.mult))
                    sy.link(dve, "dve_link", dve.tensor_tensor(h[:, j, :], h[:, j, :], rows_bc[:, 3, :], ALU.add))
                    sy.link(dve, "dve_link", dve.tensor_tensor(x[:, j, :], x[:, j, :], h[:, j, :], ALU.add))
                layernorm_rows(dve, sy, 2, x, h, st, mv, rstd)
                for j in range(NT):
                    dve.wait_ge(sy["router_psum"], j + 1)
                    sy.link(dve, "dve_link", dve.tensor_reduce(rm[:, j:j + 1], bank(6 + j)[:, 0:E], AX.X, ALU.max))
                    dve.tensor_scalar(rm[:, j:j + 1], rm[:, j:j + 1], -1.0, None, ALU.mult
                                      ).then_inc(sy["negmax_router"], 1)
                if more:
                    dve.wait_ge(sy["x_in"], (i + 2) * 16)
                    sy.alone(dve)
                    layernorm_rows(dve, sy, 3, xn, hn, st, mv, rstd)

                def shared(n):
                    m, w = MS_CHUNKS[n]
                    dve.wait_ge(sy["tanh_ready"], n + 1)
                    b = gate_bank(n)
                    ln(dve.scalar_tensor_tensor(out=shT[0:w, n, :], in0=th[0:w, n % 2, :], scalar=1.0,
                                                in1=b[0:w, 0:S], op0=ALU.add, op1=ALU.mult))
                    dve.tensor_tensor(shT[0:w, n, :], shT[0:w, n, :], b[0:w, S:2 * S], ALU.mult
                                      ).then_inc(sy["act_sh_ready"], 1)

                def route(j):
                    dve.wait_ge(sy["exp_router"], j + 1)
                    ln(dve.reciprocal(rrec[:, j:j + 1], rsum[:, j:j + 1]))
                    ln(dve.tensor_scalar(sc[:, j, :], ex[:, j, :], rrec[:, j:j + 1], None, ALU.mult))
                    ln(dve.tensor_reduce(gs[:, j, :], sc[:, j, :].rearrange("p (g e) -> p g e", g=NG), AX.X, ALU.max))
                    ln(dve.max(gtop[:, j, :], gs[:, j, :]))
                    ln(dve.max_index(gidx[:, j, :], gtop[:, j, :], gs[:, j, :]))
                    ln(dve.tensor_copy(gidxf[:, j, :], gidx[:, j, :]))
                    ln(dve.tensor_scalar(gmask[:, j, :], iota8, gidxf[:, j, 0:1], None, ALU.is_equal))
                    for g in range(1, TG):
                        ln(dve.scalar_tensor_tensor(out=gmask[:, j, :], in0=iota8, scalar=gidxf[:, j, g:g + 1],
                                                    in1=gmask[:, j, :], op0=ALU.is_equal, op1=ALU.add))
                    ln(dve.tensor_tensor(tsc[:, j, :].rearrange("p (g e) -> p g e", g=NG),
                                         sc[:, j, :].rearrange("p (g e) -> p g e", g=NG),
                                         gmask[:, j, :].unsqueeze(2).broadcast_to([P, NG, EPG]), ALU.mult))
                    ln(dve.max(etop[:, j, :], tsc[:, j, :]))
                    ln(dve.max_index(eidx[:, j, :], etop[:, j, :], tsc[:, j, :]))
                    dve.tensor_copy(eidxf[:, j, :], eidx[:, j, :]).then_inc(sy["route_ready"], 1)
                    dve.wait_ge(sy["route_ready"], j + 1)
                    ln(dve.tensor_scalar(sel[:, j, :], iota64, eidxf[:, j, 0:1], None, ALU.is_equal))
                    for k in range(1, TOPK):
                        ins = dve.scalar_tensor_tensor(out=sel[:, j, :], in0=iota64, scalar=eidxf[:, j, k:k + 1],
                                                       in1=sel[:, j, :], op0=ALU.is_equal, op1=ALU.add)
                        if k < TOPK - 1:
                            ln(ins)
                    ins.then_inc(sy["sel_ready"], 1)

                def slots(j):
                    dve.wait_ge(sy["pos_psum"], j + 1)
                    ln(dve.scalar_tensor_tensor(out=last, in0=sel[:, j, :], scalar=tok_f[:, j:j + 1], in1=last,
                                                op0=ALU.mult, op1=ALU.max))
                    ln(dve.tensor_tensor(pos[:, j, :], bank(6 + j)[:, E:2 * E], carry[:], ALU.add))
                    ln(dve.tensor_tensor(carry[:], carry[:], bank(6 + j)[:, 2 * E:3 * E], ALU.add))
                    ln(dve.tensor_scalar(taken[:, j, :], pos[:, j, :], float(CAP - 1), float(DROPPED), ALU.is_ge,
                                         ALU.mult))
                    ln(dve.scalar_tensor_tensor(out=pos[:, j, :], in0=pos[:, j, :], scalar=float(CAP - 1),
                                                in1=ebase[:], op0=ALU.min, op1=ALU.add))
                    ln(dve.tensor_tensor(pos[:, j, :], pos[:, j, :], taken[:, j, :], ALU.add))
                    for k in range(TOPK):
                        ln(dve.scalar_tensor_tensor(out=junk[:], in0=iota64, scalar=eidxf[:, j, k:k + 1],
                                                    in1=pos[:, j, :], op0=ALU.is_equal, op1=ALU.mult,
                                                    accum_out=slot_v[:, j, k:k + 1]))
                    ln(dve.tensor_scalar(over[:, j, :], slot_v[:, j, :], float(DROPPED), -float(DROPPED),
                                         ALU.is_ge, ALU.mult))
                    ln(dve.tensor_tensor(over[:, j, :], over[:, j, :], slot_v[:, j, :], ALU.add))
                    ln(dve.tensor_copy(slot_w[:, j, :], slot_v[:, j, :]))
                    ln(dve.tensor_copy(tok_i[:, j:j + 1], tok_f[:, j:j + 1]))
                    dve.tensor_copy(slot_r[:, j, :], over[:, j, :]).then_inc(sy["slot_ready"], 1)

                shared(0)
                shared(1)
                route(0)
                shared(2)
                route(1)
                shared(3)
                shared(4)
                slots(0)
                shared(5)
                slots(1)
                for j in range(NT):
                    dve.wait_ge(sy["down_psum"], j + 1)
                    dve.scalar_tensor_tensor(out=o[:, j, :], in0=bank(4 + j)[:, :], scalar=0.5, in1=x[:, j, :],
                                             op0=ALU.mult, op1=ALU.add).then_inc(sy["shared_ready"], 1)
                ln(dve.tensor_scalar(tok_f[:], tok_f[:], float(S), None, ALU.add))
                sy.end_turn(dve, i, base + 1, "dve_link")

            with dve.Fori(0, nseq - 1) as i:
                turn(i, True)
            turn(nseq - 1, False)


def phase2(nc, sy, const, dr):
    with ExitStack() as ctx:
        def sb(name, shape, dt=F32):
            return ctx.enter_context(nc.sbuf_tensor(name, shape, dt))

        wgu = [sb(f"wgu{b}", [P, 2, KC, M]) for b in range(2)]
        wd = [sb(f"wd{b}", [P, len(M_CHUNKS), D]) for b in range(2)]
        idx = [sb(f"idx{b}", [P, 2], I32) for b in range(2)]
        xg = [sb(f"xg{b}", [P, 2, D]) for b in range(2)]
        xT = [sb(f"xT{b}", [P, KC, CAP]) for b in range(2)]
        th = sb("eth", [P, len(M_CHUNKS), CAP])
        aT = [sb(f"aT{b}", [P, len(M_CHUNKS), CAP]) for b in range(2)]
        yo = [sb(f"yo{b}", [P, 2, D]) for b in range(2)]
        last_c, last_i = sb("last_c", [E, 1]), sb("last_i", [E, 1], I32)
        ident, bank = const["ident"], const["bank"]
        NM = len(M_CHUNKS)
        slot_token, expert_out = dr["slot_token"], dr["expert_out"]
        rows = dr["normed_rows"].rearrange("n s d -> (n s) d")

        block = ctx.enter_context(nc.Block())

        def pairs(eng, step):
            step(0, 0, 0, True)
            step(1, 0, 1, True)
            with eng.Fori(1, E // 2 - 1) as n:
                step(n * 2, n, 0, False)
                step(n * 2 + 1, n, 1, False)
            step(E - 2, E // 2 - 1, 0, False)
            step(E - 1, E // 2 - 1, 1, False)

        @block.sync
        def _(sp):
            sp.wait_ge(sy["last_ready"], 1)
            sp.dma_start(slot_token.rearrange("(e c) o -> e (c o)", c=CAP)[:, CAP - 1:CAP], last_i[:],
                         allow_slow_non_contiguous=True
                         ).then_inc(sy["last_out"], 16)
            sp.wait_ge(sy["last_out"], 16)

            def step(e, n, b, first):
                if not first:
                    sp.wait_ge(sy[f"xg_in{b}"], n * 32)
                sp.dma_start(idx[b][:, 0:1], slot_token[bass.ds(e * CAP, P)]).then_inc(sy[f"idx_in{b}"], 16)
                sp.dma_start(idx[b][0:CAP - P, 1:2], slot_token[bass.ds(e * CAP + P, CAP - P)]
                             ).then_inc(sy[f"idx_in{b}"], 16)
                if not first:
                    sp.wait_ge(sy["edown_psum"], e - 1)
                sp.dma_start(wgu[b][:], dr["w_gu"][bass.ds(e, 1)].rearrange("o p t c m -> (o p) t c m")
                             ).then_inc(sy[f"ew_in{b}"], 16)
                sp.dma_start(wd[b][:, 0:2, :], dr["w_d"][bass.ds(e, 1), 0:2 * P].rearrange(
                    "o (c p) n -> (o p) c n", p=P)).then_inc(sy[f"ew_in{b}"], 16)
                sp.dma_start(wd[b][0:M - 2 * P, 2, :], dr["w_d"][bass.ds(e, 1), 2 * P:M].rearrange(
                    "o p n -> (o p) n")).then_inc(sy[f"ew_in{b}"], 16)

            pairs(sp, step)

        @block.gpsimd
        def _(pool):
            def step(e, n, b, first):
                pool.wait_ge(sy[f"idx_in{b}"], n * 32 + 32)
                if not first:
                    pool.wait_ge(sy["exT_psum"], e - 1)
                sy.alone(pool)
                for t, (c0, w) in enumerate(C_TILES):
                    pool.indirect_dma_start(
                        out=xg[b][0:w, t, :], out_offset=None, in_=rows,
                        in_offset=bass.IndirectOffsetOnAxis(ap=idx[b][0:w, t:t + 1], axis=0)
                    ).then_inc(sy[f"xg_in{b}"], 16)

            pairs(pool, step)

        @block.scalar
        def _(act):
            def xT_copy(e, b):
                act.wait_ge(sy["exT_psum"], e + 1)
                for t in range(2):
                    ins = act.activation(xT[b][:, 2 * t:2 * t + 2, :],
                                         bank(t)[:, 0:2 * CAP].rearrange("p (c t) -> p c t", c=2), ACT.Copy)
                ins.then_inc(sy["exT_ready"], 1)

            def step(e, n, b, first):
                for m, (m0, w) in enumerate(M_CHUNKS):
                    act.wait_ge(sy["egu_psum"], e * NM + (m + 1))
                    if not (first and b == 0):
                        act.wait_ge(sy["eact_ready"], e * NM + (m + 1 - NM))
                    act.activation(th[0:w, m, :], bank(2 + m)[0:w, 0:CAP], ACT.Tanh, scale=0.5
                                   ).then_inc(sy["etanh_ready"], 1)
                if e is not E - 1:
                    xT_copy(e + 1, 1 - b)
                act.wait_ge(sy["edown_psum"], e + 1)
                if not first:
                    act.wait_ge(sy[f"eout{b}"], n * 32)
                for t, (c0, w) in enumerate(C_TILES):
                    ins = act.activation(yo[b][0:w, t, :], bank(5 + t)[0:w, :], ACT.Copy, scale=0.5)
                ins.then_inc(sy["eout_ready"], 1)
                act.wait_ge(sy["eout_ready"], e + 1)
                for t, (c0, w) in enumerate(C_TILES):
                    act.dma_start(expert_out[bass.ds(e * CAP + c0, w)], yo[b][0:w, t, :]).then_inc(sy[f"eout{b}"], 16)

            xT_copy(0, 0)
            pairs(act, step)
            act.wait_ge(sy["eout0"], 16 * E)
            act.wait_ge(sy["eout1"], 16 * E)

        @block.tensor
        def _(pe):
            pe.transpose(bank(7)[0:E, 0:P], const["last"], ident).then_inc(sy["last_psum"], 1)

            def turn_rows(e, b, n, first):
                pe.wait_ge(sy[f"xg_in{b}"], n * 32 + 32)
                if not first:
                    pe.wait_ge(sy["exT_ready"], e)
                for kc in range(KC):
                    for t, (c0, w) in enumerate(C_TILES):
                        at = (kc % 2) * CAP + c0
                        ins = pe.transpose(bank(kc // 2)[:, at:at + w], xg[b][0:w, t, kc * P:(kc + 1) * P],
                                           ident[0:w, 0:w])
                ins.then_inc(sy["exT_psum"], 1)

            def step(e, n, b, first):
                pe.wait_ge(sy[f"ew_in{b}"], n * 48 + 48)
                pe.wait_ge(sy["exT_ready"], e + 1)
                for m, (m0, w) in enumerate(M_CHUNKS):
                    if not (first and b == 0):
                        pe.wait_ge(sy["eact_ready"], e * NM + (m + 1 - NM))
                    for gu in range(2):
                        ins = project_pe(pe, bank(2 + m)[0:w, gu * CAP:(gu + 1) * CAP],
                                         lambda kc: wgu[b][:, gu, kc, m0:m0 + w], lambda kc: xT[b][:, kc, :])
                    ins.then_inc(sy["egu_psum"], 1)
                if e is not E - 1:
                    turn_rows(e + 1, 1 - b, n + b, False)
                for t, (c0, w) in enumerate(C_TILES):
                    if t == 0 and not (first and b == 0):
                        pe.wait_ge(sy["eout_ready"], e)
                    for m, (m0, mw) in enumerate(M_CHUNKS):
                        if t == 0:
                            pe.wait_ge(sy["eact_ready"], e * NM + (m + 1))
                        ins = pe.matmul(bank(5 + t)[0:w, :], aT[b][0:mw, m, c0:c0 + w], wd[b][0:mw, m, :],
                                        start=(m == 0), stop=(m == NM - 1))
                ins.then_inc(sy["edown_psum"], 1)

            turn_rows(0, 0, 0, True)
            pairs(pe, step)

        @block.vector
        def _(dve):
            dve.wait_ge(sy["last_psum"], 1)
            sy.link(dve, "last_link", dve.tensor_reduce(last_c[:], bank(7)[0:E, 0:P], AX.X, ALU.max))
            dve.tensor_copy(last_i[:], last_c[:]).then_inc(sy["last_ready"], 1)

            def step(e, n, b, first):
                if not first:
                    dve.wait_ge(sy["edown_psum"], e - 1)
                for m, (m0, w) in enumerate(M_CHUNKS):
                    dve.wait_ge(sy["etanh_ready"], e * NM + (m + 1))
                    g = bank(2 + m)
                    dve.scalar_tensor_tensor(out=aT[b][0:w, m, :], in0=th[0:w, m, :], scalar=1.0,
                                             in1=g[0:w, 0:CAP], op0=ALU.add, op1=ALU.mult
                                             ).then_inc(sy["egate_ready"], 1)
                    dve.wait_ge(sy["egate_ready"], e * NM + (m + 1))
                    dve.tensor_tensor(aT[b][0:w, m, :], aT[b][0:w, m, :], g[0:w, CAP:2 * CAP], ALU.mult
                                      ).then_inc(sy["eact_ready"], 1)

            pairs(dve, step)


CONV = 4
MH = 4
XBC = D + 2 * P
NXBC = XBC // P
LH = 8
LD = S // LH
HPT = P // LD
LD_SCALE = float(np.float32(1.0) / np.sqrt(np.float32(LD)))
LE, LR, LK = 8, 16, 2
F = 2048
FC = F // P
SCALING = 2.0


def phase3(nc, sy, const, dr, base, nseq=NSEQ):
    with ExitStack() as ctx:
        def sb(name, shape, dt=F32):
            return ctx.enter_context(nc.sbuf_tensor(name, shape, dt))

        w_in = sb("w_in", [P, KC, D + XBC + MH])
        w_mo = sb("w_mo", [P, KC, D])
        w1 = sb("w1", [P, KC, F])
        w2 = sb("w2", [P, FC, D])
        a1 = sb("a1", [P, KC, P])
        b1l = sb("b1l", [P, F])
        a2 = sb("a2", [P, FC, P])
        b2l = sb("b2l", [P, D])
        wr = sb("wr", [P, KC, LE])
        norm_bc, bias2_bc = sb("norm_bc", [P, D]), sb("bias2_bc", [P, D])
        small = sb("small", [P, 64])
        conv_w = small[:, 0:24].rearrange("p (c k) -> p c k", k=CONV)
        conv_b = small[:, 24:30]
        dt_bias, a_log, d_skip = small[:, 32:36], small[:, 36:40], small[:, 40:44]
        gamma, br = small[:, 44:45], small[:, 48:56]
        bias1 = sb("bias1", [P, FC])
        neg_a = sb("neg_a", [P, MH])
        tri_gt = sb("tri_gt", [P, P])
        tri_le = sb("tri_le", [P, 3 * P])
        erow = sb("erow", [P, P])

        xn = sb("xn3", [P, NT, D])
        x, h, hT = sb("x3", [P, NT, D]), sb("h3", [P, NT, D]), sb("hT3", [P, KC, S])
        cx, cxT = sb("cx", [P, NT, D]), sb("cxT", [P, KC, S])
        zs = sb("zs", [P, NT, D])
        y = sb("y", [P, NT, D])
        yk = zs
        slots, wk = sb("slots3", [P, NT, 8], I32), sb("wk", [P, NT, 8])
        scratch = sb("scratch", [P, 8192])
        st, mv = sb("st3", [P, NT, 6]), sb("mv3", [P, NT, 2])
        ve, rstd = sb("ve3", [P, NT]), sb("rstd3", [P, NT])

        def view(at, *shape):
            n = int(np.prod(shape))
            names = "abcd"[:len(shape)]
            ap = scratch[:, at:at + n]
            if len(shape) == 1:
                return ap
            return ap.rearrange(f"p ({' '.join(names)}) -> p {' '.join(names)}",
                                **{k: v for k, v in zip(names[1:], shape[1:])})

        raw, convh = view(0, NXBC, S), view(1536, NXBC, S)
        xbc = raw
        cth = view(3072, 2, S)
        xr, xdt = view(3584, NT, P), view(3840, NT, MH, P)
        trid = view(4864, MH, 3, P)
        decay, wgt = view(6400, 2, 3 * P), view(7168, 2, 3 * P)
        dts = sb("dts", [P, 10, NT * MH])
        ssq, grstd = sb("ssq", [P, NT * MH]), sb("grstd", [P, NT * MH])
        prob, probT = view(0, 2, 4, D), view(4096, 2, 4, D)
        smx, snm, ssum = sb("smx", [P, LH, 4]), sb("snm", [P, LH, 4]), sb("ssum", [P, LH, 4])
        mixT = view(0, FC, S)
        act2, ca = view(4096, 2, LK, S), view(5120, 3, LK, S)
        mrow = view(6656, NT, 4, P)
        maskT = sb("maskT", [P, 4, S])
        m0, m01, t2m, t2b = (sb(n, [P, S]) for n in ("m0", "m01", "t2m", "t2b"))
        lg = sb("lg", [P, NT, LE])
        lex, lpr, ltop, lidxf = (sb(n, [P, NT, 8]) for n in ("lex", "lpr", "ltop", "lidxf"))
        lidx = sb("lidx", [P, NT, 8], U32)
        lmax, lsum, lw = sb("lmax", [P, NT, 8]), sb("lsum", [P, NT]), sb("lw", [P, NT])

        ident, bank = const["ident"], const["bank"]
        block = ctx.enter_context(nc.Block())
        GATHERS = NT * TOPK
        W3A, W3B = 16 * 4, 16 * 9

        @block.sync
        def _(sp):
            def load(i, *what):
                for dst, src, sem in what:
                    sp.dma_start(dst[:], dr[src][bass.ds(i, 1)].rearrange("o p t d -> (o p) t d")
                                 ).then_inc(sy[sem], 16)

            routes = ((slots, "slots", "slots_in"), (wk, "route_w", "wk_in"))
            rows = (xn, "mid", "x3_in"),
            context = (cx, "ctx", "ctx3_in"), (cxT, "ctxT", "ctx3_in")
            load(0, *routes, *rows)
            for dst, src in ((w_in, "w_in"), (small, "small"), (norm_bc, "norm_bc"), (w_mo, "w_mo")):
                sp.dma_start(dst[:], dr[src]).then_inc(sy["w3_in"], 16)
            load(0, *context)
            for dst, src in ((bias1, "bias1"), (bias2_bc, "bias2_bc"), (wr, "wr"), (a1, "a1"), (b1l, "b1l"),
                             (a2, "a2"), (b2l, "b2l"), (w1, "w1"), (w2, "w2")):
                sp.dma_start(dst[:], dr[src]).then_inc(sy["w3b_in"], 16)
            sp.sem_inc(sy["out_done"], 1)
            sy.clear_turn(sp, 0, base)

            def turn(i, more):
                if more:
                    load(i + 1, *routes)
                    sp.wait_ge(sy["resid_ready"], 1)
                    load(i + 1, *rows)
                    sp.wait_ge(sy["ret_psum"], LH)
                    load(i + 1, *context)
                sp.wait_ge(sy["x_out_ready"], 2)
                sp.dma_start(dr["out"][bass.ds(i, 1)].rearrange("o (t p) d -> (o p) t d", p=P), x[:]
                             ).then_inc(sy["out_done"], 16)
                sy.clear_turn(sp, i, base + 1)

            with sp.Fori(0, nseq - 1) as i:
                turn(i, True)
            turn(nseq - 1, False)
            sp.wait_ge(sy["out_done"], nseq * 16 + 1)

        @block.gpsimd
        def _(pool):
            sy.link(pool, "init3_link", pool.memset(tri_le[:], 1.0))
            pool.affine_select(out=tri_le[:, 0:P], in_=tri_le[:, 0:P], compare_op=ALU.is_ge, fill=0.0, base=0,
                               pattern=[[1, P]], channel_multiplier=-1)
            pool.affine_select(out=tri_le[:, 2 * P:3 * P], in_=tri_le[:, 2 * P:3 * P], compare_op=ALU.is_ge,
                               fill=0.0, base=0, pattern=[[1, P]], channel_multiplier=-1)
            sy.link(pool, "init3_link", pool.memset(tri_gt[:], 1.0))
            pool.affine_select(out=tri_gt[:], in_=tri_gt[:], compare_op=ALU.is_gt, fill=0.0, base=0,
                               pattern=[[-1, P]], channel_multiplier=1)
            pool.iota(erow[:], pattern=[[1, LE], [0, LR]], base=0, channel_multiplier=0,
                      allow_small_or_imprecise_dtypes=True).then_inc(sy["init3"], 1)

            def gather(g):
                k, j = g // NT, g % NT
                if g >= 2:
                    pool.wait_ge(sy["yk_used"], g - 1)
                pool.indirect_dma_start(
                    out=yk[:, j, :], out_offset=None, in_=dr["expert_out"],
                    in_offset=bass.IndirectOffsetOnAxis(ap=slots[:, j, k:k + 1], axis=0)
                ).then_inc(sy[f"yk_in{j}"], 16)

            pool.wait_ge(sy["slots_in"], 16)
            for g in range(GATHERS):
                gather(g)
            rstd_pool(pool, sy, 0, mv, ve, rstd, const["minus_half"])
            sy.end_turn(pool, 0, base, "pool_link")

            def turn(i, more):
                pool.wait_ge(sy["dA_ready"], 1)
                dt, da = dts[:, 8, :], dts[:, 9, :]
                for hd in range(MH):
                    for m, (src, t) in enumerate(((tri_gt[:], 0), (tri_gt[:], 1), (tri_le[:, P:2 * P], 1))):
                        ins = pool.tensor_scalar(trid[:, hd, m, :], src, da[:, t * MH + hd:t * MH + hd + 1], None,
                                                 ALU.mult)
                    ins.then_inc(sy["tri_ready"], 1)
                pool.wait_ge(sy["xrows_ready"], 1)
                for t in range(NT):
                    for hd in range(MH):
                        ins = pool.tensor_scalar(xdt[:, t, hd, :], xr[:, t, :], dt[:, t * MH + hd:t * MH + hd + 1],
                                                 None, ALU.mult)
                ins.then_inc(sy["xdt_ready"], 1)
                for hd in range(MH):
                    pool.wait_ge(sy["decay_ready"], hd + 1)
                    pool.tensor_tensor(decay[:, hd % 2, :], decay[:, hd % 2, :], tri_le[:], ALU.mult
                                       ).then_inc(sy["decaymask_ready"], 1)
                pool.wait_ge(sy["sumsq_ready"], 1)
                sy.link(pool, "pool_link", pool.tensor_scalar(ssq[:], ssq[:], 1.0 / P, EPS, ALU.mult, ALU.add))
                pool.tensor_tensor(grstd[:], ssq[:], const["minus_half"][:, 0:NT * MH], ALU.pow
                                   ).then_inc(sy["gated_norm"], 1)
                rstd_pool(pool, sy, 0, mv, ve, rstd, const["minus_half"])
                for n in range(4 * LH):
                    hd, lc = n // 4, n % 4
                    pool.wait_ge(sy["smax_ready"], n + 1)
                    pool.tensor_scalar(snm[:, hd, lc:lc + 1], smx[:, hd, lc:lc + 1], -LD_SCALE, None, ALU.mult
                                       ).then_inc(sy["snegmax_ready"], 1)
                rstd_pool(pool, sy, 1, mv, ve, rstd, const["minus_half"])
                if more:
                    pool.wait_ge(sy["slots_in"], (i + 2) * 16)
                    sy.alone(pool)
                for f in range(FC):
                    if more and f < GATHERS:
                        gather(f)
                    if more and f == GATHERS + 2:
                        rstd_pool(pool, sy, 2, mv, ve, rstd, const["minus_half"])
                    pool.wait_ge(sy["ca_ready"], f + 1)
                    pool.tensor_tensor(mixT[:, f, :], ca[:, f % 3, 0, :], ca[:, f % 3, 1, :], ALU.add
                                       ).then_inc(sy["mix_ready"], 1)
                sy.end_turn(pool, i, base + 1, "pool_link")

            with pool.Fori(0, nseq - 1) as i:
                turn(i, True)
            turn(nseq - 1, False)

        @block.scalar
        def _(act):
            def cols_copy(k):
                for j in range(NT):
                    act.wait_ge(sy["rowsT_psum"], NT * k + j + 1)
                    act.activation(hT[:, :, j * P:(j + 1) * P],
                                   bank(j)[:, :].rearrange("p (c t) -> p c t", c=KC), ACT.Copy
                                   ).then_inc(sy["colsT_ready"], 1)

            act.wait_ge(sy["w3_in"], W3A)
            act.activation(neg_a[:], a_log, ACT.Exp).then_inc(sy["a_exp"], 1)
            cols_copy(0)
            sy.end_turn(act, 0, base)

            def turn(i, more):
                act.wait_ge(sy["dtabs_ready"], 1)
                act.activation(dts[:, 2, :], dts[:, 1, :], ACT.Exp, scale=-1.0).then_inc(sy["dtexp_ready"], 1)
                act.wait_ge(sy["dtone_ready"], 1)
                act.activation(dts[:, 4, :], dts[:, 3, :], ACT.Ln).then_inc(sy["dtln_ready"], 1)
                for c in range(NXBC + 1):
                    if c < NXBC:
                        act.wait_ge(sy["xbc_psum"], c + 1)
                        act.activation(raw[:, c, :], bank(2 + c % 2)[:, 0:S], ACT.Copy
                                       ).then_inc(sy["xbc_raw_ready"], 1)
                    if c >= 1:
                        act.wait_ge(sy["conv_ready"], c)
                        if c >= 3:
                            act.wait_ge(sy["xbc_ready"], c - 2)
                        act.activation(cth[:, (c - 1) % 2, :], convh[:, c - 1, :], ACT.Tanh
                                       ).then_inc(sy["convtanh_ready"], 1)
                for j in range(NT):
                    act.wait_ge(sy["z_psum"], j + 1)
                    act.activation(zs[:, j, :], bank(4 + j)[:, :], ACT.Tanh, scale=0.5
                                   ).then_inc(sy["ztanh_ready"], 1)
                act.wait_ge(sy["xrows_psum"], 1)
                act.activation(xr[:], bank(6)[:, 0:NT * P].rearrange("p (t d) -> p t d", t=NT), ACT.Copy
                               ).then_inc(sy["xrows_ready"], 1)
                for hd in range(MH):
                    act.wait_ge(sy["decay_psum"], hd + 1)
                    if hd >= 2:
                        act.wait_ge(sy["w_ready"], hd - 1)
                    act.activation(decay[:, hd % 2, :], bank(hd % 2)[:, 0:3 * P], ACT.Exp
                                   ).then_inc(sy["decay_ready"], 1)
                for j in range(NT):
                    act.wait_ge(sy["gated_ready"], j + 1)
                    for hd in range(MH):
                        ins = act.activation(h[:, j, hd * P:(hd + 1) * P], y[:, j, hd * P:(hd + 1) * P], ACT.Square,
                                             accum_out=ssq[:, j * MH + hd:j * MH + hd + 1])
                ins.then_inc(sy["sumsq_ready"], 1)
                cols_copy(0)

                def copy_blocks(n):
                    act.wait_ge(sy["sT_psum"], n + 1)
                    hd, lc = n // 4, n % 4
                    act.activation(probT[:, hd % 2, :, lc * P:(lc + 1) * P],
                                   bank(4 + lc % 2)[:, :].rearrange("p (c t) -> p c t", c=4), ACT.Copy
                                   ).then_inc(sy["sT_act"], 1)

                for n in range(4 * LH + 4):
                    if n < 4 * LH:
                        hd, lc = n // 4, n % 4
                        act.wait_ge(sy["snegmax_ready"], n + 1)
                        if hd >= 2:
                            act.wait_ge(sy["sT_psum"], n - 7)
                        act.activation(prob[:, hd % 2, lc, :], bank(lc)[:, :], ACT.Exp, bias=snm[:, hd, lc:lc + 1],
                                       scale=LD_SCALE, accum_out=ssum[:, hd, lc:lc + 1]).then_inc(sy["sexp_ready"], 1)
                    if n >= 4 and n % 2 == 0:
                        if (n - 4) % 4 == 0 and n >= 12:
                            act.wait_ge(sy["ret_psum"], (n - 4) // 4 - 1)
                        copy_blocks(n - 4)
                cols_copy(1)
                act.wait_ge(sy["w3b_in"], W3B)
                for j in range(NT):
                    act.wait_ge(sy["moe_negmax"], j + 1)
                    act.activation(lex[:, j, :], lg[:, j, :], ACT.Exp, bias=lw[:, j:j + 1],
                                   accum_out=lsum[:, j:j + 1]).then_inc(sy["moe_exp"], 1)
                for j in range(NT):
                    act.wait_ge(sy["maskT_psum"], j + 1)
                    act.activation(maskT[:, :, j * P:(j + 1) * P],
                                   bank(j)[:, :].rearrange("p (c t) -> p c t", c=4), ACT.Copy
                                   ).then_inc(sy["maskT_ready"], 1)
                for f in range(FC + 1):
                    if f < FC:
                        act.wait_ge(sy["base_psum"], f + 1)
                        if f >= 2:
                            act.wait_ge(sy["ca_ready"], f - 1)
                        act.activation(act2[:, f % 2, 0, :], bank(f % 4)[:, 0:S], ACT.Gelu_apprx_tanh,
                                       bias=bias1[:, f:f + 1]).then_inc(sy["gelu0_ready"], 1)
                    if f >= 1:
                        g = f - 1
                        act.wait_ge(sy["base1_psum"], g + 1)
                        act.activation(act2[:, g % 2, 1, :], bank(g % 4)[:, 0:S], ACT.Gelu_apprx_tanh,
                                       bias=bias1[:, g:g + 1]).then_inc(sy["gelu1_ready"], 1)
                if more:
                    cols_copy(2)
                sy.end_turn(act, i, base + 1)

            with act.Fori(0, nseq - 1) as i:
                turn(i, True)
            turn(nseq - 1, False)

        @block.tensor
        def _(pe):
            def rows_to_cols(src, ready, at):
                for j in range(NT):
                    pe.wait_ge(ready, at + j + 1)
                    transposes_pe(pe, ident, src, bank(j), j).then_inc(sy["rowsT_psum"], 1)

            rows_to_cols(h, sy["normed_ready"], 0)
            pe.wait_ge(sy["w3_in"], W3A)
            pe.wait_ge(sy["init3"], 1)
            sy.end_turn(pe, 0, base)

            def turn(i, more):
                for j in range(NT):
                    ins = project_pe(pe, bank(6)[:, j * MH:(j + 1) * MH], lambda kc: hT[:, kc, j * P:(j + 1) * P],
                                     lambda kc: w_in[:, kc, D + XBC:D + XBC + MH])
                ins.then_inc(sy["dt_psum"], 1)
                for c in range(NXBC):
                    if c >= 2:
                        pe.wait_ge(sy["xbc_raw_ready"], c - 1)
                    project_pe(pe, bank(2 + c % 2)[:, 0:S], lambda kc: w_in[:, kc, D + c * P:D + (c + 1) * P],
                               lambda kc: hT[:, kc, :]).then_inc(sy["xbc_psum"], 1)
                for j in range(NT):
                    project_pe(pe, bank(4 + j)[:, :], lambda kc: hT[:, kc, j * P:(j + 1) * P],
                               lambda kc: w_in[:, kc, 0:D]).then_inc(sy["z_psum"], 1)
                pe.wait_ge(sy["xbc_ready"], 1)
                pe.wait_ge(sy["tri_ready"], 1)
                for t in range(NT):
                    ins = pe.transpose(bank(6)[:, t * P:(t + 1) * P], xbc[:, 0, t * P:(t + 1) * P], ident)
                ins.then_inc(sy["xrows_psum"], 1)
                pe.wait_ge(sy["xbc_ready"], NXBC)
                for s in range(MH + 1):
                    if s < MH:
                        pe.wait_ge(sy["tri_ready"], s + 1)
                        if s >= 2:
                            pe.wait_ge(sy["w_ready"], s - 1)
                        b, g = bank(s % 2), bank(2 + s % 2)
                        pe.matmul(b[:, 0:2 * P], trid[:, s, 0, :], tri_le[:, 0:2 * P], start=True, stop=False,
                                  skip_group_check=True)
                        pe.matmul(b[:, P:2 * P], trid[:, s, 2, :], tri_le[:, 0:P], start=False, stop=True,
                                  skip_group_check=True)
                        pe.matmul(b[:, 2 * P:3 * P], trid[:, s, 1, :], tri_le[:, 0:P], start=True, stop=True,
                                  skip_group_check=True).then_inc(sy["decay_psum"], 1)
                        pe.matmul(g[:, 0:2 * P], xbc[:, 1, 0:P], xbc[:, 2 + s, :], start=True, stop=True)
                        pe.matmul(g[:, 2 * P:3 * P], xbc[:, 1, P:S], xbc[:, 2 + s, P:S], start=True, stop=True
                                  ).then_inc(sy["bc_psum"], 1)
                    if s >= 1:
                        hd = s - 1
                        if hd == 0:
                            pe.wait_ge(sy["zs_ready"], NT)
                            pe.wait_ge(sy["xdt_ready"], 1)
                        pe.wait_ge(sy["w_ready"], hd + 1)
                        w = wgt[:, hd % 2, :]
                        cols = slice(hd * P, (hd + 1) * P)
                        pe.matmul(bank(4)[:, cols], w[:, 0:P], xdt[:, 0, hd, :], start=True, stop=True)
                        pe.matmul(bank(5)[:, cols], w[:, P:2 * P], xdt[:, 0, hd, :], start=True, stop=False)
                        pe.matmul(bank(5)[:, cols], w[:, 2 * P:3 * P], xdt[:, 1, hd, :], start=False, stop=True
                                  ).then_inc(sy["y_psum"], 1)
                rows_to_cols(y, sy["attn_ready"], 0)
                pe.wait_ge(sy["colsT_ready"], NT)
                for j in range(NT):
                    project_pe(pe, bank(2 + j)[:, :], lambda kc: hT[:, kc, j * P:(j + 1) * P],
                               lambda kc: w_mo[:, kc, :]).then_inc(sy["out_psum"], 1)
                pe.wait_ge(sy["normed_ready"], NT)
                pe.wait_ge(sy["ctx3_in"], (i + 1) * 32)
                for n in range(4 * LH + 6):
                    if n < 4 * LH:
                        hd, lc = n // 4, n % 4
                        j, r = hd // HPT, (hd % HPT) * LD
                        if n >= 4:
                            pe.wait_ge(sy["sexp_ready"], n - 3)
                        pe.matmul(bank(lc)[:, :], h[r:r + LD, j, lc * P:(lc + 1) * P], cx[r:r + LD, j, :],
                                  start=True, stop=True).then_inc(sy["s_psum"], 1)
                    if 4 <= n < 4 * LH + 4:
                        m = n - 4
                        hd, lc = m // 4, m % 4
                        pe.wait_ge(sy["snormed_ready"], m + 1)
                        if m >= 2:
                            pe.wait_ge(sy["sT_act" if m % 2 == 0 else "sT_dve"], m // 2)
                        for mc in range(4):
                            ins = pe.transpose(bank(4 + lc % 2)[:, mc * P:(mc + 1) * P],
                                               prob[:, hd % 2, lc, mc * P:(mc + 1) * P], ident)
                        ins.then_inc(sy["sT_psum"], 1)
                    if n >= 9 and (n - 9) % 4 == 0:
                        hd = (n - 9) // 4
                        j, r = hd // HPT, (hd % HPT) * LD
                        pe.wait_ge(sy["sT_act"], 2 * hd + 2)
                        pe.wait_ge(sy["sT_dve"], 2 * hd + 2)
                        for mc in range(4):
                            ins = pe.matmul(bank(6 + j)[r:r + LD, :], cxT[:, mc, hd * LD:(hd + 1) * LD],
                                            probT[:, hd % 2, mc, :], start=(mc == 0), stop=(mc == 3),
                                            tile_position=(0, r))
                        ins.then_inc(sy["ret_psum"], 1)
                rows_to_cols(h, sy["normed_ready"], NT)
                pe.wait_ge(sy["colsT_ready"], 2 * NT)
                pe.wait_ge(sy["w3b_in"], W3B)
                for j in range(NT):
                    ins = project_pe(pe, bank(4)[:, j * LE:(j + 1) * LE], lambda kc: hT[:, kc, j * P:(j + 1) * P],
                                     lambda kc: wr[:, kc, :])
                ins.then_inc(sy["moe_psum"], 1)
                project_pe(pe, bank(5)[:, 0:S], lambda kc: a1[:, kc, :], lambda kc: hT[:, kc, :]
                           ).then_inc(sy["t1_psum"], 1)
                for j in range(NT):
                    pe.wait_ge(sy["mask_rows"], j + 1)
                    for m in range(4):
                        ins = pe.transpose(bank(j)[:, m * P:(m + 1) * P], mrow[:, j, m, :], ident)
                    ins.then_inc(sy["maskT_psum"], 1)
                pe.wait_ge(sy["m0_ready"], 1)
                for f in range(FC + 3):
                    if f < FC:
                        if f >= 4:
                            pe.wait_ge(sy["gelu1_ready"], f - 3)
                        for kc in range(KC):
                            pe.matmul(bank(f % 4)[:, 0:S], w1[:, kc, f * P:(f + 1) * P], hT[:, kc, :],
                                      start=(kc == 0), stop=False, skip_group_check=True)
                        pe.matmul(bank(f % 4)[:, 0:S], b1l[:, f * P:(f + 1) * P], m0[:], start=False, stop=True,
                                  skip_group_check=True).then_inc(sy["base_psum"], 1)
                    if 1 <= f <= FC:
                        g = f - 1
                        pe.wait_ge(sy["gelu0_ready"], g + 1)
                        pe.matmul(bank(g % 4)[:, 0:S], b1l[:, g * P:(g + 1) * P], m01[:], start=False, stop=True,
                                  skip_group_check=True).then_inc(sy["base1_psum"], 1)
                    if f == FC + 1 and more:
                        pe.wait_ge(sy["gelu1_ready"], FC)
                        rows_to_cols(h, sy["normed_ready"], 2 * NT)
                    if f >= 3:
                        g = f - 3
                        pe.wait_ge(sy["ca_ready"], g + 1)
                        pe.matmul(bank(4)[:, :], a2[:, g, :], ca[:, g % 3].rearrange("p k t -> p (k t)"),
                                  start=(g == 0), stop=(g == FC - 1)).then_inc(sy["t2_psum"], 1)
                        pe.wait_ge(sy["mix_ready"], g + 1)
                        for j in range(NT):
                            pe.matmul(bank(6 + j)[:, :], mixT[:, g, j * P:(j + 1) * P], w2[:, g, :],
                                      start=(g == 0), stop=False)
                pe.wait_ge(sy["t2m_ready"], 1)
                for j in range(NT):
                    pe.matmul(bank(6 + j)[:, :], t2m[:, j * P:(j + 1) * P], b2l[:], start=False, stop=True
                              ).then_inc(sy["y_out_psum"], 1)
                sy.end_turn(pe, i, base + 1)

            with pe.Fori(0, nseq - 1) as i:
                turn(i, True)
            turn(nseq - 1, False)

        @block.vector
        def _(dve):
            def ln(ins):
                sy.link(dve, "dve_link", ins)

            def combine(g, n):
                k, j = g // NT, g % NT
                dve.wait_ge(sy[f"yk_in{j}"], n * (16 * TOPK) + (16 * k + 16))
                sy.alone(dve)
                if g >= 2:
                    dve.wait_ge(sy["yk_used"], g - 1)
                dve.scalar_tensor_tensor(out=xn[:, j, :], in0=yk[:, j, :], scalar=wk[:, j, k:k + 1],
                                         in1=xn[:, j, :], op0=ALU.mult, op1=ALU.add).then_inc(sy["yk_used"], 1)

            dve.wait_ge(sy["x3_in"], 16)
            dve.wait_ge(sy["wk_in"], 16)
            for g in range(GATHERS):
                combine(g, 0)
            dve.wait_ge(sy["yk_used"], GATHERS)
            layernorm_rows(dve, sy, 0, xn, h, st, mv, rstd)
            dve.wait_ge(sy["w3_in"], W3A)
            dve.wait_ge(sy["init3"], 1)
            dve.wait_ge(sy["a_exp"], 1)
            sy.link(dve, "dve_link3", dve.tensor_scalar(neg_a[:], neg_a[:], -1.0, None, ALU.mult))
            sy.link(dve, "dve_link3", dve.tensor_scalar(small[:, 0:30], small[:, 0:30], 0.5, None, ALU.mult))
            sy.end_turn(dve, 0, base, "dve_link")

            def turn(i, more):
                dve.wait_ge(sy["dt_psum"], 1)
                v, av, e, w, lnw, d, m, sp_, dt, da = (dts[:, k, :] for k in range(10))
                ln(dve.tensor_tensor(v.rearrange("p (t h) -> p t h", t=NT),
                                     bank(6)[:, 0:NT * MH].rearrange("p (t h) -> p t h", t=NT),
                                     dt_bias.unsqueeze(1).broadcast_to([P, NT, MH]), ALU.add))
                dve.scalar_tensor_tensor(out=av, in0=v, scalar=-1.0, in1=v, op0=ALU.mult, op1=ALU.max).then_inc(sy["dtabs_ready"], 1)
                dve.wait_ge(sy["dtexp_ready"], 1)
                dve.tensor_scalar(w, e, 1.0, None, ALU.add).then_inc(sy["dtone_ready"], 1)
                dve.wait_ge(sy["dtln_ready"], 1)
                ln(dve.tensor_scalar(d, w, -1.0, None, ALU.add))
                ln(dve.tensor_scalar(m, d, 0.0, None, ALU.is_equal))
                ln(dve.tensor_tensor(d, d, m, ALU.add))
                ln(dve.reciprocal(d, d))
                ln(dve.tensor_tensor(m, m, lnw, ALU.add))
                ln(dve.tensor_tensor(m, m, d, ALU.mult))
                ln(dve.tensor_tensor(m, m, e, ALU.mult))
                ln(dve.scalar_tensor_tensor(out=dt, in0=v, scalar=0.0, in1=m, op0=ALU.max, op1=ALU.add))
                dve.tensor_tensor(da.rearrange("p (t h) -> p t h", t=NT), dt.rearrange("p (t h) -> p t h", t=NT),
                                  neg_a[:].unsqueeze(1).broadcast_to([P, NT, MH]), ALU.mult
                                  ).then_inc(sy["dA_ready"], 1)
                for c in range(NXBC + 1):
                    if c < NXBC:
                        dve.wait_ge(sy["xbc_raw_ready"], c + 1)
                        ln(dve.tensor_scalar(convh[:, c, :], raw[:, c, :], conv_w[:, c, 3:4], conv_b[:, c:c + 1],
                                             ALU.mult, ALU.add))
                        for k in range(CONV - 1):
                            lag = CONV - 1 - k
                            ins = dve.scalar_tensor_tensor(
                                out=convh[:, c, lag:S], in0=raw[:, c, 0:S - lag], scalar=conv_w[:, c, k:k + 1],
                                in1=convh[:, c, lag:S], op0=ALU.mult, op1=ALU.add)
                            if k < CONV - 2:
                                ln(ins)
                        ins.then_inc(sy["conv_ready"], 1)
                    if c >= 1:
                        dve.wait_ge(sy["convtanh_ready"], c)
                        dve.scalar_tensor_tensor(out=xbc[:, c - 1, :], in0=cth[:, (c - 1) % 2, :], scalar=1.0,
                                                 in1=convh[:, c - 1, :], op0=ALU.add, op1=ALU.mult
                                                 ).then_inc(sy["xbc_ready"], 1)
                for j in range(NT):
                    dve.wait_ge(sy["ztanh_ready"], j + 1)
                    dve.scalar_tensor_tensor(out=zs[:, j, :], in0=zs[:, j, :], scalar=1.0, in1=bank(4 + j)[:, :],
                                             op0=ALU.add, op1=ALU.mult).then_inc(sy["zs_ready"], 1)
                for hd in range(MH):
                    dve.wait_ge(sy["decaymask_ready"], hd + 1)
                    dve.wait_ge(sy["bc_psum"], hd + 1)
                    if hd >= 2:
                        dve.wait_ge(sy["y_psum"], hd - 1)
                    dve.tensor_tensor(wgt[:, hd % 2, :], decay[:, hd % 2, :], bank(2 + hd % 2)[:, 0:3 * P], ALU.mult
                                      ).then_inc(sy["w_ready"], 1)
                dve.wait_ge(sy["y_psum"], MH)
                for j in range(NT):
                    for hd in range(MH):
                        c = slice(hd * P, (hd + 1) * P)
                        ins = dve.scalar_tensor_tensor(out=y[:, j, c], in0=xr[:, j, :], scalar=d_skip[:, hd:hd + 1],
                                                       in1=bank(4 + j)[:, c], op0=ALU.mult, op1=ALU.add)
                    ln(ins)
                    dve.scalar_tensor_tensor(out=y[:, j, :], in0=y[:, j, :], scalar=0.5, in1=zs[:, j, :],
                                             op0=ALU.mult, op1=ALU.mult).then_inc(sy["gated_ready"], 1)
                dve.wait_ge(sy["gated_norm"], 1)
                for j in range(NT):
                    ln(dve.tensor_tensor(heads_view(y[:, j, :], MH), heads_view(y[:, j, :], MH),
                                         grstd[:, j * MH:(j + 1) * MH].unsqueeze(2).broadcast_to([P, MH, P]),
                                         ALU.mult))
                    dve.tensor_tensor(y[:, j, :], y[:, j, :], norm_bc[:], ALU.mult).then_inc(sy["attn_ready"], 1)
                dve.wait_ge(sy["out_done"], i * 16 + 1)
                sy.alone(dve)
                for j in range(NT):
                    dve.wait_ge(sy["out_psum"], j + 1)
                    ins = dve.tensor_tensor(x[:, j, :], xn[:, j, :], bank(2 + j)[:, :], ALU.add)
                ins.then_inc(sy["resid_ready"], 1)
                dve.wait_ge(sy["resid_ready"], 1)
                layernorm_rows(dve, sy, 0, x, h, st, mv, rstd)
                for n in range(4 * LH + 6):
                    if n < 4 * LH:
                        hd, lc = n // 4, n % 4
                        dve.wait_ge(sy["s_psum"], n + 1)
                        dve.tensor_reduce(smx[:, hd, lc:lc + 1], bank(lc)[:, :], AX.X, ALU.max
                                          ).then_inc(sy["smax_ready"], 1)
                    if 2 <= n < 4 * LH + 2:
                        m = n - 2
                        hd, lc = m // 4, m % 4
                        dve.wait_ge(sy["sexp_ready"], m + 1)
                        ln(dve.reciprocal(ssum[:, hd, lc:lc + 1], ssum[:, hd, lc:lc + 1]))
                        dve.tensor_scalar(prob[:, hd % 2, lc, :], prob[:, hd % 2, lc, :], ssum[:, hd, lc:lc + 1],
                                          None, ALU.mult).then_inc(sy["snormed_ready"], 1)
                    if n >= 5 and n % 2 == 1 and n - 4 < 4 * LH:
                        m = n - 4
                        hd, lc = m // 4, m % 4
                        dve.wait_ge(sy["sT_psum"], m + 1)
                        if lc == 1 and hd >= 2:
                            dve.wait_ge(sy["ret_psum"], hd - 1)
                        dve.tensor_copy(probT[:, hd % 2, :, lc * P:(lc + 1) * P],
                                        bank(4 + lc % 2)[:, :].rearrange("p (c t) -> p c t", c=4)
                                        ).then_inc(sy["sT_dve"], 1)
                for j in range(NT):
                    dve.wait_ge(sy["ret_psum"], HPT * (j + 1))
                    ins = dve.scalar_tensor_tensor(out=x[:, j, :], in0=bank(6 + j)[:, :], scalar=gamma,
                                                   in1=x[:, j, :], op0=ALU.mult, op1=ALU.add)
                ln(ins)
                layernorm_rows(dve, sy, 1, x, h, st, mv, rstd)
                dve.wait_ge(sy["w3b_in"], W3B)
                dve.wait_ge(sy["moe_psum"], 1)
                for j in range(NT):
                    ln(dve.tensor_tensor(lg[:, j, :], bank(4)[:, j * LE:(j + 1) * LE], br, ALU.add))
                    ln(dve.max(lmax[:, j, :], lg[:, j, :]))
                    dve.tensor_scalar(lw[:, j:j + 1], lmax[:, j, 0:1], -1.0, None, ALU.mult
                                      ).then_inc(sy["moe_negmax"], 1)
                for j in range(NT):
                    dve.wait_ge(sy["moe_exp"], j + 1)
                    ln(dve.reciprocal(lsum[:, j:j + 1], lsum[:, j:j + 1]))
                    ln(dve.tensor_scalar(lpr[:, j, :], lex[:, j, :], lsum[:, j:j + 1], None, ALU.mult))
                    ln(dve.max(ltop[:, j, :], lpr[:, j, :]))
                    ln(dve.max_index(lidx[:, j, :], ltop[:, j, :], lpr[:, j, :]))
                    ln(dve.tensor_copy(lidxf[:, j, :], lidx[:, j, :]))
                    for k in range(LK):
                        dve.tensor_scalar(mrow[:, j, k, :], erow[:], lidxf[:, j, k:k + 1], SCALING, ALU.is_equal,
                                          ALU.mult)
                        ins = dve.tensor_scalar(mrow[:, j, LK + k, :], tri_le[:, P:2 * P], ltop[:, j, k:k + 1], None,
                                                ALU.mult)
                    ins.then_inc(sy["mask_rows"], 1)
                    ln(dve.tensor_tensor(lw[:, j:j + 1], ltop[:, j, 0:1], ltop[:, j, 1:2], ALU.add))
                    ln(dve.scalar_tensor_tensor(out=x[:, j, :], in0=bias2_bc[:], scalar=lw[:, j:j + 1],
                                                in1=x[:, j, :], op0=ALU.mult, op1=ALU.add))
                dve.wait_ge(sy["t1_psum"], 1)
                dve.wait_ge(sy["maskT_ready"], NT)
                ln(dve.tensor_tensor(m0[:], bank(5)[:, 0:S], maskT[:, 0, :], ALU.mult))
                ln(dve.tensor_tensor(m01[:], bank(5)[:, 0:S], maskT[:, 1, :], ALU.mult))
                dve.tensor_tensor(m01[:], m01[:], m0[:], ALU.subtract).then_inc(sy["m0_ready"], 1)
                if more:
                    dve.wait_ge(sy["x3_in"], (i + 2) * 16)
                    sy.alone(dve)
                    dve.wait_ge(sy["wk_in"], (i + 2) * 16)
                    sy.alone(dve)
                for f in range(FC):
                    if more and 1 <= f <= GATHERS:
                        combine(f - 1, i + 1)
                    if more and f == GATHERS + 1:
                        dve.wait_ge(sy["yk_used"], GATHERS)
                        layernorm_stats(dve, sy, xn, st, mv)
                    if more and f == GATHERS + 2:
                        layernorm_apply(dve, sy, 2, xn, h, mv, rstd)
                    dve.wait_ge(sy["gelu1_ready"], f + 1)
                    if f >= 3:
                        dve.wait_ge(sy["t2_psum"], f - 2)
                        dve.wait_ge(sy["mix_ready"], f - 2)
                    dve.tensor_tensor(ca[:, f % 3], act2[:, f % 2], maskT[:, 2:4, :], ALU.mult
                                      ).then_inc(sy["ca_ready"], 1)
                dve.wait_ge(sy["t2_psum"], FC)
                ln(dve.tensor_tensor(t2m[:], bank(4)[:, 0:S], maskT[:, 0, :], ALU.mult))
                ln(dve.tensor_tensor(t2b[:], bank(4)[:, S:2 * S], maskT[:, 1, :], ALU.mult))
                dve.tensor_tensor(t2m[:], t2m[:], t2b[:], ALU.add).then_inc(sy["t2m_ready"], 1)
                for j in range(NT):
                    dve.wait_ge(sy["y_out_psum"], j + 1)
                    dve.tensor_tensor(x[:, j, :], x[:, j, :], bank(6 + j)[:, :], ALU.add
                                      ).then_inc(sy["x_out_ready"], 1)
                sy.end_turn(dve, i, base + 1, "dve_link")

            with dve.Fori(0, nseq - 1) as i:
                turn(i, True)
            turn(nseq - 1, False)


def constants(nc, sy, ctx):
    ident = ctx.enter_context(nc.sbuf_tensor("ident", [P, P], F32))
    iota_t = ctx.enter_context(nc.sbuf_tensor("iota_row", [P, E], F32))
    minus_half = ctx.enter_context(nc.sbuf_tensor("minus_half", [P, 16], F32))
    psum = ctx.enter_context(nc.psum_tensor("psum", [P, 8, 512], F32))
    last = ctx.enter_context(nc.sbuf_tensor("last_token", [P, E], F32))
    tri_lt = ctx.enter_context(nc.sbuf_tensor("tri_lt", [P, P], F32))
    ones = ctx.enter_context(nc.sbuf_tensor("ones", [P, P], F32))
    with nc.Block() as block:
        @block.gpsimd
        def _(pool):
            pool.memset(minus_half[:], -0.5)
            pool.memset(ones[:], 1.0)
            sy.link(pool, "const_link", pool.memset(tri_lt[:], 1.0))
            pool.affine_select(out=tri_lt[:], in_=tri_lt[:], compare_op=ALU.is_gt, fill=0.0, base=0,
                               pattern=[[1, P]], channel_multiplier=-1)
            sy.link(pool, "const_link", pool.memset(ident[:], 0.0))
            pool.affine_select(out=ident[:], in_=ident[:], compare_op=ALU.not_equal, fill=1.0, base=0,
                               pattern=[[-1, P]], channel_multiplier=1).then_inc(sy["const_ready"], 1)
            pool.iota(iota_t[:], pattern=[[1, E]], base=0, channel_multiplier=0,
                      allow_small_or_imprecise_dtypes=True).then_inc(sy["const_ready"], 1)
            pool.wait_ge(sy["const_ready"], 2)
    return {"ident": ident[:], "iota": iota_t[:], "minus_half": minus_half[:], "bank": lambda b: psum[:, b, :],
            "last": last[:], "tri_lt": tri_lt[:], "ones": ones[:]}


def program(nc, dr, phases=(1, 2, 3), nseq=NSEQ, nexp=E):
    with ExitStack() as ctx:
        sy = Sync(nc, ctx)
        for n in ("turn_done", "turn_go"):
            sy[n]
        const = constants(nc, sy, ctx)
        dr["normed_rows"] = dr.get("normed_rows", None) or nc.dram_tensor("normed_rows", [NSEQ, S, D], F32).ap()
        for name, shape in (("mid", [NSEQ, P, NT, D]), ("route_w", [NSEQ, P, NT, 8]), ("expert_out", [E * CAP, D])):
            if name not in dr:
                dr[name] = nc.dram_tensor(name, shape, F32).ap()
        for name, shape in (("slots", [NSEQ, P, NT, 8]), ("slot_token", [E * CAP, 1])):
            if name not in dr:
                dr[name] = nc.dram_tensor(name, shape, I32).ap()
        if 1 in phases:
            phase1(nc, sy, const, dr, 0, nseq)
        if 2 in phases:
            phase2(nc, sy, const, dr)
        if 3 in phases:
            phase3(nc, sy, const, dr, nseq + 1 if 1 in phases else 0, nseq)


def cols_layout(w):
    o, i = w.shape
    return w.T.reshape(i // P, P, o).transpose(1, 0, 2)


def host_layout(a):
    a = {k: np.asarray(v) for k, v in a.items()}
    inv = (1.0 / np.power(np.float32(10000.0), np.arange(0, HD, 2, dtype=np.float32) / np.float32(HD))).astype(np.float32)
    freqs = np.outer(np.arange(S, dtype=np.float32), inv).astype(np.float32)
    emb = np.concatenate([freqs, freqs], -1)
    rot = np.zeros((P, P), np.float32)
    for i in range(0, P, 2):
        rot[i + 1, i], rot[i, i + 1] = -1.0, 1.0
    q, k = np.arange(P)[:, None], np.arange(P)[None, :]
    k1 = np.arange(WINDOW, S)[None, :]
    keep = np.concatenate([(q >= k) & (q - k < WINDOW), (q + P >= k1) & (q + P - k1 < WINDOW)], 1)
    bc = lambda v: np.broadcast_to(v.reshape(1, -1), (P, v.size))
    tokens = lambda t: t.reshape(NSEQ, NT, P, -1).transpose(0, 2, 1, 3)
    d = {
        "x": tokens(a["x"]),
        "ctxT": a["ctx_2048"].transpose(0, 2, 1).reshape(NSEQ, KC, P, S).transpose(0, 2, 1, 3),
        "mask": a["mask_BxS2_ik0"].reshape(NSEQ, NT, P).transpose(0, 2, 1),
        "w_qkv": cols_layout(a["L0_attn_w_qkv"]), "w_out": cols_layout(a["L0_attn_w_out"]),
        "w_gate": cols_layout(a["L0_ffn_gate_weight"]),
        "w_sg": cols_layout(a["L0_ffn_Sg"]), "w_su": cols_layout(a["L0_ffn_Su"]), "w_sd": a["L0_ffn_Sd"].T,
        "cosT": np.tile(np.cos(emb).T, (HPC, 1)), "sinT": np.tile(np.sin(emb).T, (HPC, 1)), "rot": rot,
        "wmask": np.where(keep, 0.0, NEG).astype(np.float32),
        "bq": a["L0_xattn_bq"].reshape(KC, P).T, "bk": a["L0_xattn_bk"].reshape(KC, P).T,
        "rows_bc": np.stack([bc(a["L0_xattn_" + n]) for n in ("bv", "bo", "ln_gamma", "ln_beta")], 1),
        "rs": np.broadcast_to(a["L0_xattn_residual_scale"].reshape(1, 1), (P, 1)),
    }
    small = np.zeros((P, 64), np.float32)
    small[:, 0:24] = a["L1_attn_conv_w"].reshape(NXBC, P, CONV).transpose(1, 0, 2).reshape(P, -1)
    small[:, 24:30] = a["L1_attn_conv_b"].reshape(NXBC, P).T
    small[:, 32:36], small[:, 36:40], small[:, 40:44] = a["L1_attn_dt_bias"], a["L1_attn_A_log"], a["L1_attn_D"]
    small[:, 44], small[:, 48:56] = a["L1_xattn_gamma"], a["L1_ffn_br"]
    d |= {
        "w_gu": np.stack([a["L0_ffn_W" + n].transpose(0, 2, 1).reshape(E, KC, P, M).transpose(0, 2, 1, 3)
                          for n in "gu"], 2),
        "w_d": a["L0_ffn_Wd"].transpose(0, 2, 1),
        "ctx": tokens(a["ctx_2048"]), "small": small, "bias1": a["L1_ffn_b1"].reshape(FC, P).T,
        "w_in": cols_layout(a["L1_attn_in_proj_w"]), "w_mo": cols_layout(a["L1_attn_out_proj_w"]),
        "norm_bc": bc(a["L1_attn_norm_w"]), "bias2_bc": bc(a["L1_ffn_b2"]),
        "wr": cols_layout(a["L1_ffn_Wr"].T), "w1": cols_layout(a["L1_ffn_W1"].T),
        "w2": cols_layout(a["L1_ffn_W2"].T), "a1": cols_layout(a["L1_ffn_A1"].reshape(LE * LR, D)),
        "b1l": a["L1_ffn_B1"].transpose(0, 2, 1).reshape(LE * LR, F),
        "a2": cols_layout(a["L1_ffn_A2"].reshape(LE * LR, F)),
        "b2l": a["L1_ffn_B2"].transpose(0, 2, 1).reshape(LE * LR, D),
    }
    for n in "qkvo":
        d["w_x" + n] = cols_layout(a["L0_xattn_W" + n])
    return {k: np.ascontiguousarray(v) for k, v in d.items()}


def kernel(**inputs):
    import concourse.bacc as bacc
    from concourse.bass_utils import run_bass_kernel_spmd as run

    arrays = host_layout(inputs)
    nc = bacc.Bacc("TRN2", target_bir_lowering=False, num_devices=1)
    dr = {n: nc.dram_tensor(f"in_{n}_dram", a.shape, mybir.dt.from_np(a.dtype), kind="ExternalInput").ap()
          for n, a in arrays.items()}
    dr["out"] = nc.dram_tensor("out_dram", [NSEQ, S, D], F32, kind="ExternalOutput").ap()
    program(nc, dr)
    r = run(nc, [{f"in_{n}_dram": a for n, a in arrays.items()}], core_ids=[0])
    return r.results[0]["out_dram"]
```

```python
from contextlib import ExitStack

import numpy as np

import concourse.bass as bass
from concourse import mybir

ALU = mybir.AluOpType
ACT = mybir.ActivationFunctionType
AX = mybir.AxisListType
F32 = mybir.dt.float32
U32 = mybir.dt.uint32
I32 = mybir.dt.int32
F32R = mybir.dt.float32r

P = 128
NSEQ, S, D = 8, 256, 512
T = NSEQ * S
NT = S // P
KC = D // P
EPS = 1e-5

HEADS = 16
HD = D // HEADS
HPC = P // HD
WINDOW = 64
QK_SCALE = float(np.float32(HD ** -0.5))
SCORE_CLIP = 50.0
ROOT_HD = float(np.float32(HD ** 0.5))
NEG = -1e30
BAND = S - P + WINDOW

E, M, TOPK = 64, 352, 6
NG, TG = 8, 3
EPG = E // NG
CAP = 192
MS = 704
MS_CHUNKS = [(m, min(P, MS - m)) for m in range(0, MS, P)]
M_CHUNKS = [(m, min(P, M - m)) for m in range(0, M, P)]
C_TILES = [(0, P), (P, CAP - P)]
PRODUCTS = ((0, 0), (0, 1), (1, 0))
DROPPED = 1 << 15

TURN_SEMS = """
stats_ready rstd_ready normed_ready rowsT_psum colsT_ready dve_link pool_link attn_ready out_psum
resid_ready
""".split()
TURN_SEMS_1 = """
beta_added
attn_quarters xattn_quarters
qk_proj qk_raw_ready rope_cos_ready rot_psum rope_ready v_psum v_ready scores_psum masked_ready
negmax_ready probs_ready probsT_psum probsT_ready pv_psum xk_psum xk_ready xv_psum xv_ready xq_psum
xq_ready xs_psum clipped_ready xprobs_ready xpv_psum xattn_ready delta_psum router_psum negmax_router
exp_router gate_psum tanh_ready act_sh_ready down_psum shared_ready route_ready sel_ready pos_psum
slot_ready clip_bounds
""".split()
TURN_SEMS_3 = """
h_hi_ready h_lo_ready cx_hi_ready cx_lo_ready snormed_act snormed_dve srec_ready
xbc_psum xbc_raw_ready conv_ready convtanh_ready xbc_ready z_psum ztanh_ready zs_ready dt_psum
dtabs_ready dtexp_ready dtone_ready dtln_ready dA_ready tri_ready bc_psum decay_psum decay_ready
decaymask_ready w_ready xrows_psum xrows_ready xdt_ready y_psum gated_ready sumsq_ready gated_norm
s_psum smax_ready snegmax_ready sexp_ready sT_psum sT_act sT_dve ret_psum moe_psum
moe_negmax moe_exp mask_rows maskT_psum maskT_ready t1_psum m0_ready base_psum gelu0_ready base1_psum
gelu1_ready ca_ready mix_ready t2_psum t2m_ready y_out_psum x_out_ready yk_used
""".split()


class Sync:

    def __init__(self, nc, ctx):
        self.nc, self.ctx, self.by_name, self.counts = nc, ctx, {}, {}
        shared = TURN_SEMS_1 if len(TURN_SEMS_1) > len(TURN_SEMS_3) else TURN_SEMS_3
        for name in TURN_SEMS + shared:
            self[name]
        for one, three in zip(TURN_SEMS_1, TURN_SEMS_3):
            self.by_name[one] = self.by_name[three] = self.by_name[one if shared is TURN_SEMS_1 else three]
        nums = [self.by_name[n].num for n in TURN_SEMS + shared]
        assert nums == list(range(nums[0], nums[0] + len(nums)))
        self.turn_range = range(nums[0], nums[0] + len(nums))

    def __getitem__(self, name):
        if name not in self.by_name:
            self.by_name[name] = self.ctx.enter_context(self.nc.semaphore(name))
        return self.by_name[name]

    def link(self, eng, name, ins):
        self.counts[name] = self.counts.get(name, 0) + 1
        ins.then_inc(self[name], 1)
        eng.wait_ge(self[name], self.counts[name])

    def end_turn(self, eng, i, base, chain=None):
        if chain is not None:
            self.counts[chain] = 0
        eng.drain().then_inc(self["turn_done"], 1)
        eng.wait_ge(self["turn_go"], i + (base + 1))

    def clear_turn(self, sp, i, base):
        self.alone(sp)
        sp.wait_ge(self["turn_done"], (i + (base + 1)) * 4)
        self.alone(sp)
        sp.sem_clear(self.turn_range)
        sp.sem_inc(self["turn_go"], 1)
        sp.wait_ge(self["turn_go"], i + (base + 1))
        self.alone(sp)

    def alone(self, eng):
        eng.sem_inc(self["passed"], 1)


def layernorm_stats(dve, sy, src, st, mv, before=None):
    for j in range(NT):
        if before is not None:
            before(j)
        sy.link(dve, "dve_link", dve.bn_stats(st[:, j, :], src[:, j, :]))
        dve.bn_aggr(mv[:, j, :], st[:, j, :]).then_inc(sy["stats_ready"], 1)


def layernorm_apply(dve, sy, k, src, dst, mv, rstd):
    for j in range(NT):
        dve.wait_ge(sy["rstd_ready"], NT * k + j + 1)
        dve.tensor_scalar(dst[:, j, :], src[:, j, :], mv[:, j, 0:1], rstd[:, j:j + 1],
                          ALU.subtract, ALU.mult).then_inc(sy["normed_ready"], 1)


def layernorm_rows(dve, sy, k, src, dst, st, mv, rstd, before=None):
    layernorm_stats(dve, sy, src, st, mv, before)
    layernorm_apply(dve, sy, k, src, dst, mv, rstd)


def rstd_pool(pool, sy, k, mv, ve, rstd, minus_half):
    for j in range(NT):
        pool.wait_ge(sy["stats_ready"], NT * k + j + 1)
        sy.link(pool, "pool_link", pool.tensor_scalar(ve[:, j:j + 1], mv[:, j, 1:2], EPS, None, ALU.add))
        pool.tensor_tensor(rstd[:, j:j + 1], ve[:, j:j + 1], minus_half[:, 0:1], ALU.pow
                           ).then_inc(sy["rstd_ready"], 1)


def transposes_pe(pe, ident, src, bank, j):
    for kc in range(KC):
        ins = pe.transpose(bank[:, kc * P:(kc + 1) * P], src[:, j, kc * P:(kc + 1) * P], ident)
    return ins


def project_pe(pe, out, lhs_of, rhs_of, chunks=KC):
    for kc in range(chunks):
        ins = pe.matmul(out, lhs_of(kc), rhs_of(kc), start=(kc == 0), stop=(kc == chunks - 1))
    return ins


def phase1(nc, sy, const, dr, base, nseq=NSEQ):
    with ExitStack() as ctx:
        def sb(name, shape, dt=F32):
            return ctx.enter_context(nc.sbuf_tensor(name, shape, dt))

        w_qkv = sb("w_qkv", [P, KC, 3 * D])
        w_out = sb("w_out", [P, KC, D])
        w_x = {n: sb(f"w_x{n}", [P, KC, D]) for n in "qkvo"}
        w_gate = sb("w_gate", [P, KC, E])
        w_sg = sb("w_sg", [P, KC, MS])
        w_su = sb("w_su", [P, KC, MS])
        w_sd = sb("w_sd", [P, len(MS_CHUNKS), D])
        cosT, sinT = sb("cosT", [P, S]), sb("sinT", [P, S])
        rot = sb("rot", [P, P])
        wmask = sb("wmask", [P, P + BAND])
        bq, bk = sb("bq", [P, KC]), sb("bk", [P, KC])
        rows_bc = sb("rows_bc", [P, 4, D])
        rs, rs_bo = sb("rs", [P, 1]), sb("rs_bo", [P, D])
        mask_i = sb("mask_i", [P, NT], I32)
        hi = sb("hi", [P, NT])
        iota8, iota64 = const["iota"][:, 0:NG], const["iota"][:, 0:E]

        x = sb("x", [P, NT, D])
        xn = sb("xn", [P, NT, D])
        h = sb("h", [P, NT, D])
        hT = sb("hT", [P, KC, S])
        ctxT = sb("ctxT", [P, KC, S])
        qk_raw = sb("qk_raw", [P, 2 * KC, S])
        qk = sb("qk", [P, 2 * KC, S])
        hn = qk_raw[:, 0:KC, :].rearrange("p (t c) s -> p t (c s)", t=NT)
        xkT = sb("xkT", [P, KC, S])
        cosq, sinq = sb("cosq", [P, 2, S]), sb("sinq", [P, 2, S])
        v, xv = sb("v", [P, NT, D]), sb("xv", [P, NT, D])
        masked = sb("masked", [P, 2, P + BAND])
        probs = sb("probs", [P, 2, P + S])
        probsT = sb("probsT", [P, 2, P + S])
        smax, negmax = sb("smax", [P, HEADS, NT]), sb("negmax", [P, HEADS, NT])
        clipped, xprobs = sb("clipped", [P, 2, NT, S]), sb("xprobs", [P, 2, NT, S])
        o = sb("o", [P, NT, D])
        oT = hT
        rec, den = sb("rec", [P, 2, S]), sb("den", [P, 2, S])
        st, mv = sb("st", [P, NT, 6]), sb("mv", [P, NT, 2])
        ve, rstd = sb("ve", [P, NT]), sb("rstd", [P, NT])
        ex = sb("ex", [P, NT, E])
        sc, tsc = sb("sc", [P, NT, E]), sb("tsc", [P, NT, E])
        rm, rsum, rrec = sb("rm", [P, NT]), sb("rsum", [P, NT]), sb("rrec", [P, NT])
        gs, gtop, gmask = sb("gs", [P, NT, NG]), sb("gtop", [P, NT, 8]), sb("gmask", [P, NT, NG])
        gidx, gidxf = sb("gidx", [P, NT, 8], U32), sb("gidxf", [P, NT, 8])
        etop = sb("etop", [P, NT, 8])
        eidx, eidxf = sb("eidx", [P, NT, 8], U32), sb("eidxf", [P, NT, 8])
        sel, pos, junk = sb("sel", [P, NT, E]), sb("pos", [P, NT, E]), sb("junk", [P, E])
        taken = sb("taken", [P, NT, E])
        carry = sb("carry", [P, E])
        last = const["last"]
        slot_v, over = sb("slot_v", [P, NT, 8]), sb("over", [P, NT, 8])
        slot_w, slot_r = sb("slot_w", [P, NT, 8], I32), sb("slot_r", [P, NT, 8], I32)
        tok_f, tok_i = sb("tok_f", [P, NT]), sb("tok_i", [P, NT], I32)
        ebase = sb("ebase", [P, E])
        zeros = sb("zeros", [P, E * CAP // P], I32)
        th = sb("th", [P, 2, S])
        shT = qk[:, 0:len(MS_CHUNKS), :]

        ident, bank = const["ident"], const["bank"]

        def attended(c):
            return bank(4 + c % 2)[:, 0:S], bank(4 + c % 2)[:, S:2 * S]

        def values_pe(pe, hh, values, terms):
            r = (hh % HPC) * HD
            for which, out in enumerate(attended(hh // HPC)):
                for kt, (probabilities, q0) in enumerate(terms):
                    lhs = values[:, kt, hh * HD:(hh + 1) * HD] if which == 0 else const["ones"][:, 0:HD]
                    ins = pe.matmul(out[r:r + HD, q0:S], lhs, probabilities, start=(kt == 0),
                                    stop=(kt == len(terms) - 1), tile_position=(0, r), skip_group_check=True)
            return ins

        def gate_bank(n):
            return bank((2, 3, 0, 1)[n % 4])

        W1A, W1B = 16 * (KC + 7), 16 * 11
        block = ctx.enter_context(nc.Block())

        @block.sync
        def _(sp):
            def load_x(i):
                sp.dma_start(xn[:], dr["x"][bass.ds(i, 1)].rearrange("o p t d -> (o p) t d")
                             ).then_inc(sy["x_in"], 16)

            def load_ctx(i):
                sp.dma_start(ctxT[:], dr["ctxT"][bass.ds(i, 1)].rearrange("o p t d -> (o p) t d")
                             ).then_inc(sy["ctx_in"], 16)
                sp.dma_start(mask_i[:], dr["mask"][bass.ds(i, 1)].rearrange("o p t -> (o p) t")
                             ).then_inc(sy["mask_in"], 16)

            load_x(0)
            for kc in range(KC):
                sp.dma_start(w_qkv[:, kc, :], dr["w_qkv"][:, kc, :]).then_inc(sy["w1_in"], 16)
            for dst, src in ((cosT, "cosT"), (sinT, "sinT"), (rot, "rot"), (wmask, "wmask"), (rs, "rs"),
                             (bk, "bk"), (w_x["k"], "w_xk")):
                sp.dma_start(dst[:], dr[src]).then_inc(sy["w1_in"], 16)
            load_ctx(0)
            for dst, src in ((bq, "bq"), (rows_bc, "rows_bc"), (w_x["v"], "w_xv"),
                             (w_out, "w_out"), (w_x["q"], "w_xq"), (w_x["o"], "w_xo"), (w_gate, "w_gate"),
                             (w_sg, "w_sg"), (w_su, "w_su")):
                sp.dma_start(dst[:], dr[src]).then_inc(sy["w1b_in"], 16)
            n_full = MS // P
            sp.dma_start(w_sd[:, 0:n_full, :], dr["w_sd"][0:n_full * P].rearrange("(c p) n -> p c n", p=P)
                         ).then_inc(sy["w1b_in"], 16)
            sp.dma_start(w_sd[0:MS - n_full * P, n_full, :], dr["w_sd"][n_full * P:MS]).then_inc(sy["w1b_in"], 16)
            sp.sem_inc(sy["mid_out"], 1)
            sp.sem_inc(sy["rows_out"], 1)
            sy.clear_turn(sp, 0, base)

            def turn(i, more):
                if more:
                    sp.wait_ge(sy["resid_ready"], NT)
                    load_x(i + 1)
                    sp.wait_ge(sy["xv_psum"], NT)
                    sp.wait_ge(sy["clip_bounds"], 1)
                    load_ctx(i + 1)
                sp.wait_ge(sy["normed_ready"], 2 * NT)
                sp.dma_start(dr["normed_rows"][bass.ds(i, 1)].rearrange("o (t p) d -> (o p) t d", p=P),
                             h[:]).then_inc(sy["rows_out"], 16)
                sp.wait_ge(sy["route_ready"], 2)
                sp.dma_start(dr["route_w"][bass.ds(i, 1)].rearrange("o p t k -> (o p) t k"), etop[:]
                             ).then_inc(sy["rows_out"], 16)
                sp.wait_ge(sy["slot_ready"], 2)
                sp.dma_start(dr["slots"][bass.ds(i, 1)].rearrange("o p t k -> (o p) t k"), slot_r[:]
                             ).then_inc(sy["rows_out"], 16)
                sp.wait_ge(sy["shared_ready"], 2)
                sp.dma_start(dr["mid"][bass.ds(i, 1)].rearrange("o p t d -> (o p) t d"), o[:]
                             ).then_inc(sy["mid_out"], 16)
                sy.clear_turn(sp, i, base + 1)

            with sp.Fori(0, nseq - 1) as i:
                turn(i, True)
            turn(nseq - 1, False)
            sp.wait_ge(sy["rows_out"], nseq * 48 + 1)
            sp.wait_ge(sy["mid_out"], nseq * 16 + 1)

        @block.gpsimd
        def _(pool):
            pool.memset(probs[:, :, P:P + WINDOW], 0.0).then_inc(sy["init1"], 1)
            pool.iota(ebase[:], pattern=[[CAP, E]], base=0, channel_multiplier=0,
                      allow_small_or_imprecise_dtypes=True)
            pool.iota(tok_f[:], pattern=[[P, NT]], base=0, channel_multiplier=1,
                      allow_small_or_imprecise_dtypes=True)
            pool.memset(carry[:], 0.0)
            pool.memset(slot_v[:], 0.0)
            pool.memset(last, 0.0).then_inc(sy["init1"], 1)
            pool.memset(slot_w[:], E * CAP)
            pool.memset(tok_i[:], 0)
            pool.memset(zeros[:], 0).then_inc(sy["zeros_set"], 1)
            pool.wait_ge(sy["zeros_set"], 1)
            pool.dma_start(dr["slot_token"].rearrange("(p c) o -> p (c o)", p=P), zeros[:]
                           ).then_inc(sy["zeros_out"], 16)
            pool.wait_ge(sy["zeros_out"], 16)
            rstd_pool(pool, sy, 0, mv, ve, rstd, const["minus_half"])
            pool.wait_ge(sy["w1_in"], W1A)
            sy.end_turn(pool, 0, base, "pool_link")

            def scatter(last=False):
                for j in range(NT):
                    if last:
                        pool.wait_ge(sy["slot_ready"], j + 1)
                    for k in range(TOPK):
                        pool.indirect_dma_start(
                            out=dr["slot_token"], out_offset=bass.IndirectOffsetOnAxis(ap=slot_w[:, j, k:k + 1], axis=0),
                            in_=tok_i[:, j:j + 1], in_offset=None, bounds_check=E * CAP - 1, oob_is_err=False
                        ).then_inc(sy["scattered"], 16)

            def turn(i, more):
                for c in range(2 * KC):
                    pool.wait_ge(sy["qk_raw_ready"], c + 1)
                    if c >= 2:
                        pool.wait_ge(sy["rope_ready"], c - 1)
                    pool.tensor_tensor(cosq[:, c % 2, :], qk_raw[:, c, :], cosT[:], ALU.mult
                                       ).then_inc(sy["rope_cos_ready"], 1)
                for hh in range(HEADS):
                    pool.wait_ge(sy["masked_ready"], 2 * hh + 2)
                    pool.tensor_scalar(negmax[:, hh, :], smax[:, hh, :], -QK_SCALE, None, ALU.mult
                                       ).then_inc(sy["negmax_ready"], 1)
                pool.wait_ge(sy["mask_in"], (i + 1) * 16)
                sy.alone(pool)
                sy.link(pool, "pool_link", pool.tensor_copy(hi[:], mask_i[:]))
                sy.link(pool, "pool_link", pool.tensor_scalar(hi[:], hi[:], 0.5, None, ALU.is_gt))
                pool.tensor_scalar(hi[:], hi[:], 2 * SCORE_CLIP * ROOT_HD, -SCORE_CLIP * ROOT_HD,
                                   ALU.mult, ALU.add).then_inc(sy["clip_bounds"], 1)
                scatter()
                for k in (0, 1, 2, 3) if more else (0, 1, 2):
                    if k == 1:
                        pool.wait_ge(sy["scattered"], (i + 1) * (16 * NT * TOPK))
                        sy.alone(pool)
                        pool.wait_ge(sy["w1b_in"], W1B)
                        pool.tensor_scalar(rs_bo[:], rows_bc[:, 1, :], rs[:, 0:1], None, ALU.mult)
                        pool.wait_ge(sy["normed_ready"], NT)
                        for j in range(NT):
                            ins = pool.tensor_tensor(x[:, j, :], x[:, j, :], rows_bc[:, 3, :], ALU.add)
                        ins.then_inc(sy["beta_added"], 1)
                    rstd_pool(pool, sy, k, mv, ve, rstd, const["minus_half"])
                if not more:
                    scatter(last=True)
                sy.end_turn(pool, i, base + 1, "pool_link")

            with pool.Fori(0, nseq - 1) as i:
                turn(i, True)
            turn(nseq - 1, False)
            pool.wait_ge(sy["scattered"], (nseq + 1) * (16 * NT * TOPK))

        @block.scalar
        def _(act):
            def cols_copy(k):
                for j in range(NT):
                    act.wait_ge(sy["rowsT_psum"], NT * k + j + 1)
                    act.activation(hT[:, :, j * P:(j + 1) * P],
                                   bank(j)[:, :].rearrange("p (c t) -> p c t", c=KC), ACT.Copy
                                   ).then_inc(sy["colsT_ready"], 1)

            def keys_copy():
                for c in range(KC):
                    act.wait_ge(sy["xk_psum"], c + 1)
                    act.activation(xkT[:, c, :], bank(6 + c % 2)[:, 0:S], ACT.Identity, bias=bk[:, c:c + 1]
                                   ).then_inc(sy["xk_ready"], 1)

            cols_copy(0)
            act.wait_ge(sy["w1_in"], W1A)
            keys_copy()
            act.wait_ge(sy["init1"], 2)
            sy.end_turn(act, 0, base)

            def turn(i, more):
                for c in range(2 * KC):
                    act.wait_ge(sy["qk_proj"], c + 1)
                    act.activation(qk_raw[:, c, :], bank(2 + c % 2)[:, 0:S], ACT.Copy
                                   ).then_inc(sy["qk_raw_ready"], 1)
                for j in range(NT):
                    act.wait_ge(sy["v_psum"], j + 1)
                    act.activation(v[:, j, :], bank(6 + j)[:, :], ACT.Copy).then_inc(sy["v_ready"], 1)
                for hh in range(HEADS):
                    act.wait_ge(sy["negmax_ready"], hh + 1)
                    if hh >= 2:
                        act.wait_ge(sy["probsT_psum"], hh - 1)
                    act.activation(probs[:, hh % 2, 0:P], masked[:, hh % 2, 0:P], ACT.Exp,
                                   bias=negmax[:, hh, 0:1], scale=QK_SCALE)
                    act.activation(probs[:, hh % 2, P + WINDOW:P + S], masked[:, hh % 2, P:P + BAND], ACT.Exp,
                                   bias=negmax[:, hh, 1:2], scale=QK_SCALE).then_inc(sy["probs_ready"], 1)
                act.wait_ge(sy["w1b_in"], W1B)
                cols_copy(0)
                for c in range(KC):
                    act.wait_ge(sy["xq_psum"], c + 1)
                    act.activation(qk[:, c, :], bank(6 + c % 2)[:, 0:S], ACT.Identity, bias=bq[:, c:c + 1]
                                   ).then_inc(sy["xq_ready"], 1)
                for hh in range(HEADS):
                    act.wait_ge(sy["clipped_ready"], 2 * hh + 2)
                    if hh >= 2:
                        act.wait_ge(sy["xpv_psum"], hh - 1)
                    act.activation(xprobs[:, hh % 2], clipped[:, hh % 2], ACT.Exp, scale=1.0 / ROOT_HD
                                   ).then_inc(sy["xprobs_ready"], 1)
                if more:
                    keys_copy()
                cols_copy(1)
                for j in range(NT):
                    act.wait_ge(sy["negmax_router"], j + 1)
                    act.activation(ex[:, j, :], bank(6 + j)[:, 0:E], ACT.Exp, bias=rm[:, j:j + 1],
                                   accum_out=rsum[:, j:j + 1]).then_inc(sy["exp_router"], 1)
                for n, (m, w) in enumerate(MS_CHUNKS):
                    act.wait_ge(sy["gate_psum"], n + 1)
                    if n >= 2:
                        act.wait_ge(sy["act_sh_ready"], n - 1)
                    act.activation(th[0:w, n % 2, :], gate_bank(n)[0:w, 0:S], ACT.Tanh, scale=0.5
                                   ).then_inc(sy["tanh_ready"], 1)
                if more:
                    cols_copy(2)
                sy.end_turn(act, i, base + 1)

            with act.Fori(0, nseq - 1) as i:
                turn(i, True)
            turn(nseq - 1, False)

        @block.tensor
        def _(pe):
            def rows_to_cols(src, ready, at):
                for j in range(NT):
                    pe.wait_ge(ready, at + j + 1)
                    transposes_pe(pe, ident, src, bank(j), j).then_inc(sy["rowsT_psum"], 1)

            def keys(chunks):
                for c in chunks:
                    if c >= 2:
                        pe.wait_ge(sy["xk_ready"], c - 1)
                    project_pe(pe, bank(6 + c % 2)[:, 0:S], lambda kc: w_x["k"][:, kc, c * P:(c + 1) * P],
                               lambda kc: ctxT[:, kc, :]).then_inc(sy["xk_psum"], 1)

            rows_to_cols(hn, sy["normed_ready"], 0)
            pe.wait_ge(sy["w1_in"], W1A)
            pe.wait_ge(sy["ctx_in"], 16)
            keys(range(KC))
            pe.wait_ge(sy["init1"], 2)
            sy.end_turn(pe, 0, base)

            def turn(i, more):
                for c in range(2 * KC + 1):
                    if c < 2 * KC:
                        if c >= 2:
                            pe.wait_ge(sy["qk_raw_ready"], c - 1)
                        project_pe(pe, bank(2 + c % 2)[:, 0:S], lambda kc: w_qkv[:, kc, c * P:(c + 1) * P],
                                   lambda kc: hT[:, kc, :]).then_inc(sy["qk_proj"], 1)
                    if c >= 1:
                        pe.wait_ge(sy["qk_raw_ready"], c)
                        if c >= 3:
                            pe.wait_ge(sy["rope_ready"], c - 2)
                        pe.matmul(bank(4 + (c - 1) % 2)[:, 0:S], rot[:], qk_raw[:, c - 1, :], start=True,
                                  stop=True).then_inc(sy["rot_psum"], 1)
                for j in range(NT):
                    project_pe(pe, bank(6 + j)[:, :], lambda kc: hT[:, kc, j * P:(j + 1) * P],
                               lambda kc: w_qkv[:, kc, 2 * D:3 * D]).then_inc(sy["v_psum"], 1)
                pe.wait_ge(sy["rope_ready"], 2 * KC)
                pe.wait_ge(sy["v_ready"], NT)
                for s in range(HEADS + 2):
                    if s < HEADS:
                        c, r = s // HPC, (s % HPC) * HD
                        if s >= 2:
                            pe.wait_ge(sy["masked_ready"], 2 * (s - 1))
                        q, k, b = qk[r:r + HD, c, :], qk[r:r + HD, KC + c, :], bank(s % 2)
                        pe.matmul(b[:, 0:P], q[:, 0:P], k[:, 0:P], start=True, stop=True)
                        pe.matmul(b[:, P:P + BAND], q[:, P:S], k[:, WINDOW:S], start=True, stop=True
                                  ).then_inc(sy["scores_psum"], 1)
                    if 1 <= s <= HEADS:
                        hh = s - 1
                        pe.wait_ge(sy["probs_ready"], hh + 1)
                        if hh >= 2:
                            pe.wait_ge(sy["probsT_ready"], hh - 1)
                        for b3 in range(3):
                            ins = pe.transpose(bank(2 + hh % 2)[:, b3 * P:(b3 + 1) * P],
                                               probs[:, hh % 2, b3 * P:(b3 + 1) * P], ident)
                        ins.then_inc(sy["probsT_psum"], 1)
                    if s >= 2:
                        hh = s - 2
                        pe.wait_ge(sy["probsT_ready"], hh + 1)
                        if hh % HPC == 0 and hh >= 2 * HPC:
                            pe.wait_ge(sy["attn_ready"], hh // HPC - 1)
                        values_pe(pe, hh, v, ((probsT[:, hh % 2, 0:S], 0), (probsT[:, hh % 2, S:S + P], P))
                                  ).then_inc(sy["pv_psum"], 1)
                def cross_values(j):
                    project_pe(pe, bank(2 + j)[:, :], lambda kc: ctxT[:, kc, j * P:(j + 1) * P],
                               lambda kc: w_x["v"][:, kc, :]).then_inc(sy["xv_psum"], 1)

                pe.wait_ge(sy["w1b_in"], W1B)
                pe.wait_ge(sy["probsT_ready"], HEADS)
                cross_values(0)
                pe.wait_ge(sy["attn_ready"], KC)
                for j in range(NT):
                    project_pe(pe, bank(4 + j)[:, :], lambda kc: oT[:, kc, j * P:(j + 1) * P],
                               lambda kc: w_out[:, kc, :]).then_inc(sy["out_psum"], 1)
                cross_values(1)
                pe.wait_ge(sy["masked_ready"], 2 * HEADS)
                rows_to_cols(h, sy["normed_ready"], 0)
                pe.wait_ge(sy["colsT_ready"], NT)
                for c in range(KC):
                    if c >= 2:
                        pe.wait_ge(sy["xq_ready"], c - 1)
                    project_pe(pe, bank(6 + c % 2)[:, 0:S], lambda kc: w_x["q"][:, kc, c * P:(c + 1) * P],
                               lambda kc: hT[:, kc, :]).then_inc(sy["xq_psum"], 1)
                pe.wait_ge(sy["xq_ready"], KC)
                pe.wait_ge(sy["xv_ready"], NT)
                for s in range(HEADS + 2):
                    if s < HEADS:
                        c, r, b = s // HPC, (s % HPC) * HD, bank(s % 4)
                        if s >= 4:
                            pe.wait_ge(sy["clipped_ready"], 2 * (s - 3))
                        for kt in range(NT):
                            ins = pe.matmul(b[:, kt * S:(kt + 1) * S], xkT[r:r + HD, c, kt * P:(kt + 1) * P],
                                            qk[r:r + HD, c, :], start=True, stop=True)
                        ins.then_inc(sy["xs_psum"], 1)
                    if s >= 2:
                        hh = s - 2
                        pe.wait_ge(sy["xprobs_ready"], hh + 1)
                        if hh % HPC == 0 and hh >= 2 * HPC:
                            pe.wait_ge(sy["xattn_ready"], hh // HPC - 1)
                        values_pe(pe, hh, xv, [(xprobs[:, hh % 2, kt, :], 0) for kt in range(NT)]
                                  ).then_inc(sy["xpv_psum"], 1)
                if more:
                    pe.wait_ge(sy["ctx_in"], (i + 2) * 16)
                    keys(range(2))
                pe.wait_ge(sy["xattn_ready"], KC)
                for j in range(NT):
                    project_pe(pe, bank(2 + j)[:, :], lambda kc: oT[:, kc, j * P:(j + 1) * P],
                               lambda kc: w_x["o"][:, kc, :]).then_inc(sy["delta_psum"], 1)
                if more:
                    keys(range(2, KC))
                rows_to_cols(h, sy["normed_ready"], NT)
                pe.wait_ge(sy["colsT_ready"], 2 * NT)
                if more:
                    pe.wait_ge(sy["xk_ready"], KC)
                for j in range(NT):
                    project_pe(pe, bank(6 + j)[:, 0:E], lambda kc: hT[:, kc, j * P:(j + 1) * P],
                               lambda kc: w_gate[:, kc, :]).then_inc(sy["router_psum"], 1)
                def counts(j):
                    pe.wait_ge(sy["sel_ready"], j + 1)
                    pe.matmul(bank(6 + j)[:, E:2 * E], const["tri_lt"], sel[:, j, :], start=True, stop=True)
                    pe.matmul(bank(6 + j)[:, 2 * E:3 * E], const["ones"], sel[:, j, :], start=True, stop=True
                              ).then_inc(sy["pos_psum"], 1)

                for n, (m, w) in enumerate(MS_CHUNKS):
                    if n >= 4:
                        pe.wait_ge(sy["act_sh_ready"], n - 3)
                    b = gate_bank(n)
                    project_pe(pe, b[0:w, 0:S], lambda kc: w_sg[:, kc, m:m + w], lambda kc: hT[:, kc, :])
                    project_pe(pe, b[0:w, S:2 * S], lambda kc: w_su[:, kc, m:m + w], lambda kc: hT[:, kc, :]
                               ).then_inc(sy["gate_psum"], 1)
                    if n == 3:
                        counts(0)
                counts(1)
                if more:
                    pe.wait_ge(sy["act_sh_ready"], 4)
                    rows_to_cols(hn, sy["normed_ready"], 2 * NT)
                for j in range(NT):
                    for n, (m, w) in enumerate(MS_CHUNKS):
                        if j == 0:
                            pe.wait_ge(sy["act_sh_ready"], n + 1)
                        ins = pe.matmul(bank(4 + j)[:, :], shT[0:w, n, j * P:(j + 1) * P], w_sd[0:w, n, :],
                                        start=(n == 0), stop=(n == len(MS_CHUNKS) - 1))
                    ins.then_inc(sy["down_psum"], 1)
                sy.end_turn(pe, i, base + 1)

            with pe.Fori(0, nseq - 1) as i:
                turn(i, True)
            turn(nseq - 1, False)

        @block.vector
        def _(dve):
            def ln(ins):
                sy.link(dve, "dve_link", ins)

            dve.wait_ge(sy["x_in"], 16)
            layernorm_rows(dve, sy, 0, xn, hn, st, mv, rstd)
            dve.wait_ge(sy["w1_in"], W1A)
            dve.wait_ge(sy["init1"], 2)
            ln(dve.tensor_scalar(rs[:], rs[:], 0.0, 0.3, ALU.max, ALU.min))
            sy.end_turn(dve, 0, base, "dve_link")

            def turn(i, more):
                for c in range(2 * KC):
                    dve.wait_ge(sy["rot_psum"], c + 1)
                    sy.link(dve, "dve_link", dve.tensor_tensor(sinq[:, c % 2, :], bank(4 + c % 2)[:, 0:S],
                                                               sinT[:], ALU.mult))
                    dve.wait_ge(sy["rope_cos_ready"], c + 1)
                    dve.tensor_tensor(qk[:, c, :], cosq[:, c % 2, :], sinq[:, c % 2, :], ALU.add
                                      ).then_inc(sy["rope_ready"], 1)
                def divide(s, done, ready, quarters, add_eps):
                    c, k = (s - 6) // HPC, (s - 6) % HPC
                    if s < 6 or c >= KC:
                        return
                    out, sums = attended(c)
                    if k == 0:
                        dve.wait_ge(sy[done], (c + 1) * HPC)
                        if add_eps:
                            ln(dve.tensor_scalar(den[:, c % 2], sums, 1e-8, None, ALU.mult))
                            ln(dve.tensor_tensor(den[:, c % 2], den[:, c % 2], sums, ALU.add))
                    part = slice(k * S // HPC, (k + 1) * S // HPC)
                    ins = dve.reciprocal(rec[:, c % 2, part], (den[:, c % 2] if add_eps else sums)[:, part])
                    ins.then_inc(sy[quarters], 1)
                    if k == HPC - 1:
                        dve.wait_ge(sy[quarters], (c + 1) * HPC)
                        dve.tensor_tensor(oT[:, c, :], out, rec[:, c % 2], ALU.mult).then_inc(sy[ready], 1)

                for s in range(HEADS + 6):
                    if s < HEADS:
                        dve.wait_ge(sy["scores_psum"], s + 1)
                        if s >= 2:
                            dve.wait_ge(sy["probs_ready"], s - 1)
                        for j, (a, w) in enumerate(((0, P), (P, BAND))):
                            dve.tensor_tensor_reduce(
                                out=masked[:, s % 2, a:a + w], in0=bank(s % 2)[:, a:a + w], in1=wmask[:, a:a + w],
                                scale=1.0, scalar=3 * NEG, op0=ALU.add, op1=ALU.max,
                                accum_out=smax[:, s, j:j + 1]).then_inc(sy["masked_ready"], 1)
                    if 1 <= s <= HEADS:
                        hh = s - 1
                        dve.wait_ge(sy["probsT_psum"], hh + 1)
                        if hh >= 2:
                            dve.wait_ge(sy["pv_psum"], hh - 1)
                        dve.tensor_copy(probsT[:, hh % 2], bank(2 + hh % 2)[:, 0:P + S]
                                        ).then_inc(sy["probsT_ready"], 1)
                    divide(s, "pv_psum", "attn_ready", "attn_quarters", False)
                dve.wait_ge(sy["mid_out"], i * 16 + 1)
                dve.wait_ge(sy["rows_out"], i * 48 + 1)
                sy.alone(dve)

                def residual(j):
                    dve.wait_ge(sy["out_psum"], j + 1)
                    dve.tensor_tensor(x[:, j, :], xn[:, j, :], bank(4 + j)[:, :], ALU.add
                                      ).then_inc(sy["resid_ready"], 1)
                    dve.wait_ge(sy["resid_ready"], j + 1)

                layernorm_rows(dve, sy, 0, x, h, st, mv, rstd, residual)
                dve.wait_ge(sy["w1b_in"], W1B)
                for j in range(NT):
                    dve.wait_ge(sy["xv_psum"], j + 1)
                    dve.tensor_tensor(xv[:, j, :], bank(2 + j)[:, :], rows_bc[:, 0, :], ALU.add
                                      ).then_inc(sy["xv_ready"], 1)
                dve.wait_ge(sy["clip_bounds"], 1)
                for s in range(HEADS + 6):
                    if s < HEADS:
                        hh = s
                        dve.wait_ge(sy["xs_psum"], hh + 1)
                        if hh >= 2:
                            dve.wait_ge(sy["xprobs_ready"], hh - 1)
                        for kt in range(NT):
                            dve.tensor_scalar(clipped[:, hh % 2, kt, :], bank(hh % 4)[:, kt * S:(kt + 1) * S],
                                              hi[:, kt:kt + 1], -SCORE_CLIP * ROOT_HD, ALU.min, ALU.max
                                              ).then_inc(sy["clipped_ready"], 1)
                    divide(s, "xpv_psum", "xattn_ready", "xattn_quarters", True)
                dve.wait_ge(sy["beta_added"], 1)

                def delta(j):
                    dve.wait_ge(sy["delta_psum"], j + 1)
                    ln(dve.scalar_tensor_tensor(out=h[:, j, :], in0=bank(2 + j)[:, :], scalar=rs[:, 0:1],
                                                in1=rs_bo[:], op0=ALU.mult, op1=ALU.add))

                def add_delta(j):
                    dve.wait_ge(sy["rstd_ready"], NT + j + 1)
                    ln(dve.scalar_tensor_tensor(out=x[:, j, :], in0=h[:, j, :], scalar=rstd[:, j:j + 1],
                                                in1=x[:, j, :], op0=ALU.mult, op1=ALU.add))

                layernorm_stats(dve, sy, h, st, mv, delta)
                for j in range(NT):
                    dve.wait_ge(sy["stats_ready"], NT + j + 1)
                    ins = dve.scalar_tensor_tensor(out=h[:, j, :], in0=h[:, j, :], scalar=mv[:, j, 0:1],
                                                   in1=rows_bc[:, 2, :], op0=ALU.subtract, op1=ALU.mult)
                ln(ins)
                layernorm_rows(dve, sy, 2, x, h, st, mv, rstd, add_delta)
                for j in range(NT):
                    dve.wait_ge(sy["router_psum"], j + 1)
                    sy.link(dve, "dve_link", dve.tensor_reduce(rm[:, j:j + 1], bank(6 + j)[:, 0:E], AX.X, ALU.max))
                    dve.tensor_scalar(rm[:, j:j + 1], rm[:, j:j + 1], -1.0, None, ALU.mult
                                      ).then_inc(sy["negmax_router"], 1)
                if more:
                    dve.wait_ge(sy["x_in"], (i + 2) * 16)
                    sy.alone(dve)
                    layernorm_rows(dve, sy, 3, xn, hn, st, mv, rstd)

                def shared(n):
                    m, w = MS_CHUNKS[n]
                    dve.wait_ge(sy["tanh_ready"], n + 1)
                    b = gate_bank(n)
                    ln(dve.scalar_tensor_tensor(out=shT[0:w, n, :], in0=th[0:w, n % 2, :], scalar=1.0,
                                                in1=b[0:w, 0:S], op0=ALU.add, op1=ALU.mult))
                    dve.tensor_tensor(shT[0:w, n, :], shT[0:w, n, :], b[0:w, S:2 * S], ALU.mult
                                      ).then_inc(sy["act_sh_ready"], 1)

                def route(j):
                    dve.wait_ge(sy["exp_router"], j + 1)
                    ln(dve.reciprocal(rrec[:, j:j + 1], rsum[:, j:j + 1]))
                    ln(dve.tensor_scalar(sc[:, j, :], ex[:, j, :], rrec[:, j:j + 1], None, ALU.mult))
                    ln(dve.tensor_reduce(gs[:, j, :], sc[:, j, :].rearrange("p (g e) -> p g e", g=NG), AX.X, ALU.max))
                    ln(dve.max(gtop[:, j, :], gs[:, j, :]))
                    ln(dve.max_index(gidx[:, j, :], gtop[:, j, :], gs[:, j, :]))
                    ln(dve.tensor_copy(gidxf[:, j, :], gidx[:, j, :]))
                    ln(dve.tensor_scalar(gmask[:, j, :], iota8, gidxf[:, j, 0:1], None, ALU.is_equal))
                    for g in range(1, TG):
                        ln(dve.scalar_tensor_tensor(out=gmask[:, j, :], in0=iota8, scalar=gidxf[:, j, g:g + 1],
                                                    in1=gmask[:, j, :], op0=ALU.is_equal, op1=ALU.add))
                    ln(dve.tensor_tensor(tsc[:, j, :].rearrange("p (g e) -> p g e", g=NG),
                                         sc[:, j, :].rearrange("p (g e) -> p g e", g=NG),
                                         gmask[:, j, :].unsqueeze(2).broadcast_to([P, NG, EPG]), ALU.mult))
                    ln(dve.max(etop[:, j, :], tsc[:, j, :]))
                    ln(dve.max_index(eidx[:, j, :], etop[:, j, :], tsc[:, j, :]))
                    dve.tensor_copy(eidxf[:, j, :], eidx[:, j, :]).then_inc(sy["route_ready"], 1)
                    dve.wait_ge(sy["route_ready"], j + 1)
                    ln(dve.tensor_scalar(sel[:, j, :], iota64, eidxf[:, j, 0:1], None, ALU.is_equal))
                    for k in range(1, TOPK):
                        ins = dve.scalar_tensor_tensor(out=sel[:, j, :], in0=iota64, scalar=eidxf[:, j, k:k + 1],
                                                       in1=sel[:, j, :], op0=ALU.is_equal, op1=ALU.add)
                        if k < TOPK - 1:
                            ln(ins)
                    ins.then_inc(sy["sel_ready"], 1)

                def slots(j):
                    dve.wait_ge(sy["pos_psum"], j + 1)
                    ln(dve.scalar_tensor_tensor(out=last, in0=sel[:, j, :], scalar=tok_f[:, j:j + 1], in1=last,
                                                op0=ALU.mult, op1=ALU.max))
                    ln(dve.tensor_tensor(pos[:, j, :], bank(6 + j)[:, E:2 * E], carry[:], ALU.add))
                    ln(dve.tensor_tensor(carry[:], carry[:], bank(6 + j)[:, 2 * E:3 * E], ALU.add))
                    ln(dve.tensor_scalar(taken[:, j, :], pos[:, j, :], float(CAP - 1), float(DROPPED), ALU.is_ge,
                                         ALU.mult))
                    ln(dve.scalar_tensor_tensor(out=pos[:, j, :], in0=pos[:, j, :], scalar=float(CAP - 1),
                                                in1=ebase[:], op0=ALU.min, op1=ALU.add))
                    ln(dve.tensor_tensor(pos[:, j, :], pos[:, j, :], taken[:, j, :], ALU.add))
                    for k in range(TOPK):
                        ln(dve.scalar_tensor_tensor(out=junk[:], in0=iota64, scalar=eidxf[:, j, k:k + 1],
                                                    in1=pos[:, j, :], op0=ALU.is_equal, op1=ALU.mult,
                                                    accum_out=slot_v[:, j, k:k + 1]))
                    ln(dve.tensor_scalar(over[:, j, :], slot_v[:, j, :], float(DROPPED), -float(DROPPED),
                                         ALU.is_ge, ALU.mult))
                    ln(dve.tensor_tensor(over[:, j, :], over[:, j, :], slot_v[:, j, :], ALU.add))
                    ln(dve.tensor_copy(slot_w[:, j, :], slot_v[:, j, :]))
                    ln(dve.tensor_copy(tok_i[:, j:j + 1], tok_f[:, j:j + 1]))
                    dve.tensor_copy(slot_r[:, j, :], over[:, j, :]).then_inc(sy["slot_ready"], 1)

                shared(0)
                shared(1)
                route(0)
                shared(2)
                route(1)
                shared(3)
                shared(4)
                slots(0)
                shared(5)
                slots(1)
                for j in range(NT):
                    dve.wait_ge(sy["down_psum"], j + 1)
                    dve.scalar_tensor_tensor(out=o[:, j, :], in0=bank(4 + j)[:, :], scalar=0.5, in1=x[:, j, :],
                                             op0=ALU.mult, op1=ALU.add).then_inc(sy["shared_ready"], 1)
                ln(dve.tensor_scalar(tok_f[:], tok_f[:], float(S), None, ALU.add))
                sy.end_turn(dve, i, base + 1, "dve_link")

            with dve.Fori(0, nseq - 1) as i:
                turn(i, True)
            turn(nseq - 1, False)


def phase2(nc, sy, const, dr, next_weights):
    with ExitStack() as ctx:
        def sb(name, shape, dt=F32):
            return ctx.enter_context(nc.sbuf_tensor(name, shape, dt))

        def parts(name, shape):
            return [[sb(f"{name}_{part}{b}", shape, F32R) for part in ("hi", "lo")] for b in range(2)]

        NM = len(M_CHUNKS)
        wgu = [sb(f"wgu{b}", [P, 2, KC, M]) for b in range(2)]
        wd = [sb(f"wd{b}", [P, NM, D]) for b in range(2)]
        wgu2, wd2 = parts("wgu", [P, 2, KC, M]), parts("wd", [P, NM, D])
        idx = [sb(f"idx{b}", [P, 2], I32) for b in range(2)]
        xg = [sb(f"xg{b}", [P, 2, D]) for b in range(2)]
        xT2 = parts("xT", [P, KC, CAP])
        th, act = sb("eth", [P, NM, CAP]), sb("eact", [P, NM, CAP])
        aT2 = parts("aT", [P, NM, CAP])
        yo = [sb(f"yo{b}", [P, 2, D]) for b in range(2)]
        last_c, last_i = sb("last_c", [E, 1]), sb("last_i", [E, 1], I32)
        ident, bank = const["ident"], const["bank"]
        slot_token, expert_out = dr["slot_token"], dr["expert_out"]
        rows = dr["normed_rows"].rearrange("n s d -> (n s) d")
        tail = M - (NM - 1) * P

        block = ctx.enter_context(nc.Block())

        def pairs(eng, step):
            step(0, 0, 0, True)
            step(1, 0, 1, True)
            with eng.Fori(1, E // 2 - 1) as n:
                step(n * 2, n, 0, False)
                step(n * 2 + 1, n, 1, False)
            step(E - 2, E // 2 - 1, 0, False)
            step(E - 1, E // 2 - 1, 1, False)

        def turned(t):
            return bank(t)[:, 0:2 * CAP].rearrange("p (c t) -> p c t", c=2)

        @block.sync
        def _(sp):
            def load_weights(e, b):
                sp.dma_start(wgu[b][:], dr["w_gu"][bass.ds(e, 1)].rearrange("o p t c m -> (o p) t c m")
                             ).then_inc(sy[f"ew_in{b}"], 16)
                sp.dma_start(wd[b][:, 0:NM - 1, :], dr["w_d"][bass.ds(e, 1), 0:(NM - 1) * P].rearrange(
                    "o (c p) n -> (o p) c n", p=P)).then_inc(sy[f"ew_in{b}"], 16)
                sp.dma_start(wd[b][0:tail, NM - 1, :], dr["w_d"][bass.ds(e, 1), (NM - 1) * P:M].rearrange(
                    "o p n -> (o p) n")).then_inc(sy[f"ew_in{b}"], 16)

            load_weights(0, 0)
            sp.wait_ge(sy["last_ready"], 1)
            sp.dma_start(slot_token.rearrange("(e c) o -> e (c o)", c=CAP)[:, CAP - 1:CAP], last_i[:],
                         allow_slow_non_contiguous=True
                         ).then_inc(sy["last_out"], 16)
            sp.wait_ge(sy["last_out"], 16)

            def step(e, n, b, first):
                if not first:
                    sp.wait_ge(sy[f"xg_in{b}"], n * 32)
                    sy.alone(sp)
                sp.dma_start(idx[b][:, 0:1], slot_token[bass.ds(e * CAP, P)]).then_inc(sy[f"idx_in{b}"], 16)
                sp.dma_start(idx[b][0:CAP - P, 1:2], slot_token[bass.ds(e * CAP + P, CAP - P)]
                             ).then_inc(sy[f"idx_in{b}"], 16)
                if not first:
                    sp.wait_ge(sy["wgu_lo"], (e - 1) * 2)
                    sy.alone(sp)
                    sp.wait_ge(sy["wd_lo"], e - 1)
                    sy.alone(sp)
                if not (first and b == 0):
                    load_weights(e, b)

            pairs(sp, step)
            for dst, src in next_weights:
                sp.dma_start(dst, src).then_inc(sy["w3_in"], 16)

        @block.gpsimd
        def _(pool):
            def gather(e, n, b, first):
                pool.wait_ge(sy[f"idx_in{b}"], n * 32 + 32)
                sy.alone(pool)
                if not first:
                    pool.wait_ge(sy["exT_psum"], e - 1)
                    sy.alone(pool)
                for t, (c0, w) in enumerate(C_TILES):
                    pool.indirect_dma_start(
                        out=xg[b][0:w, t, :], out_offset=None, in_=rows,
                        in_offset=bass.IndirectOffsetOnAxis(ap=idx[b][0:w, t:t + 1], axis=0)
                    ).then_inc(sy[f"xg_in{b}"], 16)

            def lo_parts(e, b, first):
                pool.wait_ge(sy["wd_hi"], e + 1)
                sy.alone(pool)
                if not first:
                    pool.wait_ge(sy["edown_psum"], e - 1)
                    sy.alone(pool)
                pool.tensor_tensor(wd2[b][1][:, 0:NM - 1, :], wd[b][:, 0:NM - 1, :],
                                   wd2[b][0][:, 0:NM - 1, :].bitcast(F32), ALU.subtract)
                pool.tensor_tensor(wd2[b][1][0:tail, NM - 1, :], wd[b][0:tail, NM - 1, :],
                                   wd2[b][0][0:tail, NM - 1, :].bitcast(F32), ALU.subtract).then_inc(sy["wd_lo"], 1)

            def step(e, n, b, first):
                if e is not E - 1:
                    gather(e + 1, n + b, 1 - b, first and b == 0)
                    lo_parts(e + 1, 1 - b, first and b == 0)

            gather(0, 0, 0, True)
            lo_parts(0, 0, True)
            pairs(pool, step)

        @block.scalar
        def _(act):
            def xT_copy(e, b):
                act.wait_ge(sy["exT_psum"], e + 1)
                for t in range(2):
                    ins = act.activation(xT2[b][0][:, 2 * t:2 * t + 2, :], turned(t), ACT.Copy)
                ins.then_inc(sy["exT_hi"], 1)

            def hi_gu(n, b):
                act.wait_ge(sy[f"ew_in{b}"], n * 48 + 48)
                for gu in range(2):
                    act.activation(wgu2[b][0][:, gu], wgu[b][:, gu], ACT.Copy).then_inc(sy["wgu_hi"], 1)

            def hi_down(b):
                act.activation(wd2[b][0][:, 0:NM - 1, :], wd[b][:, 0:NM - 1, :], ACT.Copy)
                act.activation(wd2[b][0][0:tail, NM - 1, :], wd[b][0:tail, NM - 1, :], ACT.Copy
                               ).then_inc(sy["wd_hi"], 1)

            def step(e, n, b, first):
                more = e is not E - 1
                if more:
                    hi_down(1 - b)
                for m, (m0, w) in enumerate(M_CHUNKS):
                    act.wait_ge(sy["egu_psum"], e * NM + (m + 1))
                    if not (first and b == 0):
                        act.wait_ge(sy["egate_ready"], e * NM + (m + 1 - NM))
                    act.activation(th[0:w, m, :], bank(2 + m)[0:w, 0:CAP], ACT.Tanh, scale=0.5
                                   ).then_inc(sy["etanh_ready"], 1)
                if more:
                    xT_copy(e + 1, 1 - b)
                if more and e is not E - 2:
                    hi_gu(n + 1, b)
                act.wait_ge(sy["edown_psum"], e + 1)
                if not first:
                    act.wait_ge(sy[f"eout{b}"], n * 32)
                for t, (c0, w) in enumerate(C_TILES):
                    ins = act.activation(yo[b][0:w, t, :], bank(5 + t)[0:w, :], ACT.Copy, scale=0.5)
                ins.then_inc(sy["eout_ready"], 1)
                act.wait_ge(sy["eout_ready"], e + 1)
                for t, (c0, w) in enumerate(C_TILES):
                    act.dma_start(expert_out[bass.ds(e * CAP + c0, w)], yo[b][0:w, t, :]).then_inc(sy[f"eout{b}"], 16)

            hi_gu(0, 0)
            hi_down(0)
            xT_copy(0, 0)
            hi_gu(0, 1)
            pairs(act, step)
            act.wait_ge(sy["eout0"], 16 * E)
            act.wait_ge(sy["eout1"], 16 * E)

        @block.tensor
        def _(pe):
            pe.transpose(bank(7)[0:E, 0:P], const["last"], ident).then_inc(sy["last_psum"], 1)

            def turn_rows(e, b, n, first):
                pe.wait_ge(sy[f"xg_in{b}"], n * 32 + 32)
                if not first:
                    pe.wait_ge(sy["exT_lo"], e)
                for kc in range(KC):
                    for t, (c0, w) in enumerate(C_TILES):
                        at = (kc % 2) * CAP + c0
                        ins = pe.transpose(bank(kc // 2)[:, at:at + w], xg[b][0:w, t, kc * P:(kc + 1) * P],
                                           ident[0:w, 0:w])
                ins.then_inc(sy["exT_psum"], 1)

            def step(e, n, b, first):
                pe.wait_ge(sy["wgu_lo"], e * 2 + 2)
                pe.wait_ge(sy["exT_lo"], e + 1)
                for m, (m0, w) in enumerate(M_CHUNKS):
                    if not (first and b == 0):
                        pe.wait_ge(sy["eact_ready"], e * NM + (m + 1 - NM))
                    for gu in range(2):
                        for i, (wp, xp) in enumerate(PRODUCTS):
                            for kc in range(KC):
                                ins = pe.matmul(bank(2 + m)[0:w, gu * CAP:(gu + 1) * CAP],
                                                wgu2[b][wp][:, gu, kc, m0:m0 + w], xT2[b][xp][:, kc, :],
                                                start=(i == 0 and kc == 0), stop=(i == 2 and kc == KC - 1))
                    ins.then_inc(sy["egu_psum"], 1)
                if e is not E - 1:
                    turn_rows(e + 1, 1 - b, n + b, False)
                pe.wait_ge(sy["wd_lo"], e + 1)
                for t, (c0, w) in enumerate(C_TILES):
                    if t == 0 and not (first and b == 0):
                        pe.wait_ge(sy["eout_ready"], e)
                    for m, (m0, mw) in enumerate(M_CHUNKS):
                        if t == 0:
                            pe.wait_ge(sy["eact_ready"], e * NM + (m + 1))
                        for i, (ap, wp) in enumerate(PRODUCTS):
                            ins = pe.matmul(bank(5 + t)[0:w, :], aT2[b][ap][0:mw, m, c0:c0 + w],
                                            wd2[b][wp][0:mw, m, :], start=(m == 0 and i == 0),
                                            stop=(m == NM - 1 and i == 2))
                ins.then_inc(sy["edown_psum"], 1)

            turn_rows(0, 0, 0, True)
            pairs(pe, step)

        @block.vector
        def _(dve):
            dve.wait_ge(sy["last_psum"], 1)
            sy.link(dve, "last_link", dve.tensor_reduce(last_c[:], bank(7)[0:E, 0:P], AX.X, ALU.max))
            dve.tensor_copy(last_i[:], last_c[:]).then_inc(sy["last_ready"], 1)

            def lo_gu(e, b, gu):
                dve.wait_ge(sy["wgu_hi"], e * 2 + (gu + 1))
                dve.tensor_tensor(wgu2[b][1][:, gu], wgu[b][:, gu], wgu2[b][0][:, gu].bitcast(F32), ALU.subtract
                                  ).then_inc(sy["wgu_lo"], 1)

            def xT_lo(e, b):
                dve.wait_ge(sy["exT_hi"], e + 1)
                for t in range(2):
                    ins = dve.tensor_tensor(xT2[b][1][:, 2 * t:2 * t + 2, :], turned(t),
                                            xT2[b][0][:, 2 * t:2 * t + 2, :].bitcast(F32), ALU.subtract)
                ins.then_inc(sy["exT_lo"], 1)

            def step(e, n, b, first):
                more = e is not E - 1
                if not first:
                    dve.wait_ge(sy["edown_psum"], e - 1)
                    sy.alone(dve)
                if more:
                    if not (first and b == 0):
                        dve.wait_ge(sy["edown_psum"], e)
                    lo_gu(e + 1, 1 - b, 0)
                for m, (m0, w) in enumerate(M_CHUNKS):
                    g, hi, lo = bank(2 + m), aT2[b][0][0:w, m, :], aT2[b][1][0:w, m, :]
                    at = e * NM + (m + 1)
                    dve.wait_ge(sy["etanh_ready"], at)
                    dve.scalar_tensor_tensor(out=act[0:w, m, :], in0=th[0:w, m, :], scalar=1.0,
                                             in1=g[0:w, 0:CAP], op0=ALU.add, op1=ALU.mult
                                             ).then_inc(sy["egate_ready"], 1)
                    dve.wait_ge(sy["egate_ready"], at)
                    dve.tensor_tensor(act[0:w, m, :], act[0:w, m, :], g[0:w, CAP:2 * CAP], ALU.mult
                                      ).then_inc(sy["eup_ready"], 1)
                    dve.wait_ge(sy["eup_ready"], at)
                    dve.tensor_copy(hi, act[0:w, m, :]).then_inc(sy["ehi_ready"], 1)
                    dve.wait_ge(sy["ehi_ready"], at)
                    dve.tensor_tensor(lo, act[0:w, m, :], hi.bitcast(F32), ALU.subtract
                                      ).then_inc(sy["eact_ready"], 1)
                if more:
                    xT_lo(e + 1, 1 - b)
                    lo_gu(e + 1, 1 - b, 1)

            for gu in range(2):
                lo_gu(0, 0, gu)
            xT_lo(0, 0)
            pairs(dve, step)


CONV = 4
MH = 4
XBC = D + 2 * P
NXBC = XBC // P
LH = 8
LD = S // LH
HPT = P // LD
LD_SCALE = float(np.float32(1.0) / np.sqrt(np.float32(LD)))
LE, LR, LK = 8, 16, 2
F = 2048
FC = F // P
SCALING = 2.0


def mixer_weights(nc, ctx, dr):
    shapes = {"w_in": [P, KC, D + XBC + MH], "small": [P, 64], "norm_bc": [P, D], "w_mo": [P, KC, D]}
    tiles = {n: ctx.enter_context(nc.sbuf_tensor(n, shape, F32)) for n, shape in shapes.items()}
    return tiles, [(t[:], dr[n]) for n, t in tiles.items()]


def phase3(nc, sy, const, dr, base, tiles, nseq=NSEQ):
    with ExitStack() as ctx:
        def sb(name, shape, dt=F32):
            return ctx.enter_context(nc.sbuf_tensor(name, shape, dt))

        w_in, w_mo, norm_bc, small = (tiles[n] for n in ("w_in", "w_mo", "norm_bc", "small"))
        w1 = sb("w1", [P, KC, F])
        w2 = sb("w2", [P, FC, D])
        a1 = sb("a1", [P, KC, P])
        b1l = sb("b1l", [P, F])
        a2 = sb("a2", [P, FC, P])
        b2l = sb("b2l", [P, D])
        wr = sb("wr", [P, KC, LE])
        bias2_bc = sb("bias2_bc", [P, D])
        conv_w = small[:, 0:24].rearrange("p (c k) -> p c k", k=CONV)
        conv_b = small[:, 24:30]
        dt_bias, a_log, d_skip = small[:, 32:36], small[:, 36:40], small[:, 40:44]
        gamma, br = small[:, 44:45], small[:, 48:56]
        bias1 = sb("bias1", [P, FC])
        neg_a = sb("neg_a", [P, MH])
        tri_gt = sb("tri_gt", [P, P])
        tri_le = sb("tri_le", [P, 3 * P])
        erow = sb("erow", [P, P])

        xn = sb("xn3", [P, NT, D])
        x, h, hT = sb("x3", [P, NT, D]), sb("h3", [P, NT, D]), sb("hT3", [P, KC, S])
        cx, cxT = sb("cx", [P, NT, D]), sb("cxT", [P, KC, S])
        zs = sb("zs", [P, NT, D])
        y = sb("y", [P, NT, D])
        h2 = [sb(f"h_{part}", [P, NT, D], F32R) for part in ("hi", "lo")]
        cx2 = [sb(f"cx_{part}", [P, NT, D], F32R) for part in ("hi", "lo")]
        yk = zs
        slots, wk = sb("slots3", [P, NT, 8], I32), sb("wk", [P, NT, 8])
        scratch = sb("scratch", [P, 8192])
        st, mv = sb("st3", [P, NT, 6]), sb("mv3", [P, NT, 2])
        ve, rstd = sb("ve3", [P, NT]), sb("rstd3", [P, NT])

        def view(at, *shape):
            n = int(np.prod(shape))
            names = "abcd"[:len(shape)]
            ap = scratch[:, at:at + n]
            if len(shape) == 1:
                return ap
            return ap.rearrange(f"p ({' '.join(names)}) -> p {' '.join(names)}",
                                **{k: v for k, v in zip(names[1:], shape[1:])})

        raw, convh = view(0, NXBC, S), view(1536, NXBC, S)
        xbc = raw
        cth = view(3072, 2, S)
        xr, xdt = view(3584, NT, P), view(3840, NT, MH, P)
        trid = view(4864, MH, 3, P)
        decay, wgt = view(6400, 2, 3 * P), view(7168, 2, 3 * P)
        dts = sb("dts", [P, 10, NT * MH])
        ssq, grstd = sb("ssq", [P, NT * MH]), sb("grstd", [P, NT * MH])
        yk0 = view(0, NT * TOPK, D)
        prob, probT = view(0, 2, 4, D), view(4096, 2, 4, D)
        smx, snm, ssum = sb("smx", [P, LH, 4]), sb("snm", [P, LH, 4]), sb("ssum", [P, LH, 4])
        mixT = view(0, FC, S)
        act2, ca = view(4096, 2, LK, S), view(5120, 3, LK, S)
        mrow = view(6656, NT, 4, P)
        maskT = sb("maskT", [P, 4, S])
        m0, m01, t2m, t2b = (y[:, k // 2, (k % 2) * S:(k % 2 + 1) * S] for k in range(4))
        lg = sb("lg", [P, NT, LE])
        lex, lpr, ltop, lidxf = (sb(n, [P, NT, 8]) for n in ("lex", "lpr", "ltop", "lidxf"))
        lidx = sb("lidx", [P, NT, 8], U32)
        lmax, lsum, lw = sb("lmax", [P, NT, 8]), sb("lsum", [P, NT]), sb("lw", [P, NT])

        ident, bank = const["ident"], const["bank"]

        def hidden(f):
            return bank((f + 2) % 4)[:, 0:S]

        def by_tile(per_head):
            return per_head[:].rearrange("p (t h) -> p t h", t=NT)

        def y_bank(hd, j):
            return bank(4 + hd)[:, j * P:(j + 1) * P]

        block = ctx.enter_context(nc.Block())
        GATHERS = NT * TOPK
        W3A, W3B = 16 * 4, 16 * 9

        @block.sync
        def _(sp):
            def load(i, *what):
                for dst, src, sem in what:
                    sp.dma_start(dst[:], dr[src][bass.ds(i, 1)].rearrange("o p t d -> (o p) t d")
                                 ).then_inc(sy[sem], 16)

            routes = ((slots, "slots", "slots_in"), (wk, "route_w", "wk_in"))
            rows = (xn, "mid", "x3_in"),
            context = (cx, "ctx", "ctx3_in"), (cxT, "ctxT", "ctx3_in")
            load(0, *routes, *rows)
            sp.wait_ge(sy["stats_ready"], NT)
            load(0, *context)
            for dst, src in ((bias1, "bias1"), (bias2_bc, "bias2_bc"), (wr, "wr"), (a1, "a1"), (b1l, "b1l"),
                             (a2, "a2"), (b2l, "b2l"), (w1, "w1"), (w2, "w2")):
                sp.dma_start(dst[:], dr[src]).then_inc(sy["w3b_in"], 16)
            sp.sem_inc(sy["out_done"], 1)
            sy.clear_turn(sp, 0, base)

            def turn(i, more):
                if more:
                    load(i + 1, *routes)
                    sp.wait_ge(sy["resid_ready"], NT)
                    load(i + 1, *rows)
                    sp.wait_ge(sy["ret_psum"], LH)
                    load(i + 1, *context)
                sp.wait_ge(sy["x_out_ready"], 2)
                sp.dma_start(dr["out"][bass.ds(i, 1)].rearrange("o (t p) d -> (o p) t d", p=P), x[:]
                             ).then_inc(sy["out_done"], 16)
                sy.clear_turn(sp, i, base + 1)

            with sp.Fori(0, nseq - 1) as i:
                turn(i, True)
            turn(nseq - 1, False)
            sp.wait_ge(sy["out_done"], nseq * 16 + 1)

        @block.gpsimd
        def _(pool):
            sy.link(pool, "init3_link", pool.memset(tri_le[:], 1.0))
            pool.affine_select(out=tri_le[:, 0:P], in_=tri_le[:, 0:P], compare_op=ALU.is_ge, fill=0.0, base=0,
                               pattern=[[1, P]], channel_multiplier=-1)
            pool.affine_select(out=tri_le[:, 2 * P:3 * P], in_=tri_le[:, 2 * P:3 * P], compare_op=ALU.is_ge,
                               fill=0.0, base=0, pattern=[[1, P]], channel_multiplier=-1)
            sy.link(pool, "init3_link", pool.memset(tri_gt[:], 1.0))
            pool.affine_select(out=tri_gt[:], in_=tri_gt[:], compare_op=ALU.is_gt, fill=0.0, base=0,
                               pattern=[[-1, P]], channel_multiplier=1)
            pool.iota(erow[:], pattern=[[1, LE], [0, LR]], base=0, channel_multiplier=0,
                      allow_small_or_imprecise_dtypes=True).then_inc(sy["init3"], 1)

            def gather(g, out):
                k, j = g // NT, g % NT
                pool.indirect_dma_start(
                    out=out, out_offset=None, in_=dr["expert_out"],
                    in_offset=bass.IndirectOffsetOnAxis(ap=slots[:, j, k:k + 1], axis=0)
                ).then_inc(sy[f"yk_in{j}"], 16)

            pool.wait_ge(sy["slots_in"], 16)
            for j in range(NT):
                for k in range(TOPK):
                    gather(NT * k + j, yk0[:, NT * k + j, :])
            rstd_pool(pool, sy, 0, mv, ve, rstd, const["minus_half"])
            sy.end_turn(pool, 0, base, "pool_link")

            def turn(i, more):
                pool.wait_ge(sy["dA_ready"], 1)
                da = dts[:, 9, :]
                for hd in range(MH):
                    for m, (src, t) in enumerate(((tri_gt[:], 0), (tri_gt[:], 1), (tri_le[:, P:2 * P], 1))):
                        ins = pool.tensor_scalar(trid[:, hd, m, :], src, da[:, t * MH + hd:t * MH + hd + 1], None,
                                                 ALU.mult)
                    ins.then_inc(sy["tri_ready"], 1)
                for hd in range(MH):
                    pool.wait_ge(sy["decay_ready"], hd + 1)
                    pool.tensor_tensor(decay[:, hd % 2, :], decay[:, hd % 2, :], tri_le[:], ALU.mult
                                       ).then_inc(sy["decaymask_ready"], 1)
                for hd in range(MH):
                    pool.wait_ge(sy["sumsq_ready"], hd + 1)
                    sums = by_tile(ssq)[:, :, hd]
                    sy.link(pool, "pool_link", pool.tensor_scalar(sums, sums, 1.0 / P, EPS, ALU.mult, ALU.add))
                    pool.tensor_tensor(by_tile(grstd)[:, :, hd], sums, const["minus_half"][:, 0:NT], ALU.pow
                                       ).then_inc(sy["gated_norm"], 1)
                pool.wait_ge(sy["cx_hi_ready"], 1)
                pool.tensor_tensor(cx2[1][:], cx[:], cx2[0][:].bitcast(F32), ALU.subtract).then_inc(sy["cx_lo_ready"], 1)
                rstd_pool(pool, sy, 0, mv, ve, rstd, const["minus_half"])
                for n in range(4 * LH):
                    hd, lc = n // 4, n % 4
                    pool.wait_ge(sy["smax_ready"], n + 1)
                    pool.tensor_scalar(snm[:, hd, lc:lc + 1], smx[:, hd, lc:lc + 1], -LD_SCALE, None, ALU.mult
                                       ).then_inc(sy["snegmax_ready"], 1)
                rstd_pool(pool, sy, 1, mv, ve, rstd, const["minus_half"])
                if more:
                    pool.wait_ge(sy["slots_in"], (i + 2) * 16)
                    sy.alone(pool)
                for f in range(FC):
                    if more and f < GATHERS:
                        if f >= 2:
                            pool.wait_ge(sy["yk_used"], f - 1)
                        gather(f, yk[:, f % 2, :])
                    if more and f == GATHERS + 2:
                        rstd_pool(pool, sy, 2, mv, ve, rstd, const["minus_half"])
                    pool.wait_ge(sy["ca_ready"], f + 1)
                    pool.tensor_tensor(mixT[:, f, :], ca[:, f % 3, 0, :], ca[:, f % 3, 1, :], ALU.add
                                       ).then_inc(sy["mix_ready"], 1)
                sy.end_turn(pool, i, base + 1, "pool_link")

            with pool.Fori(0, nseq - 1) as i:
                turn(i, True)
            turn(nseq - 1, False)

        @block.scalar
        def _(act):
            def cols_copy(k):
                for j in range(NT):
                    act.wait_ge(sy["rowsT_psum"], NT * k + j + 1)
                    act.activation(hT[:, :, j * P:(j + 1) * P],
                                   bank(j)[:, :].rearrange("p (c t) -> p c t", c=KC), ACT.Copy
                                   ).then_inc(sy["colsT_ready"], 1)

            act.wait_ge(sy["w3_in"], W3A)
            act.activation(neg_a[:], a_log, ACT.Exp).then_inc(sy["a_exp"], 1)
            cols_copy(0)
            sy.end_turn(act, 0, base)

            def turn(i, more):
                act.wait_ge(sy["dtabs_ready"], 1)
                act.activation(dts[:, 2, :], dts[:, 1, :], ACT.Exp, scale=-1.0).then_inc(sy["dtexp_ready"], 1)
                act.wait_ge(sy["dtone_ready"], 1)
                act.activation(dts[:, 4, :], dts[:, 3, :], ACT.Ln).then_inc(sy["dtln_ready"], 1)
                for c in range(NXBC + 1):
                    if c < NXBC:
                        act.wait_ge(sy["xbc_psum"], c + 1)
                        act.activation(raw[:, c, :], bank(2 + c % 2)[:, 0:S], ACT.Copy
                                       ).then_inc(sy["xbc_raw_ready"], 1)
                    if c >= 1:
                        act.wait_ge(sy["conv_ready"], c)
                        if c >= 3:
                            act.wait_ge(sy["xbc_ready"], c - 2)
                        act.activation(cth[:, (c - 1) % 2, :], convh[:, c - 1, :], ACT.Tanh
                                       ).then_inc(sy["convtanh_ready"], 1)
                for j in range(NT):
                    act.wait_ge(sy["z_psum"], j + 1)
                    act.activation(zs[:, j, :], bank(4 + j)[:, :], ACT.Tanh, scale=0.5
                                   ).then_inc(sy["ztanh_ready"], 1)
                act.wait_ge(sy["ctx3_in"], (i + 1) * 32)
                sy.alone(act)
                act.activation(cx2[0][:], cx[:], ACT.Copy).then_inc(sy["cx_hi_ready"], 1)
                act.wait_ge(sy["xrows_psum"], 1)
                act.activation(xr[:], bank(6)[:, 0:NT * P].rearrange("p (t d) -> p t d", t=NT), ACT.Copy
                               ).then_inc(sy["xrows_ready"], 1)
                act.wait_ge(sy["xrows_ready"], 1)
                act.wait_ge(sy["dA_ready"], 1)
                for t in range(NT):
                    for hd in range(MH):
                        ins = act.activation(xdt[:, t, hd, :], xr[:, t, :], ACT.Copy,
                                             scale=dts[:, 8, t * MH + hd:t * MH + hd + 1])
                ins.then_inc(sy["xdt_ready"], 1)
                for hd in range(MH):
                    act.wait_ge(sy["decay_psum"], hd + 1)
                    if hd >= 2:
                        act.wait_ge(sy["w_ready"], hd - 1)
                    act.activation(decay[:, hd % 2, :], bank(hd % 2)[:, 0:3 * P], ACT.Exp
                                   ).then_inc(sy["decay_ready"], 1)
                for hd in range(MH):
                    act.wait_ge(sy["gated_ready"], hd + 1)
                    for j in range(NT):
                        ins = act.activation(h[:, j, hd * P:(hd + 1) * P], y[:, j, hd * P:(hd + 1) * P], ACT.Square,
                                             accum_out=ssq[:, j * MH + hd:j * MH + hd + 1])
                    ins.then_inc(sy["sumsq_ready"], 1)
                cols_copy(0)
                for j in range(NT):
                    act.wait_ge(sy["normed_ready"], j + 1)
                    act.activation(h2[0][:, j, :], h[:, j, :], ACT.Copy).then_inc(sy["h_hi_ready"], 1)

                def copy_blocks(n):
                    act.wait_ge(sy["sT_psum"], n + 1)
                    hd, lc = n // 4, n % 4
                    act.activation(probT[:, hd % 2, :, lc * P:(lc + 1) * P],
                                   bank(4 + lc % 2)[:, :].rearrange("p (c t) -> p c t", c=4), ACT.Copy
                                   ).then_inc(sy["sT_act"], 1)

                for n in range(4 * LH + 4):
                    if n < 4 * LH:
                        hd, lc = n // 4, n % 4
                        act.wait_ge(sy["snegmax_ready"], n + 1)
                        if hd >= 2:
                            act.wait_ge(sy["sT_psum"], n - 7)
                        act.activation(prob[:, hd % 2, lc, :], bank(lc)[:, :], ACT.Exp, bias=snm[:, hd, lc:lc + 1],
                                       scale=LD_SCALE, accum_out=ssum[:, hd, lc:lc + 1]).then_inc(sy["sexp_ready"], 1)
                    if n >= 2 and n % 2 == 1 and n - 2 < 4 * LH:
                        m = n - 2
                        hd, lc = m // 4, m % 4
                        act.wait_ge(sy["srec_ready"], m // 2 + 1)
                        act.activation(prob[:, hd % 2, lc, :], prob[:, hd % 2, lc, :], ACT.Copy,
                                       scale=ssum[:, hd, lc:lc + 1]).then_inc(sy["snormed_act"], 1)
                    if n >= 4 and n % 2 == 0:
                        if (n - 4) % 4 == 0 and n >= 12:
                            act.wait_ge(sy["ret_psum"], (n - 4) // 4 - 1)
                        copy_blocks(n - 4)
                cols_copy(1)
                act.wait_ge(sy["w3b_in"], W3B)
                for j in range(NT):
                    act.wait_ge(sy["moe_negmax"], j + 1)
                    act.activation(lex[:, j, :], lg[:, j, :], ACT.Exp, bias=lw[:, j:j + 1],
                                   accum_out=lsum[:, j:j + 1]).then_inc(sy["moe_exp"], 1)
                for j in range(NT):
                    act.wait_ge(sy["maskT_psum"], j + 1)
                    act.activation(maskT[:, :, j * P:(j + 1) * P],
                                   bank(j)[:, :].rearrange("p (c t) -> p c t", c=4), ACT.Copy
                                   ).then_inc(sy["maskT_ready"], 1)
                for f in range(FC + 1):
                    if f < FC:
                        act.wait_ge(sy["base_psum"], f + 1)
                        if f >= 2:
                            act.wait_ge(sy["ca_ready"], f - 1)
                        act.activation(act2[:, f % 2, 0, :], hidden(f), ACT.Gelu_apprx_tanh,
                                       bias=bias1[:, f:f + 1]).then_inc(sy["gelu0_ready"], 1)
                    if f >= 1:
                        g = f - 1
                        act.wait_ge(sy["base1_psum"], g + 1)
                        act.activation(act2[:, g % 2, 1, :], hidden(g), ACT.Gelu_apprx_tanh,
                                       bias=bias1[:, g:g + 1]).then_inc(sy["gelu1_ready"], 1)
                if more:
                    cols_copy(2)
                sy.end_turn(act, i, base + 1)

            with act.Fori(0, nseq - 1) as i:
                turn(i, True)
            turn(nseq - 1, False)

        @block.tensor
        def _(pe):
            def rows_to_cols(src, ready, at):
                for j in range(NT):
                    pe.wait_ge(ready, at + j + 1)
                    transposes_pe(pe, ident, src, bank(j), j).then_inc(sy["rowsT_psum"], 1)

            rows_to_cols(h, sy["normed_ready"], 0)
            pe.wait_ge(sy["w3_in"], W3A)
            pe.wait_ge(sy["init3"], 1)
            sy.end_turn(pe, 0, base)

            def turn(i, more):
                for j in range(NT):
                    ins = project_pe(pe, bank(6)[:, j * MH:(j + 1) * MH], lambda kc: hT[:, kc, j * P:(j + 1) * P],
                                     lambda kc: w_in[:, kc, D + XBC:D + XBC + MH])
                ins.then_inc(sy["dt_psum"], 1)
                for c in range(NXBC):
                    if c >= 2:
                        pe.wait_ge(sy["xbc_raw_ready"], c - 1)
                    project_pe(pe, bank(2 + c % 2)[:, 0:S], lambda kc: w_in[:, kc, D + c * P:D + (c + 1) * P],
                               lambda kc: hT[:, kc, :]).then_inc(sy["xbc_psum"], 1)
                for j in range(NT):
                    project_pe(pe, bank(4 + j)[:, :], lambda kc: hT[:, kc, j * P:(j + 1) * P],
                               lambda kc: w_in[:, kc, 0:D]).then_inc(sy["z_psum"], 1)
                pe.wait_ge(sy["xbc_ready"], 1)
                pe.wait_ge(sy["tri_ready"], 1)
                for t in range(NT):
                    ins = pe.transpose(bank(6)[:, t * P:(t + 1) * P], xbc[:, 0, t * P:(t + 1) * P], ident)
                ins.then_inc(sy["xrows_psum"], 1)
                pe.wait_ge(sy["xbc_raw_ready"], NXBC)
                for s in range(MH + 1):
                    if s < MH:
                        pe.wait_ge(sy["xbc_ready"], s + 3)
                        pe.wait_ge(sy["tri_ready"], s + 1)
                        if s >= 2:
                            pe.wait_ge(sy["w_ready"], s - 1)
                        b, g = bank(s % 2), bank(2 + s % 2)
                        pe.matmul(b[:, 0:2 * P], trid[:, s, 0, :], tri_le[:, 0:2 * P], start=True, stop=False,
                                  skip_group_check=True)
                        pe.matmul(b[:, P:2 * P], trid[:, s, 2, :], tri_le[:, 0:P], start=False, stop=True,
                                  skip_group_check=True)
                        pe.matmul(b[:, 2 * P:3 * P], trid[:, s, 1, :], tri_le[:, 0:P], start=True, stop=True,
                                  skip_group_check=True).then_inc(sy["decay_psum"], 1)
                        pe.matmul(g[:, 0:2 * P], xbc[:, 1, 0:P], xbc[:, 2 + s, :], start=True, stop=True)
                        pe.matmul(g[:, 2 * P:3 * P], xbc[:, 1, P:S], xbc[:, 2 + s, P:S], start=True, stop=True
                                  ).then_inc(sy["bc_psum"], 1)
                    if s >= 1:
                        hd = s - 1
                        if hd == 0:
                            pe.wait_ge(sy["zs_ready"], NT)
                            pe.wait_ge(sy["xdt_ready"], 1)
                        pe.wait_ge(sy["w_ready"], hd + 1)
                        w = wgt[:, hd % 2, :]
                        pe.matmul(y_bank(hd, 0), w[:, 0:P], xdt[:, 0, hd, :], start=True, stop=True)
                        pe.matmul(y_bank(hd, 1), w[:, P:2 * P], xdt[:, 0, hd, :], start=True, stop=False)
                        pe.matmul(y_bank(hd, 1), w[:, 2 * P:3 * P], xdt[:, 1, hd, :], start=False, stop=True
                                  ).then_inc(sy["y_psum"], 1)
                rows_to_cols(y, sy["attn_ready"], 0)
                pe.wait_ge(sy["colsT_ready"], NT)
                for j in range(NT):
                    project_pe(pe, bank(2 + j)[:, :], lambda kc: hT[:, kc, j * P:(j + 1) * P],
                               lambda kc: w_mo[:, kc, :]).then_inc(sy["out_psum"], 1)
                pe.wait_ge(sy["ctx3_in"], (i + 1) * 32)
                pe.wait_ge(sy["cx_lo_ready"], 1)
                for n in range(4 * LH + 6):
                    if n < 4 * LH:
                        hd, lc = n // 4, n % 4
                        j, r = hd // HPT, (hd % HPT) * LD
                        pe.wait_ge(sy["h_lo_ready"], j + 1)
                        if n >= 4:
                            pe.wait_ge(sy["sexp_ready"], n - 3)
                        for m, (hp, cp) in enumerate(PRODUCTS):
                            ins = pe.matmul(bank(lc)[:, :], h2[hp][r:r + LD, j, lc * P:(lc + 1) * P],
                                            cx2[cp][r:r + LD, j, :], start=(m == 0), stop=(m == 2))
                        ins.then_inc(sy["s_psum"], 1)
                    if 4 <= n < 4 * LH + 4:
                        m = n - 4
                        hd, lc = m // 4, m % 4
                        pe.wait_ge(sy["snormed_act" if m % 2 else "snormed_dve"], m // 2 + 1)
                        if m >= 2:
                            pe.wait_ge(sy["sT_act" if m % 2 == 0 else "sT_dve"], m // 2)
                        for mc in range(4):
                            ins = pe.transpose(bank(4 + lc % 2)[:, mc * P:(mc + 1) * P],
                                               prob[:, hd % 2, lc, mc * P:(mc + 1) * P], ident)
                        ins.then_inc(sy["sT_psum"], 1)
                    if n >= 9 and (n - 9) % 4 == 0:
                        hd = (n - 9) // 4
                        j, r = hd // HPT, (hd % HPT) * LD
                        pe.wait_ge(sy["sT_act"], 2 * hd + 2)
                        pe.wait_ge(sy["sT_dve"], 2 * hd + 2)
                        for mc in range(4):
                            ins = pe.matmul(bank(6 + j)[r:r + LD, :], cxT[:, mc, hd * LD:(hd + 1) * LD],
                                            probT[:, hd % 2, mc, :], start=(mc == 0), stop=(mc == 3),
                                            tile_position=(0, r))
                        ins.then_inc(sy["ret_psum"], 1)
                rows_to_cols(h, sy["normed_ready"], NT)
                pe.wait_ge(sy["colsT_ready"], 2 * NT)
                pe.wait_ge(sy["w3b_in"], W3B)
                for j in range(NT):
                    ins = project_pe(pe, bank(4)[:, j * LE:(j + 1) * LE], lambda kc: hT[:, kc, j * P:(j + 1) * P],
                                     lambda kc: wr[:, kc, :])
                ins.then_inc(sy["moe_psum"], 1)
                project_pe(pe, bank(5)[:, 0:S], lambda kc: a1[:, kc, :], lambda kc: hT[:, kc, :]
                           ).then_inc(sy["t1_psum"], 1)
                def first_product(f):
                    for kc in range(KC):
                        pe.matmul(hidden(f), w1[:, kc, f * P:(f + 1) * P], hT[:, kc, :],
                                  start=(kc == 0), stop=False, skip_group_check=True)

                first_product(0)
                first_product(1)
                for j in range(NT):
                    pe.wait_ge(sy["mask_rows"], j + 1)
                    for m in range(4):
                        ins = pe.transpose(bank(j)[:, m * P:(m + 1) * P], mrow[:, j, m, :], ident)
                    ins.then_inc(sy["maskT_psum"], 1)
                pe.wait_ge(sy["m0_ready"], 1)
                for f in range(FC + 3):
                    if f < FC:
                        if f >= 4:
                            pe.wait_ge(sy["gelu1_ready"], f - 3)
                        if f >= 2:
                            first_product(f)
                        pe.matmul(hidden(f), b1l[:, f * P:(f + 1) * P], m0, start=False, stop=True,
                                  skip_group_check=True).then_inc(sy["base_psum"], 1)
                    if 1 <= f <= FC:
                        g = f - 1
                        pe.wait_ge(sy["gelu0_ready"], g + 1)
                        pe.matmul(hidden(g), b1l[:, g * P:(g + 1) * P], m01, start=False, stop=True,
                                  skip_group_check=True).then_inc(sy["base1_psum"], 1)
                    if f == FC + 1 and more:
                        pe.wait_ge(sy["gelu1_ready"], FC)
                        rows_to_cols(h, sy["normed_ready"], 2 * NT)
                    if f >= 3:
                        g = f - 3
                        pe.wait_ge(sy["ca_ready"], g + 1)
                        pe.matmul(bank(4)[:, :], a2[:, g, :], ca[:, g % 3].rearrange("p k t -> p (k t)"),
                                  start=(g == 0), stop=(g == FC - 1)).then_inc(sy["t2_psum"], 1)
                        pe.wait_ge(sy["mix_ready"], g + 1)
                        for j in range(NT):
                            pe.matmul(bank(6 + j)[:, :], mixT[:, g, j * P:(j + 1) * P], w2[:, g, :],
                                      start=(g == 0), stop=False)
                pe.wait_ge(sy["t2m_ready"], 1)
                for j in range(NT):
                    pe.matmul(bank(6 + j)[:, :], t2m[:, j * P:(j + 1) * P], b2l[:], start=False, stop=True
                              ).then_inc(sy["y_out_psum"], 1)
                sy.end_turn(pe, i, base + 1)

            with pe.Fori(0, nseq - 1) as i:
                turn(i, True)
            turn(nseq - 1, False)

        @block.vector
        def _(dve):
            def ln(ins):
                sy.link(dve, "dve_link", ins)

            def combine(g, src):
                k, j = g // NT, g % NT
                if g >= 2:
                    dve.wait_ge(sy["yk_used"], g - 1)
                dve.scalar_tensor_tensor(out=xn[:, j, :], in0=src, scalar=wk[:, j, k:k + 1],
                                         in1=xn[:, j, :], op0=ALU.mult, op1=ALU.add).then_inc(sy["yk_used"], 1)

            dve.wait_ge(sy["x3_in"], 16)
            dve.wait_ge(sy["wk_in"], 16)

            def combine_first(j):
                dve.wait_ge(sy[f"yk_in{j}"], 16 * TOPK)
                for k in range(TOPK):
                    ln(dve.scalar_tensor_tensor(out=xn[:, j, :], in0=yk0[:, NT * k + j, :], scalar=wk[:, j, k:k + 1],
                                                in1=xn[:, j, :], op0=ALU.mult, op1=ALU.add))

            layernorm_rows(dve, sy, 0, xn, h, st, mv, rstd, combine_first)
            dve.wait_ge(sy["w3_in"], W3A)
            dve.wait_ge(sy["init3"], 1)
            dve.wait_ge(sy["a_exp"], 1)
            sy.link(dve, "dve_link3", dve.tensor_scalar(neg_a[:], neg_a[:], -1.0, None, ALU.mult))
            sy.link(dve, "dve_link3", dve.tensor_scalar(small[:, 0:30], small[:, 0:30], 0.5, None, ALU.mult))
            sy.end_turn(dve, 0, base, "dve_link")

            def turn(i, more):
                dve.wait_ge(sy["dt_psum"], 1)
                v, av, e, w, lnw, d, m, sp_, dt, da = (dts[:, k, :] for k in range(10))
                ln(dve.tensor_tensor(v.rearrange("p (t h) -> p t h", t=NT),
                                     bank(6)[:, 0:NT * MH].rearrange("p (t h) -> p t h", t=NT),
                                     dt_bias.unsqueeze(1).broadcast_to([P, NT, MH]), ALU.add))
                dve.scalar_tensor_tensor(out=av, in0=v, scalar=-1.0, in1=v, op0=ALU.mult, op1=ALU.max
                                         ).then_inc(sy["dtabs_ready"], 1)
                dve.wait_ge(sy["dtexp_ready"], 1)
                dve.tensor_scalar(w, e, 1.0, None, ALU.add).then_inc(sy["dtone_ready"], 1)
                dve.wait_ge(sy["dtln_ready"], 1)
                ln(dve.tensor_scalar(d, w, -1.0, None, ALU.add))
                ln(dve.tensor_scalar(m, d, 0.0, None, ALU.is_equal))
                ln(dve.tensor_tensor(d, d, m, ALU.add))
                ln(dve.reciprocal(d, d))
                ln(dve.tensor_tensor(m, m, lnw, ALU.add))
                ln(dve.tensor_tensor(m, m, d, ALU.mult))
                ln(dve.tensor_tensor(m, m, e, ALU.mult))
                ln(dve.scalar_tensor_tensor(out=dt, in0=v, scalar=0.0, in1=m, op0=ALU.max, op1=ALU.add))
                dve.tensor_tensor(da.rearrange("p (t h) -> p t h", t=NT), dt.rearrange("p (t h) -> p t h", t=NT),
                                  neg_a[:].unsqueeze(1).broadcast_to([P, NT, MH]), ALU.mult
                                  ).then_inc(sy["dA_ready"], 1)
                for c in range(NXBC + 1):
                    if c < NXBC:
                        dve.wait_ge(sy["xbc_raw_ready"], c + 1)
                        ln(dve.tensor_scalar(convh[:, c, :], raw[:, c, :], conv_w[:, c, 3:4], conv_b[:, c:c + 1],
                                             ALU.mult, ALU.add))
                        for k in range(CONV - 1):
                            lag = CONV - 1 - k
                            ins = dve.scalar_tensor_tensor(
                                out=convh[:, c, lag:S], in0=raw[:, c, 0:S - lag], scalar=conv_w[:, c, k:k + 1],
                                in1=convh[:, c, lag:S], op0=ALU.mult, op1=ALU.add)
                            if k < CONV - 2:
                                ln(ins)
                        ins.then_inc(sy["conv_ready"], 1)
                    if c >= 1:
                        dve.wait_ge(sy["convtanh_ready"], c)
                        dve.scalar_tensor_tensor(out=xbc[:, c - 1, :], in0=cth[:, (c - 1) % 2, :], scalar=1.0,
                                                 in1=convh[:, c - 1, :], op0=ALU.add, op1=ALU.mult
                                                 ).then_inc(sy["xbc_ready"], 1)
                for j in range(NT):
                    dve.wait_ge(sy["ztanh_ready"], j + 1)
                    dve.scalar_tensor_tensor(out=zs[:, j, :], in0=zs[:, j, :], scalar=1.0, in1=bank(4 + j)[:, :],
                                             op0=ALU.add, op1=ALU.mult).then_inc(sy["zs_ready"], 1)
                for s in range(MH + 3):
                    if s < MH:
                        dve.wait_ge(sy["decaymask_ready"], s + 1)
                        dve.wait_ge(sy["bc_psum"], s + 1)
                        if s >= 2:
                            dve.wait_ge(sy["y_psum"], s - 1)
                        dve.tensor_tensor(wgt[:, s % 2, :], decay[:, s % 2, :], bank(2 + s % 2)[:, 0:3 * P],
                                          ALU.mult).then_inc(sy["w_ready"], 1)
                    if 2 <= s < MH + 2:
                        hd = s - 2
                        c = slice(hd * P, (hd + 1) * P)
                        dve.wait_ge(sy["y_psum"], hd + 1)
                        for j in range(NT):
                            ins = dve.scalar_tensor_tensor(out=y[:, j, c], in0=xr[:, j, :],
                                                           scalar=d_skip[:, hd:hd + 1], in1=y_bank(hd, j),
                                                           op0=ALU.mult, op1=ALU.add)
                        ln(ins)
                        for j in range(NT):
                            ins = dve.scalar_tensor_tensor(out=y[:, j, c], in0=y[:, j, c], scalar=0.5,
                                                           in1=zs[:, j, c], op0=ALU.mult, op1=ALU.mult)
                        ins.then_inc(sy["gated_ready"], 1)
                    if s >= 3:
                        hd = s - 3
                        c = slice(hd * P, (hd + 1) * P)
                        dve.wait_ge(sy["gated_norm"], hd + 1)
                        for j in range(NT):
                            ins = dve.scalar_tensor_tensor(out=y[:, j, c], in0=y[:, j, c],
                                                           scalar=grstd[:, j * MH + hd:j * MH + hd + 1],
                                                           in1=norm_bc[:, c], op0=ALU.mult, op1=ALU.mult)
                            if hd == MH - 1:
                                ins.then_inc(sy["attn_ready"], 1)
                dve.wait_ge(sy["out_done"], i * 16 + 1)
                sy.alone(dve)

                def residual(j):
                    dve.wait_ge(sy["out_psum"], j + 1)
                    dve.tensor_tensor(x[:, j, :], xn[:, j, :], bank(2 + j)[:, :], ALU.add
                                      ).then_inc(sy["resid_ready"], 1)
                    dve.wait_ge(sy["resid_ready"], j + 1)

                layernorm_rows(dve, sy, 0, x, h, st, mv, rstd, residual)
                for j in range(NT):
                    dve.wait_ge(sy["h_hi_ready"], j + 1)
                    dve.tensor_tensor(h2[1][:, j, :], h[:, j, :], h2[0][:, j, :].bitcast(F32), ALU.subtract
                                      ).then_inc(sy["h_lo_ready"], 1)
                for n in range(4 * LH + 6):
                    if n < 4 * LH:
                        hd, lc = n // 4, n % 4
                        dve.wait_ge(sy["s_psum"], n + 1)
                        dve.tensor_reduce(smx[:, hd, lc:lc + 1], bank(lc)[:, :], AX.X, ALU.max
                                          ).then_inc(sy["smax_ready"], 1)
                    if 2 <= n < 4 * LH + 2:
                        m = n - 2
                        hd, lc = m // 4, m % 4
                        dve.wait_ge(sy["sexp_ready"], m + 1)
                        ins = dve.reciprocal(ssum[:, hd, lc:lc + 1], ssum[:, hd, lc:lc + 1])
                        if m % 2:
                            ins.then_inc(sy["srec_ready"], 1)
                        else:
                            ln(ins)
                            dve.tensor_scalar(prob[:, hd % 2, lc, :], prob[:, hd % 2, lc, :],
                                              ssum[:, hd, lc:lc + 1], None, ALU.mult).then_inc(sy["snormed_dve"], 1)
                    if n >= 5 and n % 2 == 1 and n - 4 < 4 * LH:
                        m = n - 4
                        hd, lc = m // 4, m % 4
                        dve.wait_ge(sy["sT_psum"], m + 1)
                        if lc == 1 and hd >= 2:
                            dve.wait_ge(sy["ret_psum"], hd - 1)
                        dve.tensor_copy(probT[:, hd % 2, :, lc * P:(lc + 1) * P],
                                        bank(4 + lc % 2)[:, :].rearrange("p (c t) -> p c t", c=4)
                                        ).then_inc(sy["sT_dve"], 1)

                def attended(j):
                    dve.wait_ge(sy["ret_psum"], HPT * (j + 1))
                    ln(dve.scalar_tensor_tensor(out=x[:, j, :], in0=bank(6 + j)[:, :], scalar=gamma,
                                                in1=x[:, j, :], op0=ALU.mult, op1=ALU.add))

                layernorm_rows(dve, sy, 1, x, h, st, mv, rstd, attended)
                dve.wait_ge(sy["w3b_in"], W3B)
                dve.wait_ge(sy["moe_psum"], 1)
                for j in range(NT):
                    ln(dve.tensor_tensor(lg[:, j, :], bank(4)[:, j * LE:(j + 1) * LE], br, ALU.add))
                    ln(dve.max(lmax[:, j, :], lg[:, j, :]))
                    dve.tensor_scalar(lw[:, j:j + 1], lmax[:, j, 0:1], -1.0, None, ALU.mult
                                      ).then_inc(sy["moe_negmax"], 1)
                for j in range(NT):
                    dve.wait_ge(sy["moe_exp"], j + 1)
                    ln(dve.reciprocal(lsum[:, j:j + 1], lsum[:, j:j + 1]))
                    ln(dve.tensor_scalar(lpr[:, j, :], lex[:, j, :], lsum[:, j:j + 1], None, ALU.mult))
                    ln(dve.max(ltop[:, j, :], lpr[:, j, :]))
                    ln(dve.max_index(lidx[:, j, :], ltop[:, j, :], lpr[:, j, :]))
                    ln(dve.tensor_copy(lidxf[:, j, :], lidx[:, j, :]))
                    for k in range(LK):
                        dve.tensor_scalar(mrow[:, j, k, :], erow[:], lidxf[:, j, k:k + 1], SCALING, ALU.is_equal,
                                          ALU.mult)
                        ins = dve.tensor_scalar(mrow[:, j, LK + k, :], tri_le[:, P:2 * P], ltop[:, j, k:k + 1], None,
                                                ALU.mult)
                    ins.then_inc(sy["mask_rows"], 1)
                dve.wait_ge(sy["t1_psum"], 1)
                dve.wait_ge(sy["maskT_ready"], NT)
                ln(dve.tensor_tensor(m0, bank(5)[:, 0:S], maskT[:, 0, :], ALU.mult))
                ln(dve.tensor_tensor(m01, bank(5)[:, 0:S], maskT[:, 1, :], ALU.mult))
                dve.tensor_tensor(m01, m01, m0, ALU.subtract).then_inc(sy["m0_ready"], 1)
                for j in range(NT):
                    ln(dve.tensor_tensor(lw[:, j:j + 1], ltop[:, j, 0:1], ltop[:, j, 1:2], ALU.add))
                    ln(dve.scalar_tensor_tensor(out=x[:, j, :], in0=bias2_bc[:], scalar=lw[:, j:j + 1],
                                                in1=x[:, j, :], op0=ALU.mult, op1=ALU.add))
                if more:
                    dve.wait_ge(sy["x3_in"], (i + 2) * 16)
                    sy.alone(dve)
                    dve.wait_ge(sy["wk_in"], (i + 2) * 16)
                    sy.alone(dve)
                for f in range(FC):
                    if more and 1 <= f <= GATHERS:
                        k, j = (f - 1) // NT, (f - 1) % NT
                        dve.wait_ge(sy[f"yk_in{j}"], (i + 1) * (16 * TOPK) + (16 * k + 16))
                        sy.alone(dve)
                        combine(f - 1, yk[:, j, :])
                    if more and f == GATHERS + 1:
                        dve.wait_ge(sy["yk_used"], GATHERS)
                        layernorm_stats(dve, sy, xn, st, mv)
                    if more and f == GATHERS + 2:
                        layernorm_apply(dve, sy, 2, xn, h, mv, rstd)
                    dve.wait_ge(sy["gelu1_ready"], f + 1)
                    if f >= 3:
                        dve.wait_ge(sy["t2_psum"], f - 2)
                        dve.wait_ge(sy["mix_ready"], f - 2)
                    dve.tensor_tensor(ca[:, f % 3], act2[:, f % 2], maskT[:, 2:4, :], ALU.mult
                                      ).then_inc(sy["ca_ready"], 1)
                dve.wait_ge(sy["t2_psum"], FC)
                ln(dve.tensor_tensor(t2m, bank(4)[:, 0:S], maskT[:, 0, :], ALU.mult))
                ln(dve.tensor_tensor(t2b, bank(4)[:, S:2 * S], maskT[:, 1, :], ALU.mult))
                dve.tensor_tensor(t2m, t2m, t2b, ALU.add).then_inc(sy["t2m_ready"], 1)
                for j in range(NT):
                    dve.wait_ge(sy["y_out_psum"], j + 1)
                    dve.tensor_tensor(x[:, j, :], x[:, j, :], bank(6 + j)[:, :], ALU.add
                                      ).then_inc(sy["x_out_ready"], 1)
                sy.end_turn(dve, i, base + 1, "dve_link")

            with dve.Fori(0, nseq - 1) as i:
                turn(i, True)
            turn(nseq - 1, False)


def constants(nc, sy, ctx):
    ident = ctx.enter_context(nc.sbuf_tensor("ident", [P, P], F32))
    iota_t = ctx.enter_context(nc.sbuf_tensor("iota_row", [P, E], F32))
    minus_half = ctx.enter_context(nc.sbuf_tensor("minus_half", [P, 16], F32))
    psum = ctx.enter_context(nc.psum_tensor("psum", [P, 8, 512], F32))
    last = ctx.enter_context(nc.sbuf_tensor("last_token", [P, E], F32))
    tri_lt = ctx.enter_context(nc.sbuf_tensor("tri_lt", [P, P], F32))
    ones = ctx.enter_context(nc.sbuf_tensor("ones", [P, P], F32))
    with nc.Block() as block:
        @block.gpsimd
        def _(pool):
            pool.memset(minus_half[:], -0.5)
            pool.memset(ones[:], 1.0)
            sy.link(pool, "const_link", pool.memset(tri_lt[:], 1.0))
            pool.affine_select(out=tri_lt[:], in_=tri_lt[:], compare_op=ALU.is_gt, fill=0.0, base=0,
                               pattern=[[1, P]], channel_multiplier=-1)
            sy.link(pool, "const_link", pool.memset(ident[:], 0.0))
            pool.affine_select(out=ident[:], in_=ident[:], compare_op=ALU.not_equal, fill=1.0, base=0,
                               pattern=[[-1, P]], channel_multiplier=1).then_inc(sy["const_ready"], 1)
            pool.iota(iota_t[:], pattern=[[1, E]], base=0, channel_multiplier=0,
                      allow_small_or_imprecise_dtypes=True).then_inc(sy["const_ready"], 1)
            pool.wait_ge(sy["const_ready"], 2)
    return {"ident": ident[:], "iota": iota_t[:], "minus_half": minus_half[:], "bank": lambda b: psum[:, b, :],
            "last": last[:], "tri_lt": tri_lt[:], "ones": ones[:]}


def program(nc, dr, phases=(1, 2, 3), nseq=NSEQ):
    with ExitStack() as ctx:
        sy = Sync(nc, ctx)
        for n in ("turn_done", "turn_go"):
            sy[n]
        const = constants(nc, sy, ctx)
        dr["normed_rows"] = dr.get("normed_rows", None) or nc.dram_tensor("normed_rows", [NSEQ, S, D], F32).ap()
        for name, shape in (("mid", [NSEQ, P, NT, D]), ("route_w", [NSEQ, P, NT, 8]), ("expert_out", [E * CAP, D])):
            if name not in dr:
                dr[name] = nc.dram_tensor(name, shape, F32).ap()
        for name, shape in (("slots", [NSEQ, P, NT, 8]), ("slot_token", [E * CAP, 1])):
            if name not in dr:
                dr[name] = nc.dram_tensor(name, shape, I32).ap()
        if 1 in phases:
            phase1(nc, sy, const, dr, 0, nseq)
        tiles, loads = mixer_weights(nc, ctx, dr)
        if 2 in phases:
            phase2(nc, sy, const, dr, loads)
        if 3 in phases:
            phase3(nc, sy, const, dr, nseq + 1 if 1 in phases else 0, tiles, nseq)


def cols_layout(w):
    o, i = w.shape
    return w.T.reshape(i // P, P, o).transpose(1, 0, 2)


def host_layout(a):
    a = {k: np.asarray(v) for k, v in a.items()}
    inv = (1.0 / np.power(np.float32(10000.0), np.arange(0, HD, 2, dtype=np.float32) / np.float32(HD))).astype(np.float32)
    freqs = np.outer(np.arange(S, dtype=np.float32), inv).astype(np.float32)
    emb = np.concatenate([freqs, freqs], -1)
    rot = np.zeros((P, P), np.float32)
    for i in range(0, P, 2):
        rot[i + 1, i], rot[i, i + 1] = -1.0, 1.0
    q, k = np.arange(P)[:, None], np.arange(P)[None, :]
    k1 = np.arange(WINDOW, S)[None, :]
    keep = np.concatenate([(q >= k) & (q - k < WINDOW), (q + P >= k1) & (q + P - k1 < WINDOW)], 1)
    bc = lambda v: np.broadcast_to(v.reshape(1, -1), (P, v.size))
    tokens = lambda t: t.reshape(NSEQ, NT, P, -1).transpose(0, 2, 1, 3)
    d = {
        "x": tokens(a["x"]),
        "ctxT": a["ctx_2048"].transpose(0, 2, 1).reshape(NSEQ, KC, P, S).transpose(0, 2, 1, 3),
        "mask": a["mask_BxS2_ik0"].reshape(NSEQ, NT, P).transpose(0, 2, 1),
        "w_qkv": cols_layout(a["L0_attn_w_qkv"]), "w_out": cols_layout(a["L0_attn_w_out"]),
        "w_gate": cols_layout(a["L0_ffn_gate_weight"]),
        "w_sg": cols_layout(a["L0_ffn_Sg"]), "w_su": cols_layout(a["L0_ffn_Su"]), "w_sd": a["L0_ffn_Sd"].T,
        "cosT": np.tile(np.cos(emb).T, (HPC, 1)), "sinT": np.tile(np.sin(emb).T, (HPC, 1)), "rot": rot,
        "wmask": np.where(keep, 0.0, NEG).astype(np.float32),
        "bq": a["L0_xattn_bq"].reshape(KC, P).T, "bk": a["L0_xattn_bk"].reshape(KC, P).T,
        "rows_bc": np.stack([bc(a["L0_xattn_" + n]) for n in ("bv", "bo", "ln_gamma", "ln_beta")], 1),
        "rs": np.broadcast_to(a["L0_xattn_residual_scale"].reshape(1, 1), (P, 1)),
    }
    small = np.zeros((P, 64), np.float32)
    small[:, 0:24] = a["L1_attn_conv_w"].reshape(NXBC, P, CONV).transpose(1, 0, 2).reshape(P, -1)
    small[:, 24:30] = a["L1_attn_conv_b"].reshape(NXBC, P).T
    small[:, 32:36], small[:, 36:40], small[:, 40:44] = a["L1_attn_dt_bias"], a["L1_attn_A_log"], a["L1_attn_D"]
    small[:, 44], small[:, 48:56] = a["L1_xattn_gamma"], a["L1_ffn_br"]
    d |= {
        "w_gu": np.stack([a["L0_ffn_W" + n].transpose(0, 2, 1).reshape(E, KC, P, M).transpose(0, 2, 1, 3)
                          for n in "gu"], 2),
        "w_d": a["L0_ffn_Wd"].transpose(0, 2, 1),
        "ctx": tokens(a["ctx_2048"]), "small": small, "bias1": a["L1_ffn_b1"].reshape(FC, P).T,
        "w_in": cols_layout(a["L1_attn_in_proj_w"]), "w_mo": cols_layout(a["L1_attn_out_proj_w"]),
        "norm_bc": bc(a["L1_attn_norm_w"]), "bias2_bc": bc(a["L1_ffn_b2"]),
        "wr": cols_layout(a["L1_ffn_Wr"].T), "w1": cols_layout(a["L1_ffn_W1"].T),
        "w2": cols_layout(a["L1_ffn_W2"].T), "a1": cols_layout(a["L1_ffn_A1"].reshape(LE * LR, D)),
        "b1l": a["L1_ffn_B1"].transpose(0, 2, 1).reshape(LE * LR, F),
        "a2": cols_layout(a["L1_ffn_A2"].reshape(LE * LR, F)),
        "b2l": a["L1_ffn_B2"].transpose(0, 2, 1).reshape(LE * LR, D),
    }
    for n in "qkvo":
        d["w_x" + n] = cols_layout(a["L0_xattn_W" + n])
    return {k: np.ascontiguousarray(v) for k, v in d.items()}


def kernel(**inputs):
    import concourse.bacc as bacc
    from concourse.bass_utils import run_bass_kernel_spmd as run

    arrays = host_layout(inputs)
    nc = bacc.Bacc("TRN2", target_bir_lowering=False, num_devices=1)
    dr = {n: nc.dram_tensor(f"in_{n}_dram", a.shape, mybir.dt.from_np(a.dtype), kind="ExternalInput").ap()
          for n, a in arrays.items()}
    dr["out"] = nc.dram_tensor("out_dram", [NSEQ, S, D], F32, kind="ExternalOutput").ap()
    program(nc, dr)
    r = run(nc, [{f"in_{n}_dram": a for n, a in arrays.items()}], core_ids=[0])
    return r.results[0]["out_dram"]
```
